# Optimizing a Trainium2 kernel written in Bass

```python
import numpy as np
import jax
import jax.numpy as jnp

def _softmax(x, axis=-1):
    return jax.nn.softmax(x, axis=axis)

def _gelu(x):
    return jax.nn.gelu(x, approximate=True)

def _silu(x):
    return jax.nn.silu(x)

def _sigmoid(x):
    return jax.nn.sigmoid(x)

def _layernorm(x, axis=-1, eps=1e-05):
    m = jnp.mean(x, axis=axis, keepdims=True)
    v = jnp.var(x, axis=axis, keepdims=True)
    return (x - m) / jnp.sqrt(v + eps)

def _scatter_add(tgt, idx, src, axis=0):
    return tgt.at[idx].add(src)

def _segment_sum(src, seg, n):
    return jax.ops.segment_sum(src, seg, n)
kernel_name = 'mk_vit_tower_cls_d4_tok_img256_r4_ffa447'

def setup_inputs(seed: int=0):
    np.random.seed(seed)
    _w = jnp.asarray

    def _rec_inputs():
        import jax
        import jax.numpy as jnp
        _rk = jax.random.key(seed)
        x = -7.10856e-05 + 0.999911 * jax.random.normal(jax.random.fold_in(_rk, 1), (2, 64, 128, 64), jnp.float32)
        cls_tok = 0.02 * jax.random.normal(jax.random.fold_in(_rk, 5), (1, 1, 64), jnp.float32)
        return (x, cls_tok)
    x, cls_tok = _rec_inputs()

    def _L0_tok_setup():
        import jax, jax.numpy as jnp
        import numpy as np
        PATCH_LEN = 16
        STRIDE = 8
        PAD = 8
        key = jax.random.key(seed)
        k1, k2 = jax.random.split(key)
        x = jax.random.normal(k1, (32, 64, 128, 64), dtype=jnp.float32)
        in_feat = 64 * (PATCH_LEN // 2 + 1) * 2
        W = jax.random.normal(k2, (64, in_feat), dtype=jnp.float32) * 0.02
        return {'x': x, 'W': W}
    _L0_tok_all = _L0_tok_setup()
    _L0_tok_in = {k: v for k, v in _L0_tok_all.items() if k in ('W',)}
    del _L0_tok_all

    def _L0_attn_setup():
        import jax, jax.numpy as jnp
        import numpy as np
        B, T, D = (4, 512, 64)
        W_LORA, A_LORA, G_LORA = (64, 64, 128)
        DECAY_SCALE = -0.6065306597126334
        EPS = D * 1e-05

        def _forward(x, x_mix, W_r, W_k, W_v, W_o, A_w, B_w, b_w, A_a, B_a, b_a, A_g, B_g, k_k, k_a, r_k, gn_w, gn_b):
            b, t, d = x.shape
            shifted = jnp.pad(x, ((0, 0), (1, 0), (0, 0)))[:, :-1]
            delta = shifted - x
            xr, xw, xk, xv, xa, xg = [x + delta * x_mix[i] for i in range(6)]
            r = xr @ W_r
            w = DECAY_SCALE * jax.nn.sigmoid(jnp.tanh(xw @ A_w) @ B_w + b_w)
            k = xk @ W_k
            v = xv @ W_v
            a = jax.nn.sigmoid(xa @ A_a @ B_a + b_a)
            g = jax.nn.sigmoid(xg @ A_g) @ B_g
            kk = k * k_k
            kk = kk / jnp.maximum(jnp.linalg.norm(kk, axis=-1, keepdims=True), 1e-12)
            k = k * (1.0 + (a - 1.0) * k_a)
            decay = jnp.exp(w)

            def step(S, inp):
                r_t, dec_t, k_t, v_t, kk_t, a_t = inp
                b_t = kk_t * a_t
                sa = jnp.einsum('bvk,bk->bv', S, -kk_t)
                S = S * dec_t[:, None, :] + sa[:, :, None] * b_t[:, None, :] + v_t[:, :, None] * k_t[:, None, :]
                o_t = jnp.einsum('bvk,bk->bv', S, r_t)
                return (S, o_t)
            tm = lambda z: jnp.swapaxes(z, 0, 1)
            S0 = jnp.zeros((b, d, d), x.dtype)
            _, o = jax.lax.scan(step, S0, (tm(r), tm(decay), tm(k), tm(v), tm(kk), tm(a)))
            o = jnp.swapaxes(o, 0, 1)
            mu = jnp.mean(o, axis=-1, keepdims=True)
            var = jnp.var(o, axis=-1, keepdims=True)
            o = (o - mu) * jax.lax.rsqrt(var + EPS) * gn_w + gn_b
            o = o + jnp.sum(r * k * r_k, axis=-1, keepdims=True) * v
            return o * g @ W_o
        key = jax.random.key(seed)
        ks = jax.random.split(key, 20)
        n = jax.random.normal
        p = {}
        p['x'] = n(ks[0], (B, T, D), jnp.float32)
        p['x_mix'] = n(ks[1], (6, D), jnp.float32) * 0.1
        s = 1.0 / np.sqrt(D).astype(np.float32)
        p['W_r'] = n(ks[2], (D, D), jnp.float32) * s
        p['W_k'] = n(ks[3], (D, D), jnp.float32) * s
        p['W_v'] = n(ks[4], (D, D), jnp.float32) * s
        p['W_o'] = n(ks[5], (D, D), jnp.float32) * s
        p['A_w'] = n(ks[6], (D, W_LORA), jnp.float32) * s
        p['B_w'] = n(ks[7], (W_LORA, D), jnp.float32) / np.sqrt(W_LORA).astype(np.float32)
        p['b_w'] = n(ks[8], (D,), jnp.float32) * 0.5
        p['A_a'] = n(ks[9], (D, A_LORA), jnp.float32) * s
        p['B_a'] = n(ks[10], (A_LORA, D), jnp.float32) / np.sqrt(A_LORA).astype(np.float32)
        p['b_a'] = n(ks[11], (D,), jnp.float32) * 0.1
        p['A_g'] = n(ks[12], (D, G_LORA), jnp.float32) * s
        p['B_g'] = n(ks[13], (G_LORA, D), jnp.float32) / np.sqrt(G_LORA).astype(np.float32)
        p['k_k'] = n(ks[14], (D,), jnp.float32) * 0.5 + 0.85
        p['k_a'] = n(ks[15], (D,), jnp.float32) * 0.1 + 1.0
        p['r_k'] = n(ks[16], (D,), jnp.float32) * 0.1
        p['gn_w'] = jnp.ones((D,), jnp.float32)
        p['gn_b'] = jnp.zeros((D,), jnp.float32)
        return p
    _L0_attn_all = _L0_attn_setup()
    _L0_attn_in = {k: v for k, v in _L0_attn_all.items() if k in ('x_mix', 'W_r', 'W_k', 'W_v', 'W_o', 'A_w', 'B_w', 'b_w', 'A_a', 'B_a', 'b_a', 'A_g', 'B_g', 'k_k', 'k_a', 'r_k', 'gn_w', 'gn_b')}
    del _L0_attn_all

    def _L0_ffn_setup():
        import jax, jax.numpy as jnp
        import numpy as np
        B, S, D = (8, 1024, 64)
        H = 4 * D
        CAPACITY = 0.5
        key = jax.random.key(seed)
        ks = jax.random.split(key, 6)
        x = jax.random.normal(ks[0], (B, S, D), dtype=jnp.float32)
        attention_mask = jnp.zeros((B, 1, 1, S), dtype=jnp.float32)
        wr = jax.random.normal(ks[1], (D, 1), dtype=jnp.float32) * 0.02
        br = jnp.zeros((1,), dtype=jnp.float32)
        w1 = jax.random.normal(ks[2], (D, H), dtype=jnp.float32) * 0.02
        b1 = jnp.zeros((H,), dtype=jnp.float32)
        w2 = jax.random.normal(ks[3], (H, D), dtype=jnp.float32) * 0.02
        b2 = jnp.zeros((D,), dtype=jnp.float32)
        return {'x': x, 'attention_mask': attention_mask, 'wr': wr, 'br': br, 'w1': w1, 'b1': b1, 'w2': w2, 'b2': b2}
    _L0_ffn_all = _L0_ffn_setup()
    _L0_ffn_in = {k: v for k, v in _L0_ffn_all.items() if k in ('attention_mask', 'wr', 'br', 'w1', 'b1', 'w2', 'b2')}
    del _L0_ffn_all

    def _L1_attn_setup():
        import jax, jax.numpy as jnp
        import numpy as np
        NUM_HEADS = 8

        def _to_heads(y, R, C, H, hd):
            y = y.reshape(R, C, H, hd).transpose(0, 2, 1, 3)
            y = jnp.transpose(y, (2, 1, 0, 3)).reshape(1, H, C, R * hd)
            return y

        def _reference_tuple_inner(x, Wq, bq, Wk, bk, Wv, bv):
            R, C, E = x.shape
            H = NUM_HEADS
            hd = E // H
            q = _to_heads(x @ Wq.T + bq, R, C, H, hd)
            k = _to_heads(x @ Wk.T + bk, R, C, H, hd)
            v = _to_heads(x @ Wv.T + bv, R, C, H, hd)
            d = q.shape[-1]
            q = jax.nn.softmax(q, axis=-1)
            k = jax.nn.softmax(k, axis=-2)
            q = q * jnp.asarray(float(d) ** 0.5, dtype=q.dtype)
            attn_weights = jnp.einsum('bhnd,bhmd->bhnm', q, k).sum(0)
            context = jnp.einsum('bhnd,bhne->bhde', k, v)
            out = jnp.einsum('bhnd,bhde->hbne', q, context)
            out = out.reshape(H, C, R, hd)
            out = jnp.transpose(out, (2, 1, 0, 3)).reshape(R, C, E)
            return (out, attn_weights)
        key = jax.random.key(seed)
        ks = jax.random.split(key, 7)
        R, C, E = (16, 512, 64)
        x = jax.random.normal(ks[0], (R, C, E), dtype=jnp.float32)
        s = 0.02
        Wq = jax.random.normal(ks[1], (E, E), dtype=jnp.float32) * s
        bq = jax.random.normal(ks[2], (E,), dtype=jnp.float32) * s
        Wk = jax.random.normal(ks[3], (E, E), dtype=jnp.float32) * s
        bk = jax.random.normal(ks[4], (E,), dtype=jnp.float32) * s
        Wv = jax.random.normal(ks[5], (E, E), dtype=jnp.float32) * s
        bv = jax.random.normal(ks[6], (E,), dtype=jnp.float32) * s
        return {'x': x, 'Wq': Wq, 'bq': bq, 'Wk': Wk, 'bk': bk, 'Wv': Wv, 'bv': bv}
    _L1_attn_all = _L1_attn_setup()
    _L1_attn_in = {k: v for k, v in _L1_attn_all.items() if k in ('Wq', 'bq', 'Wk', 'bk', 'Wv', 'bv')}
    del _L1_attn_all

    def _L1_ffn_setup():
        import jax, jax.numpy as jnp
        import numpy as np
        B, T, C = (64, 96, 64)
        NH, NKV = (4, 2)
        HD = C // NH
        NREP = NH // NKV
        NE, TOPK = (8, 2)
        HID = int(8 / 3 * C)
        EPS_RMS = 1e-06

        def _rope_tables(t_len):
            inv_freq = 1.0 / 10000.0 ** (np.arange(0, HD, 2, dtype=np.float32) / HD)
            t = np.arange(t_len, dtype=np.float32)
            freqs = np.outer(t, inv_freq)
            emb = np.concatenate([freqs, freqs], axis=-1)
            return (jnp.asarray(np.cos(emb)), jnp.asarray(np.sin(emb)))

        def _rotate_half(x):
            h = x.shape[-1] // 2
            return jnp.concatenate([-x[..., h:], x[..., :h]], axis=-1)

        def _rmsnorm(v, w):
            return v * jax.lax.rsqrt(jnp.mean(v * v, axis=-1, keepdims=True) + EPS_RMS) * w
        key = jax.random.key(seed)
        ks = jax.random.split(key, 10)
        s = lambda k, shape: jax.random.normal(k, shape, jnp.float32) * 0.02
        return {'x': jax.random.normal(ks[0], (B, T, C), jnp.float32), 'ln1_w': jnp.ones((C,), jnp.float32), 'ln2_w': jnp.ones((C,), jnp.float32), 'wq': s(ks[1], (NH * HD, C)), 'wk': s(ks[2], (NKV * HD, C)), 'wv': s(ks[3], (NKV * HD, C)), 'wo': s(ks[4], (C, C)), 'router_w': s(ks[5], (NE, C)), 'w1': s(ks[6], (NE, HID, C)), 'w2': s(ks[7], (NE, C, HID)), 'w3': s(ks[8], (NE, HID, C))}
    _L1_ffn_all = _L1_ffn_setup()
    _L1_ffn_in = {k: v for k, v in _L1_ffn_all.items() if k in ('ln1_w', 'ln2_w', 'wq', 'wk', 'wv', 'wo', 'router_w', 'w1', 'w2', 'w3')}
    del _L1_ffn_all

    def _L2_attn_setup():
        import jax, jax.numpy as jnp
        import numpy as np
        EPS = 1e-06

        def _rmsnorm(x, w):
            xf = x.astype(jnp.float32)
            y = xf * jax.lax.rsqrt(jnp.mean(xf * xf, axis=-1, keepdims=True) + EPS)
            return y.astype(x.dtype) * w
        key = jax.random.key(seed)
        k0, k1, k2 = jax.random.split(key, 3)
        B, T, C = (2, 256, 64)
        x = jax.random.normal(k0, (B, T, C), jnp.float32)
        w_qkv = jax.random.normal(k1, (3 * C, C), jnp.float32) / np.float32(np.sqrt(C))
        w_proj = jax.random.normal(k2, (C, C), jnp.float32) / np.float32(np.sqrt(C))
        qn_w = jnp.ones((2,), jnp.float32)
        kn_w = jnp.ones((2,), jnp.float32)
        return {'x': x, 'w_qkv': w_qkv, 'w_proj': w_proj, 'qn_w': qn_w, 'kn_w': kn_w}
    _L2_attn_all = _L2_attn_setup()
    _L2_attn_in = {k: v for k, v in _L2_attn_all.items() if k in ('w_qkv', 'w_proj', 'qn_w', 'kn_w')}
    del _L2_attn_all

    def _L2_ffn_setup():
        import jax, jax.numpy as jnp
        import numpy as np
        B, K, D = (128, 16, 64)
        E = 32
        H = int(D * 0.25)
        key = jax.random.key(seed)
        ks = jax.random.split(key, 7)
        d_rs = D ** (-0.5)
        h_rs = H ** (-0.5)
        x = jax.random.normal(ks[0], (B, K, D), dtype=jnp.float32)
        router_w = jax.random.uniform(ks[1], (E, D), jnp.float32, -d_rs, d_rs)
        router_b = jax.random.uniform(ks[2], (E,), jnp.float32, -d_rs, d_rs)
        W1 = jax.random.uniform(ks[3], (E, D, H), jnp.float32, -h_rs, h_rs)
        b1 = jax.random.uniform(ks[4], (E, H), jnp.float32, -h_rs, h_rs)
        W2 = jax.random.uniform(ks[5], (E, H, D), jnp.float32, -d_rs, d_rs)
        b2 = jax.random.uniform(ks[6], (E, D), jnp.float32, -d_rs, d_rs)
        return {'x': x, 'router_w': router_w, 'router_b': router_b, 'W1': W1, 'b1': b1, 'W2': W2, 'b2': b2}
    _L2_ffn_all = _L2_ffn_setup()
    _L2_ffn_in = {k: v for k, v in _L2_ffn_all.items() if k in ('router_w', 'router_b', 'W1', 'b1', 'W2', 'b2')}
    del _L2_ffn_all

    def _L3_attn_setup():
        import jax, jax.numpy as jnp
        import numpy as np
        import math
        D_MODEL = 64
        N_HEAD = 8
        BATCH = 2
        NTOK = 256
        A2LEN = 255

        def _linm(w, x):
            return jnp.einsum('oi,bti->bto', w[:, :-1], x) + w[:, -1]
        key = jax.random.key(seed)
        ks = jax.random.split(key, 5)
        scl = 0.02 / math.sqrt(2 * 9)
        x = jax.random.normal(ks[0], (BATCH, NTOK, D_MODEL), jnp.float32)
        wq = (scl * jax.random.normal(ks[1], (N_HEAD * D_MODEL, D_MODEL + 1), jnp.float32)).at[:, -1].set(0.0)
        wv = (scl * jax.random.normal(ks[2], (N_HEAD * D_MODEL, D_MODEL + 1), jnp.float32)).at[:, -1].set(0.0)
        wk = 0.005 * jnp.ones((N_HEAD, D_MODEL), jnp.float32)
        fanout_w = (scl * jax.random.normal(ks[3], (D_MODEL, D_MODEL + 1), jnp.float32)).at[:, -1].set(0.0)
        a2a = jax.random.permutation(ks[4], NTOK)[:A2LEN].astype(jnp.int32)
        return {'x': x, 'wq': wq, 'wv': wv, 'wk': wk, 'fanout_w': fanout_w, 'a2a': a2a}
    _L3_attn_all = _L3_attn_setup()
    _L3_attn_in = {k: v for k, v in _L3_attn_all.items() if k in ('wq', 'wv', 'wk', 'fanout_w', 'a2a')}
    del _L3_attn_all

    def _L3_ffn_setup():
        import math
        import jax, jax.numpy as jnp
        import numpy as np
        CAPACITY_FACTOR = 1.25
        key = jax.random.key(seed)
        ks = jax.random.split(key, 5)
        B, L, D, F, E = (8, 2048, 64, 256, 8)
        h = jax.random.normal(ks[0], (B, L, D), dtype=jnp.float32)
        gate_w = jax.random.normal(ks[1], (D, E), dtype=jnp.float32) * 0.02
        gate_b = jnp.zeros((E,), dtype=jnp.float32)
        w1 = jax.random.normal(ks[2], (E, D, F), dtype=jnp.float32) * (1.0 / math.sqrt(D))
        b1 = jnp.zeros((E, F), dtype=jnp.float32)
        w2 = jax.random.normal(ks[3], (E, F, D), dtype=jnp.float32) * (1.0 / math.sqrt(F))
        b2 = jnp.zeros((E, D), dtype=jnp.float32)
        return {'h': h, 'gate_w': gate_w, 'gate_b': gate_b, 'w1': w1, 'b1': b1, 'w2': w2, 'b2': b2}
    _L3_ffn_all = _L3_ffn_setup()
    _L3_ffn_in = {k: v for k, v in _L3_ffn_all.items() if k in ('gate_w', 'gate_b', 'w1', 'b1', 'w2', 'b2')}
    del _L3_ffn_all
    return {'x': x, 'cls_tok': cls_tok, 'L0_tok_W': _L0_tok_in['W'], 'L0_attn_x_mix': _L0_attn_in['x_mix'], 'L0_attn_W_r': _L0_attn_in['W_r'], 'L0_attn_W_k': _L0_attn_in['W_k'], 'L0_attn_W_v': _L0_attn_in['W_v'], 'L0_attn_W_o': _L0_attn_in['W_o'], 'L0_attn_A_w': _L0_attn_in['A_w'], 'L0_attn_B_w': _L0_attn_in['B_w'], 'L0_attn_b_w': _L0_attn_in['b_w'], 'L0_attn_A_a': _L0_attn_in['A_a'], 'L0_attn_B_a': _L0_attn_in['B_a'], 'L0_attn_b_a': _L0_attn_in['b_a'], 'L0_attn_A_g': _L0_attn_in['A_g'], 'L0_attn_B_g': _L0_attn_in['B_g'], 'L0_attn_k_k': _L0_attn_in['k_k'], 'L0_attn_k_a': _L0_attn_in['k_a'], 'L0_attn_r_k': _L0_attn_in['r_k'], 'L0_attn_gn_w': _L0_attn_in['gn_w'], 'L0_attn_gn_b': _L0_attn_in['gn_b'], 'L0_ffn_attention_mask': _L0_ffn_in['attention_mask'], 'L0_ffn_wr': _L0_ffn_in['wr'], 'L0_ffn_br': _L0_ffn_in['br'], 'L0_ffn_w1': _L0_ffn_in['w1'], 'L0_ffn_b1': _L0_ffn_in['b1'], 'L0_ffn_w2': _L0_ffn_in['w2'], 'L0_ffn_b2': _L0_ffn_in['b2'], 'L1_attn_Wq': _L1_attn_in['Wq'], 'L1_attn_bq': _L1_attn_in['bq'], 'L1_attn_Wk': _L1_attn_in['Wk'], 'L1_attn_bk': _L1_attn_in['bk'], 'L1_attn_Wv': _L1_attn_in['Wv'], 'L1_attn_bv': _L1_attn_in['bv'], 'L1_ffn_ln1_w': _L1_ffn_in['ln1_w'], 'L1_ffn_ln2_w': _L1_ffn_in['ln2_w'], 'L1_ffn_wq': _L1_ffn_in['wq'], 'L1_ffn_wk': _L1_ffn_in['wk'], 'L1_ffn_wv': _L1_ffn_in['wv'], 'L1_ffn_wo': _L1_ffn_in['wo'], 'L1_ffn_router_w': _L1_ffn_in['router_w'], 'L1_ffn_w1': _L1_ffn_in['w1'], 'L1_ffn_w2': _L1_ffn_in['w2'], 'L1_ffn_w3': _L1_ffn_in['w3'], 'L2_attn_w_qkv': _L2_attn_in['w_qkv'], 'L2_attn_w_proj': _L2_attn_in['w_proj'], 'L2_attn_qn_w': _L2_attn_in['qn_w'], 'L2_attn_kn_w': _L2_attn_in['kn_w'], 'L2_ffn_router_w': _L2_ffn_in['router_w'], 'L2_ffn_router_b': _L2_ffn_in['router_b'], 'L2_ffn_W1': _L2_ffn_in['W1'], 'L2_ffn_b1': _L2_ffn_in['b1'], 'L2_ffn_W2': _L2_ffn_in['W2'], 'L2_ffn_b2': _L2_ffn_in['b2'], 'L3_attn_wq': _L3_attn_in['wq'], 'L3_attn_wv': _L3_attn_in['wv'], 'L3_attn_wk': _L3_attn_in['wk'], 'L3_attn_fanout_w': _L3_attn_in['fanout_w'], 'L3_attn_a2a': _L3_attn_in['a2a'], 'L3_ffn_gate_w': _L3_ffn_in['gate_w'], 'L3_ffn_gate_b': _L3_ffn_in['gate_b'], 'L3_ffn_w1': _L3_ffn_in['w1'], 'L3_ffn_b1': _L3_ffn_in['b1'], 'L3_ffn_w2': _L3_ffn_in['w2'], 'L3_ffn_b2': _L3_ffn_in['b2']}

def reference(x, cls_tok, L0_tok_W, L0_attn_x_mix, L0_attn_W_r, L0_attn_W_k, L0_attn_W_v, L0_attn_W_o, L0_attn_A_w, L0_attn_B_w, L0_attn_b_w, L0_attn_A_a, L0_attn_B_a, L0_attn_b_a, L0_attn_A_g, L0_attn_B_g, L0_attn_k_k, L0_attn_k_a, L0_attn_r_k, L0_attn_gn_w, L0_attn_gn_b, L0_ffn_attention_mask, L0_ffn_wr, L0_ffn_br, L0_ffn_w1, L0_ffn_b1, L0_ffn_w2, L0_ffn_b2, L1_attn_Wq, L1_attn_bq, L1_attn_Wk, L1_attn_bk, L1_attn_Wv, L1_attn_bv, L1_ffn_ln1_w, L1_ffn_ln2_w, L1_ffn_wq, L1_ffn_wk, L1_ffn_wv, L1_ffn_wo, L1_ffn_router_w, L1_ffn_w1, L1_ffn_w2, L1_ffn_w3, L2_attn_w_qkv, L2_attn_w_proj, L2_attn_qn_w, L2_attn_kn_w, L2_ffn_router_w, L2_ffn_router_b, L2_ffn_W1, L2_ffn_b1, L2_ffn_W2, L2_ffn_b2, L3_attn_wq, L3_attn_wv, L3_attn_wk, L3_attn_fanout_w, L3_attn_a2a, L3_ffn_gate_w, L3_ffn_gate_b, L3_ffn_w1, L3_ffn_b1, L3_ffn_w2, L3_ffn_b2):
    import jax
    import jax.numpy as jnp

    def _L0_tok_ref(x, W):
        import jax, jax.numpy as jnp
        import numpy as np
        PATCH_LEN = 16
        STRIDE = 8
        PAD = 8
        B, C, T, V = x.shape
        xp = jnp.pad(x, ((0, 0), (0, 0), (0, PAD), (0, 0)), mode='edge')
        Tp = T + PAD
        N = (Tp - PATCH_LEN) // STRIDE + 1
        idx = jnp.arange(N)[:, None] * STRIDE + jnp.arange(PATCH_LEN)[None, :]
        patches = xp[:, :, idx, :]
        patches = jnp.transpose(patches, (0, 4, 2, 3, 1))
        xf = jnp.fft.rfft(patches, axis=-2, norm='ortho')
        F = xf.shape[-2]
        x_real = xf.real.reshape(B, V, N, F * C)
        x_imag = xf.imag.reshape(B, V, N, F * C)
        x_emb = jnp.concatenate([x_real, x_imag], axis=-1)
        x_emb = x_emb @ W.T
        return x_emb.reshape(B, V * N, -1)

    def _L0_attn_ref(x, x_mix, W_r, W_k, W_v, W_o, A_w, B_w, b_w, A_a, B_a, b_a, A_g, B_g, k_k, k_a, r_k, gn_w, gn_b):
        import jax, jax.numpy as jnp
        import numpy as np
        B, T, D = (4, 512, 64)
        W_LORA, A_LORA, G_LORA = (64, 64, 128)
        DECAY_SCALE = -0.6065306597126334
        EPS = D * 1e-05

        def _forward(x, x_mix, W_r, W_k, W_v, W_o, A_w, B_w, b_w, A_a, B_a, b_a, A_g, B_g, k_k, k_a, r_k, gn_w, gn_b):
            b, t, d = x.shape
            shifted = jnp.pad(x, ((0, 0), (1, 0), (0, 0)))[:, :-1]
            delta = shifted - x
            xr, xw, xk, xv, xa, xg = [x + delta * x_mix[i] for i in range(6)]
            r = xr @ W_r
            w = DECAY_SCALE * jax.nn.sigmoid(jnp.tanh(xw @ A_w) @ B_w + b_w)
            k = xk @ W_k
            v = xv @ W_v
            a = jax.nn.sigmoid(xa @ A_a @ B_a + b_a)
            g = jax.nn.sigmoid(xg @ A_g) @ B_g
            kk = k * k_k
            kk = kk / jnp.maximum(jnp.linalg.norm(kk, axis=-1, keepdims=True), 1e-12)
            k = k * (1.0 + (a - 1.0) * k_a)
            decay = jnp.exp(w)

            def step(S, inp):
                r_t, dec_t, k_t, v_t, kk_t, a_t = inp
                b_t = kk_t * a_t
                sa = jnp.einsum('bvk,bk->bv', S, -kk_t)
                S = S * dec_t[:, None, :] + sa[:, :, None] * b_t[:, None, :] + v_t[:, :, None] * k_t[:, None, :]
                o_t = jnp.einsum('bvk,bk->bv', S, r_t)
                return (S, o_t)
            tm = lambda z: jnp.swapaxes(z, 0, 1)
            S0 = jnp.zeros((b, d, d), x.dtype)
            _, o = jax.lax.scan(step, S0, (tm(r), tm(decay), tm(k), tm(v), tm(kk), tm(a)))
            o = jnp.swapaxes(o, 0, 1)
            mu = jnp.mean(o, axis=-1, keepdims=True)
            var = jnp.var(o, axis=-1, keepdims=True)
            o = (o - mu) * jax.lax.rsqrt(var + EPS) * gn_w + gn_b
            o = o + jnp.sum(r * k * r_k, axis=-1, keepdims=True) * v
            return o * g @ W_o
        return _forward(x, x_mix, W_r, W_k, W_v, W_o, A_w, B_w, b_w, A_a, B_a, b_a, A_g, B_g, k_k, k_a, r_k, gn_w, gn_b)

    def _L0_ffn_ref(x, attention_mask, wr, br, w1, b1, w2, b2):
        import jax, jax.numpy as jnp
        import numpy as np
        B, S, D = (8, 1024, 64)
        H = 4 * D
        CAPACITY = 0.5
        b, s, d = x.shape
        weights = (jnp.einsum('bsd,do->bso', x, wr) + br)[..., 0]
        k = max(1, int(CAPACITY * s))
        kk = k - 1 if k > 1 else 1
        _, idx = jax.lax.top_k(weights, k)
        sel_idx = idx[:, :kk]
        sel = jnp.take_along_axis(x, sel_idx[:, :, None], axis=1)
        h = jax.nn.gelu(jnp.einsum('bkd,dh->bkh', sel, w1) + b1)
        y = jnp.einsum('bkh,hd->bkd', h, w2) + b2
        w_sel = jnp.take_along_axis(weights, sel_idx, axis=1)
        y = y * w_sel[..., None]
        batch_idx = jnp.arange(b)[:, None]
        processed = jnp.zeros_like(x).at[batch_idx, sel_idx].set(y)
        return processed + x

    def _L1_attn_ref(x, Wq, bq, Wk, bk, Wv, bv):
        import jax, jax.numpy as jnp
        import numpy as np
        NUM_HEADS = 8

        def _to_heads(y, R, C, H, hd):
            y = y.reshape(R, C, H, hd).transpose(0, 2, 1, 3)
            y = jnp.transpose(y, (2, 1, 0, 3)).reshape(1, H, C, R * hd)
            return y

        def _reference_tuple_inner(x, Wq, bq, Wk, bk, Wv, bv):
            R, C, E = x.shape
            H = NUM_HEADS
            hd = E // H
            q = _to_heads(x @ Wq.T + bq, R, C, H, hd)
            k = _to_heads(x @ Wk.T + bk, R, C, H, hd)
            v = _to_heads(x @ Wv.T + bv, R, C, H, hd)
            d = q.shape[-1]
            q = jax.nn.softmax(q, axis=-1)
            k = jax.nn.softmax(k, axis=-2)
            q = q * jnp.asarray(float(d) ** 0.5, dtype=q.dtype)
            attn_weights = jnp.einsum('bhnd,bhmd->bhnm', q, k).sum(0)
            context = jnp.einsum('bhnd,bhne->bhde', k, v)
            out = jnp.einsum('bhnd,bhde->hbne', q, context)
            out = out.reshape(H, C, R, hd)
            out = jnp.transpose(out, (2, 1, 0, 3)).reshape(R, C, E)
            return (out, attn_weights)
        return _reference_tuple_inner(x, Wq, bq, Wk, bk, Wv, bv)[0]

    def _L1_ffn_ref(x, ln1_w, ln2_w, wq, wk, wv, wo, router_w, w1, w2, w3):
        import jax, jax.numpy as jnp
        import numpy as np
        B, T, C = (64, 96, 64)
        NH, NKV = (4, 2)
        HD = C // NH
        NREP = NH // NKV
        NE, TOPK = (8, 2)
        HID = int(8 / 3 * C)
        EPS_RMS = 1e-06

        def _rope_tables(t_len):
            inv_freq = 1.0 / 10000.0 ** (np.arange(0, HD, 2, dtype=np.float32) / HD)
            t = np.arange(t_len, dtype=np.float32)
            freqs = np.outer(t, inv_freq)
            emb = np.concatenate([freqs, freqs], axis=-1)
            return (jnp.asarray(np.cos(emb)), jnp.asarray(np.sin(emb)))

        def _rotate_half(x):
            h = x.shape[-1] // 2
            return jnp.concatenate([-x[..., h:], x[..., :h]], axis=-1)

        def _rmsnorm(v, w):
            return v * jax.lax.rsqrt(jnp.mean(v * v, axis=-1, keepdims=True) + EPS_RMS) * w
        Bx, Tx, Cx = x.shape
        h = _rmsnorm(x, ln1_w)
        q = (h @ wq.T).reshape(Bx, Tx, NH, HD).transpose(0, 2, 1, 3)
        k = (h @ wk.T).reshape(Bx, Tx, NKV, HD).transpose(0, 2, 1, 3)
        v = (h @ wv.T).reshape(Bx, Tx, NKV, HD).transpose(0, 2, 1, 3)
        cos, sin = _rope_tables(Tx)
        cos, sin = (cos[None, None], sin[None, None])
        q = q * cos + _rotate_half(q) * sin
        k = k * cos + _rotate_half(k) * sin
        k = jnp.repeat(k, NREP, axis=1)
        v = jnp.repeat(v, NREP, axis=1)
        scores = jnp.einsum('bhtd,bhsd->bhts', q, k) / jnp.sqrt(jnp.float32(HD))
        causal = jnp.tril(jnp.ones((Tx, Tx), dtype=bool))
        scores = jnp.where(causal[None, None], scores, jnp.float32(-1e+30))
        att = jax.nn.softmax(scores, axis=-1)
        y = jnp.einsum('bhts,bhsd->bhtd', att, v).transpose(0, 2, 1, 3).reshape(Bx, Tx, Cx)
        x = x + y @ wo.T
        flat = _rmsnorm(x, ln2_w).reshape(-1, Cx)
        probs = jax.nn.softmax(flat @ router_w.T, axis=-1)
        tp, ti = jax.lax.top_k(probs, TOPK)
        tp = tp / (jnp.sum(tp, axis=-1, keepdims=True) + 1e-09)
        weights = jnp.sum(tp[..., None] * jax.nn.one_hot(ti, NE, dtype=flat.dtype), axis=1)
        out = jnp.zeros_like(flat)
        for e in range(NE):
            hh = jax.nn.silu(flat @ w1[e].T) * (flat @ w3[e].T)
            out = out + weights[:, e:e + 1] * (hh @ w2[e].T)
        return x + out.reshape(Bx, Tx, Cx)

    def _L2_attn_ref(x, w_qkv, w_proj, qn_w, kn_w):
        import jax, jax.numpy as jnp
        import numpy as np
        EPS = 1e-06

        def _rmsnorm(x, w):
            xf = x.astype(jnp.float32)
            y = xf * jax.lax.rsqrt(jnp.mean(xf * xf, axis=-1, keepdims=True) + EPS)
            return y.astype(x.dtype) * w
        B, T, C = x.shape
        HD = 2
        H = C // HD
        qkv = x @ w_qkv.T
        q, k, v = jnp.split(qkv, 3, axis=-1)
        heads = lambda t: t.reshape(B, T, H, HD).transpose(0, 2, 1, 3)
        q = _rmsnorm(heads(q), qn_w)
        k = _rmsnorm(heads(k), kn_w)
        v = heads(v)
        scale = np.float32(1.0 / np.sqrt(HD))
        att = jnp.einsum('bhtd,bhsd->bhts', q, k) * scale
        causal = jnp.tril(jnp.ones((T, T), bool))
        att = jnp.where(causal, att, jnp.float32(-1e+30))
        att = jax.nn.softmax(att, axis=-1)
        y = jnp.einsum('bhts,bhsd->bhtd', att, v)
        y = y.transpose(0, 2, 1, 3).reshape(B, T, C)
        return y @ w_proj.T

    def _L2_ffn_ref(x, router_w, router_b, W1, b1, W2, b2):
        import jax, jax.numpy as jnp
        import numpy as np
        B, K, D = (128, 16, 64)
        E = 32
        H = int(D * 0.25)
        xf = x.reshape(-1, D)
        logits = xf @ router_w.T + router_b
        idx = jnp.argmax(logits, axis=-1)
        w1t = jnp.take(W1, idx, axis=0)
        h = jnp.einsum('nd,ndh->nh', xf, w1t) + jnp.take(b1, idx, axis=0)
        h = jax.nn.relu(h)
        w2t = jnp.take(W2, idx, axis=0)
        out = jnp.einsum('nh,nhd->nd', h, w2t) + jnp.take(b2, idx, axis=0)
        out = jax.nn.relu(out)
        return out.reshape(x.shape)

    def _L3_attn_ref(x, wq, wv, wk, fanout_w, a2a):
        import jax, jax.numpy as jnp
        import numpy as np
        import math
        D_MODEL = 64
        N_HEAD = 8
        BATCH = 2
        NTOK = 256
        A2LEN = 255

        def _linm(w, x):
            return jnp.einsum('oi,bti->bto', w[:, :-1], x) + w[:, -1]
        b, ntok, d = x.shape
        h = N_HEAD
        q = _linm(wq, x).reshape(b, ntok, h, d)
        v = _linm(wv, x).reshape(b, ntok, h, d)
        k = x[:, :, None, :] * wk[None, None, :, :]
        a2len = A2LEN
        qg, kg, vg = (q[:, a2a], k[:, a2a], v[:, a2a])
        padded = (a2len + 15) // 16 * 16
        padn = padded - a2len
        qq = jnp.pad(qg, ((0, 0), (0, padn), (0, 0), (0, 0)))
        kk = jnp.pad(kg, ((0, 0), (0, padn), (0, 0), (0, 0)))
        scale = 1.0 / math.sqrt(d)
        attn = -scale * jnp.sum(jnp.abs(qq[:, None, :, :, :] - kk[:, :, None, :, :]), axis=-1)
        a = attn[:, :a2len + 1, :a2len, :]
        a = a.at[:, a2len, :, :].set(0.0)
        a = jax.nn.softmax(a, axis=1)
        a = a[:, :a2len]
        bb = jnp.einsum('bsdh,bshw->bdhw', a, vg)
        bout = jnp.zeros((b, ntok, h, d), x.dtype).at[:, a2a].set(bb)
        bsum = jnp.sum(bout, axis=2)
        y = bsum * jax.nn.sigmoid(1.702 * bsum)
        y = _linm(fanout_w, y)
        return x + y

    def _L3_ffn_ref(h, gate_w, gate_b, w1, b1, w2, b2):
        import math
        import jax, jax.numpy as jnp
        import numpy as np
        CAPACITY_FACTOR = 1.25
        B, L, D = h.shape
        E = gate_w.shape[1]
        T = B * L
        C = max(1, math.ceil(CAPACITY_FACTOR * T / E))
        x = h.reshape(T, D)
        logits = x @ gate_w + gate_b
        probs = jax.nn.softmax(logits, axis=-1)
        idx = jnp.argmax(probs, axis=-1)
        prb = jnp.take_along_axis(probs, idx[:, None], axis=1)[:, 0]
        one_hot = jax.nn.one_hot(idx, E, dtype=jnp.float32)
        pos = (jnp.cumsum(one_hot, axis=0) * one_hot).sum(-1).astype(jnp.int32) - 1
        kept = pos < C
        pos_safe = jnp.where(kept, pos, C)
        buf = jnp.zeros((E, C, D), dtype=h.dtype).at[idx, pos_safe].set(x, mode='drop')
        hmid = jax.nn.relu(jnp.einsum('ecd,edf->ecf', buf, w1) + b1[:, None, :])
        ybuf = jnp.einsum('ecf,efd->ecd', hmid, w2) + b2[:, None, :]
        pos_g = jnp.minimum(pos, C - 1)
        y_tok = ybuf[idx, pos_g] * (prb * kept)[:, None]
        y = y_tok.reshape(B, L, D)
        y = jnp.nan_to_num(y, nan=0.0, posinf=10000.0, neginf=-10000.0)
        return y
    h = _L0_tok_ref(x, L0_tok_W)
    h = jnp.concatenate([jnp.broadcast_to(cls_tok, (h.shape[0], 1, h.shape[2])), h], axis=1)
    h = h + _L0_attn_ref(_layernorm(h, axis=-1), L0_attn_x_mix, L0_attn_W_r, L0_attn_W_k, L0_attn_W_v, L0_attn_W_o, L0_attn_A_w, L0_attn_B_w, L0_attn_b_w, L0_attn_A_a, L0_attn_B_a, L0_attn_b_a, L0_attn_A_g, L0_attn_B_g, L0_attn_k_k, L0_attn_k_a, L0_attn_r_k, L0_attn_gn_w, L0_attn_gn_b)
    h = h + _L0_ffn_ref(_layernorm(h, axis=-1), L0_ffn_attention_mask, L0_ffn_wr, L0_ffn_br, L0_ffn_w1, L0_ffn_b1, L0_ffn_w2, L0_ffn_b2)
    h = h + _L1_attn_ref(_layernorm(h, axis=-1), L1_attn_Wq, L1_attn_bq, L1_attn_Wk, L1_attn_bk, L1_attn_Wv, L1_attn_bv)
    h = h + _L1_ffn_ref(_layernorm(h, axis=-1), L1_ffn_ln1_w, L1_ffn_ln2_w, L1_ffn_wq, L1_ffn_wk, L1_ffn_wv, L1_ffn_wo, L1_ffn_router_w, L1_ffn_w1, L1_ffn_w2, L1_ffn_w3)
    h = h + _L2_attn_ref(_layernorm(h, axis=-1), L2_attn_w_qkv, L2_attn_w_proj, L2_attn_qn_w, L2_attn_kn_w)
    h = h + _L2_ffn_ref(_layernorm(h, axis=-1), L2_ffn_router_w, L2_ffn_router_b, L2_ffn_W1, L2_ffn_b1, L2_ffn_W2, L2_ffn_b2)
    h = h + _L3_attn_ref(_layernorm(h, axis=-1), L3_attn_wq, L3_attn_wv, L3_attn_wk, L3_attn_fanout_w, L3_attn_a2a)
    h = h + _L3_ffn_ref(_layernorm(h, axis=-1), L3_ffn_gate_w, L3_ffn_gate_b, L3_ffn_w1, L3_ffn_b1, L3_ffn_w2, L3_ffn_b2)
    return h

_drawn_inputs = setup_inputs


def setup_inputs(seed=0):
    import zlib

    import numpy as np

    out = dict(_drawn_inputs(seed))
    spreads = {'L0_attn_gn_w': (1.0, 0.2),
     'L0_attn_gn_b': (0.0, 0.1),
     'L0_ffn_b1': (0.0, 0.8),
     'L0_ffn_b2': (0.0, 0.784),
     'L1_ffn_ln1_w': (1.0, 0.6),
     'L1_ffn_ln2_w': (1.0, 0.6),
     'L2_attn_qn_w': (1.0, 0.6),
     'L2_attn_kn_w': (1.0, 0.6),
     'L3_attn_wk': (0.004999999888241291, 0.6),
     'L3_ffn_gate_b': (0.0, 0.305),
     'L3_ffn_b1': (0.0, 2.0),
     'L3_ffn_b2': (0.0, 2.0)}
    factors = {'L0_ffn_wr': 7.206,
     'L0_ffn_w1': 8.0,
     'L0_ffn_w2': 8.0,
     'L1_attn_Wq': 8.0,
     'L1_attn_bq': 8.0,
     'L1_attn_Wk': 8.0,
     'L1_attn_bk': 8.0,
     'L1_attn_bv': 5.86,
     'L1_ffn_wq': 8.0,
     'L1_ffn_wk': 8.0,
     'L1_ffn_wv': 8.0,
     'L1_ffn_wo': 8.0,
     'L1_ffn_router_w': 8.0,
     'L1_ffn_w1': 8.0,
     'L1_ffn_w2': 8.0,
     'L1_ffn_w3': 8.0,
     'L2_ffn_b1': 25.116,
     'L2_ffn_b2': 8.796,
     'L3_attn_wq': 200.0,
     'L3_attn_wv': 200.0,
     'L3_attn_fanout_w': 64.0,
     'L3_ffn_w1': 8.474,
     'L2_ffn_router_b': 3.817,
     'L2_ffn_W1': 3.054,
     'L3_ffn_gate_w': 3.315}
    for name, (base, spread) in spreads.items():
        noise = np.random.default_rng([zlib.crc32(name.encode()), seed]).standard_normal(out[name].shape)
        drawn = base * np.exp(spread * noise) if base else spread * noise
        out[name] = jnp.asarray(drawn.astype(out[name].dtype))
    for name, factor in factors.items():
        out[name] = (out[name] * factor).astype(out[name].dtype)
    return out
```

```python
from contextlib import ExitStack

import numpy as np

import concourse.bass as bass
from concourse import mybir

ALU = mybir.AluOpType
ACT = mybir.ActivationFunctionType
F32 = mybir.dt.float32
I32 = mybir.dt.int32
BF16 = mybir.dt.bfloat16
AX = mybir.AxisListType

B = 2
D = 64
SEQ = 1025
P = 114
NT = 9
T = B * NT
PADSEQ = P * NT
COLS = B * PADSEQ
GRP = 3 * P
NG = T // 3
LAST = P - 2
DECAY = -0.6065306597126334
MID = 56
LEVELS = (2, 4, 8, 16, 32, 64)


class Chain:

    def __init__(self, eng, sem):
        self.eng, self.sem, self.n = eng, sem, 0

    def __call__(self, ins):
        self.n += 1
        ins.then_inc(self.sem, 1)
        self.eng.wait_ge(self.sem, self.n)


def constants():
    c = {}
    ident = np.eye(128, dtype=np.float32)
    c["c_ident"] = ident
    c["c_ident2"] = np.concatenate([np.eye(64), np.eye(64)]).astype(np.float32)
    dft = np.zeros((128, 9, 16), np.float64)
    for slot in range(18):
        f, imag = slot % 9, slot // 9
        ang = 2 * np.pi * f * np.arange(16) / 16
        row = (-np.sin(ang) if imag else np.cos(ang)) / 4.0
        dft[(slot % 2) * 64:(slot % 2) * 64 + 64, slot // 2, :] = row
    c["c_dft"] = dft.astype(np.float32)
    s = np.arange(P)[:, None]
    t = np.arange(P)[None, :]
    mid = (s <= MID).astype(np.float64)
    rel = np.stack([(s <= t) - mid, (s < t) - mid], 1)
    c["c_rel"] = rel.astype(np.float32)
    c["c_sums"] = np.concatenate([s <= MID, s > MID], 1).astype(np.float32)
    c["c_mask4"] = np.stack([-(s < t).astype(float), (s <= t), -(s < t).astype(float), (s <= t)], 1).astype(np.float32)
    lev = []
    for l in (1,) + LEVELS:
        lev.append(((s // (2 * l)) == (t // (2 * l))) & ((s // l) % 2 == 0) & ((t // l) % 2 == 1))
    c["c_levels"] = np.stack(lev, 1).astype(np.float32)
    c["c_sub"] = -lev[0].T.astype(np.float32)
    c["c_before"] = (t < s).astype(np.float32)
    rm = np.ones((P, 1), np.float32)
    rm[P - 1] = 0.0
    c["c_rowmask"] = rm
    blk = np.arange(128)
    c["c_block16"] = ((blk[:, None] // 16) == (blk[None, :] // 16)).astype(np.float32)
    inv = 1.0 / 10000.0 ** (np.arange(0, 16, 2, dtype=np.float32) / 16)
    freqs = np.outer(np.arange(PADSEQ, dtype=np.float32), inv)
    cos, sin = np.cos(freqs), np.sin(freqs)
    rope = np.stack([np.concatenate([cos, cos], 1), np.concatenate([-sin, sin], 1)], 1)
    c["c_rope"] = np.ascontiguousarray(rope.reshape(NT, P, 2, 16).transpose(1, 2, 0, 3)).astype(np.float32)
    c["c_negmask"] = np.where(t > s, np.float32(-1e30), np.float32(0))
    e = np.arange(8)
    c["c_before8"] = np.tile((e[None, :] < e[:, None]).astype(np.float32).reshape(1, 8, 8), (P, 1, 1))
    c["c_causal"] = (t >= s).astype(np.float32)
    for n in (8, 32):
        c[f"c_eye{n}"] = np.eye(n, dtype=np.float32)
        c[f"c_first{n}"] = np.tile(np.arange(n, 0, -1, dtype=np.float32)[None, :], (P, 1))
    c["c_token"] = np.ascontiguousarray(np.arange(PADSEQ, dtype=np.float32).reshape(NT, P).T)
    c["c_tokenrow"] = np.arange(PADSEQ, dtype=np.float32)
    half = (np.arange(128) // 16) % 2
    c["c_half"] = np.stack([half == 0, half == 1], 1).astype(np.float32)
    win = np.zeros((128, 47), np.float32)
    win[:64, 15] = 2.0
    win[64:, 31] = 2.0
    c["c_window"] = win
    own = -((np.arange(128)[:, None] // 64) == half[None, :]).astype(np.float32)
    c["c_own"] = np.stack([own, np.where(np.isin(np.arange(128), (111, 127)), 0, own)], 1).astype(np.float32)
    return c


def bc(ap, n):
    return ap.unsqueeze(1).to_broadcast([ap.shape[0], n, ap.shape[1]])


def bcl(ap, w):
    return ap.unsqueeze(2).to_broadcast([ap.shape[0], ap.shape[1], w])


class Core:

    def __init__(self, nc, A, ctx):
        self.nc, self.A, self.ctx = nc, A, ctx
        self.ps = ctx.enter_context(nc.psum_tensor("ps", [128, 8, 512], F32))
        self.h = self.sb("h", [P, T, D])
        self.ident = self.sb("ident", [128, 128])
        self.written = nc.alloc_semaphore(name="out_written")
        self.sems = []

    def sb(self, name, shape, dt=F32, ctx=None):
        return (ctx or self.ctx).enter_context(self.nc.sbuf_tensor(name, shape, dt))

    def sem(self, name):
        self.sems.append(self.nc.alloc_semaphore(name=name))
        return self.sems[-1]

    def recycle_semaphores(self):
        with self.nc.Block() as block:
            @block.gpsimd
            def _(pool):
                self.nc.clear_and_free_semaphores(self.sems)
        self.sems = []


def row(ap, n):
    return ap.unsqueeze(0).to_broadcast([n, ap.shape[0]])


def transposes(nc, K, src, rows, cols, done, free=None):
    for g in range(NG):
        if free is not None:
            free(g)
        for j in range(3):
            ins = nc.tensor.transpose(K.ps[0:cols, g, j * rows:(j + 1) * rows], src(3 * g + j),
                                      K.ident[0:rows, 0:rows])
        ins.then_inc(done, 1)


def layernorm_dve(nc, dve, link, x, out, tmp, st, var_ready, std_ready, eps=1e-5):
    w = x.shape[2]
    link(nc.vector.tensor_reduce(st[:, 0, :], x, AX.X, ALU.add))
    link(nc.vector.tensor_scalar(st[:, 0, :], st[:, 0, :], 1.0 / w, None, ALU.mult))
    link(nc.vector.tensor_tensor(out, x, bcl(st[:, 0, :], w), ALU.subtract))
    link(nc.vector.tensor_tensor(tmp, out, out, ALU.mult))
    link(nc.vector.tensor_reduce(st[:, 1, :], tmp, AX.X, ALU.add))
    nc.vector.tensor_scalar(st[:, 1, :], st[:, 1, :], 1.0 / w, eps, ALU.mult, ALU.add).then_inc(var_ready, 1)
    dve.wait_ge(std_ready, 1)
    link(nc.vector.reciprocal(st[:, 3, :], st[:, 2, :]))
    link(nc.vector.tensor_tensor(out, out, bcl(st[:, 3, :], w), ALU.mult))


def root_act(nc, act, st, var_ready, std_ready, n=1):
    act.wait_ge(var_ready, n)
    nc.scalar.activation(st[:, 2, :], st[:, 1, :], ACT.Sqrt).then_inc(std_ready, 1)


def stage_embed(nc, K, A):
    with ExitStack() as ctx:
        sb = lambda n, s: K.sb("em_" + n, s, ctx=ctx)
        sem = lambda n: K.sem("em_" + n)
        W = sb("W", [64, 1152])
        WT = sb("WT", [128, 9, 64])
        id2 = sb("id2", [128, 64])
        dft = sb("dft", [128, 9, 16])
        kron = sb("kron", [128, 9, 16, 64])
        Wc = sb("Wc", [128, 8, 64])
        xs = sb("xs", [128, 2, 68, 64])
        XT = sb("XT", [64, COLS])
        w_in, id_in, x_in, cls_in = sem("w_in"), sem("id_in"), [sem("x_in0"), sem("x_in1")], sem("cls_in")
        wt_ps, wt_sb, kron_ok, wc_ps, wc_sb = sem("wt_ps"), sem("wt_sb"), sem("kron_ok"), sem("wc_ps"), sem("wc_sb")
        emb_ps, emb_sb, tr_ps, h_ok = sem("emb_ps"), sem("emb_sb"), sem("tr_ps"), sem("h_ok")
        ps = K.ps
        x = A["x"]
        with nc.Block() as block:
            @block.sync
            def _(sp):
                sp.dma_start(W[:], A["L0_tok_W"]).then_inc(w_in, 16)
                sp.dma_start(K.ident[:], A["c_ident"]).then_inc(id_in, 16)
                sp.dma_start(id2[:], A["c_ident2"]).then_inc(id_in, 16)
                sp.dma_start(dft[:], A["c_dft"]).then_inc(id_in, 16)
                for b in range(2):
                    v = x[b].rearrange("c (t p) v -> p c t v", p=2)
                    for par in range(2):
                        sp.dma_start(xs[64 * par:64 * par + 64, b, 0:64, :], v[par]).then_inc(x_in[b], 16)
                        sp.dma_start(xs[64 * par:64 * par + 64, b, 64:68, :],
                                     x[b, :, 127:128, :].to_broadcast([64, 4, 64])).then_inc(x_in[b], 16)
                    sp.dma_start(XT[:, b * PADSEQ:b * PADSEQ + 1],
                                 A["cls_tok"][0, 0, :].unsqueeze(1)).then_inc(cls_in, 16)

            @block.vector
            def _(dve):
                dve.wait_ge(id_in, 48)
                for k in range(9):
                    nc.vector.tensor_tensor(kron[:, k], bc(id2[:], 16), bcl(dft[:, k, :], 64),
                                            ALU.mult).then_inc(kron_ok, 1)
                for b in range(2):
                    nc.vector.memset(XT[:, b * PADSEQ + SEQ:(b + 1) * PADSEQ], 0.0).then_inc(emb_sb, 1)
                for q in range(4):
                    dve.wait_ge(emb_ps, q + 1)
                    c0 = (q // 2) * PADSEQ + 1 + 512 * (q % 2)
                    nc.vector.tensor_copy(XT[:, c0:c0 + 512], ps[0:64, 4 + q, :]).then_inc(emb_sb, 1)
                for g in range(NG):
                    dve.wait_ge(tr_ps, g + 1)
                    nc.vector.tensor_copy(K.h[:, 3 * g:3 * g + 3, :].rearrange("p a b -> p (a b)"),
                                          ps[0:P, g, 0:192]).then_inc(h_ok, 1)

            @block.scalar
            def _(act):
                act.wait_ge(wt_ps, 1)
                nc.scalar.copy(WT[:, 0:8, :].rearrange("p a b -> p (a b)"), ps[:, 0, :]).then_inc(wt_sb, 1)
                nc.scalar.copy(WT[:, 8, :], ps[:, 1, 0:64]).then_inc(wt_sb, 1)
                act.wait_ge(wc_ps, 1)
                nc.scalar.copy(Wc[:].rearrange("p a b -> p (a b)"), ps[:, 2, :]).then_inc(wc_sb, 1)

            @block.tensor
            def _(pe):
                pe.wait_ge(w_in, 16)
                pe.wait_ge(id_in, 48)
                for k in range(9):
                    ins = nc.tensor.transpose(ps[:, k // 8, (k % 8) * 64:(k % 8) * 64 + 64],
                                              W[:, k * 128:(k + 1) * 128], K.ident[0:64, 0:64])
                ins.then_inc(wt_ps, 1)
                pe.wait_ge(wt_sb, 2)
                pe.wait_ge(kron_ok, 9)
                for j in range(8):
                    for k in range(9):
                        ins = nc.tensor.matmul(ps[:, 2, j * 64:(j + 1) * 64],
                                               kron[:, k, 2 * j:2 * j + 2, :].rearrange("p a b -> p (a b)"),
                                               WT[:, k, :], start=(k == 0), stop=(k == 8))
                ins.then_inc(wc_ps, 1)
                pe.wait_ge(wc_sb, 1)
                for b in range(2):
                    pe.wait_ge(x_in[b], 64)
                    for half in range(2):
                        for j in range(8):
                            ins = nc.tensor.matmul(
                                ps[0:64, 4 + 2 * b + half, :], Wc[:, j, :],
                                xs[:, b, j:j + 61:4, 32 * half:32 * half + 32].rearrange("p n v -> p v n"),
                                start=(j == 0), stop=(j == 7))
                        ins.then_inc(emb_ps, 1)
                pe.wait_ge(emb_sb, 6)
                pe.wait_ge(cls_in, 32)
                for g in range(NG):
                    for j in range(3):
                        t = 3 * g + j
                        ins = nc.tensor.transpose(ps[0:P, g, j * 64:(j + 1) * 64], XT[:, t * P:(t + 1) * P],
                                                  K.ident[0:64, 0:64])
                    ins.then_inc(tr_ps, 1)


def stage_rwkv(nc, K, A):
    outer = ExitStack()
    with outer:
        sb = lambda n, s: K.sb("rw_" + n, s, ctx=outer)
        TM = sb("TM", [P, T, 384])
        rwkv_projections(nc, K, A, TM)
        QT = sb("QT", [64, T, 4, P])
        Bt = sb("Bt", [P, T, 64])
        Kt = sb("Kt", [P, T, 64])
        Y = sb("Y", [P, T, 128])
        bonus = sb("bonus", [P, T])
        F = sb("F", [64, T])
        rwkv_scaled(nc, K, A, TM, QT, Bt, Kt, Y, bonus, F)
        O = sb("O", [P, T, 64])
        rwkv_chunks(nc, K, A, TM, QT, Bt, Kt, Y, F, O)
        rwkv_output(nc, K, A, TM, O, bonus)


R_, K_, V_, G_, W_, A_ = (slice(64 * i, 64 * i + 64) for i in range(6))


def rwkv_projections(nc, K, A, TM):
    with ExitStack() as ctx:
        sb = lambda n, s: K.sb("rp_" + n, s, ctx=ctx)
        sem = lambda n: K.sem("rp_" + n)
        ps, ident = K.ps, K.ident
        x2 = sb("x2", [P, T, 128])
        tmp = sb("tmp", [P, T, 64])
        st = sb("st", [P, 4, T])
        S = sb("S", [128, 2, PADSEQ + 1])
        mix = sb("mix", [128, 6])
        WA = sb("WA", [128, 512])
        BB = sb("BB", [128, 128])
        BG = sb("BG", [128, 64])
        H1 = sb("H1", [128, COLS])
        H2 = sb("H2", [128, COLS])
        w_in, mix_in, z_ok, wmix = sem("w_in"), sem("mix_in"), sem("zeros"), sem("wmix")
        chain, var_ready, std_ready, x_ready, x_twice = (sem("chain"), sem("var"), sem("std"), sem("x"), sem("x_twice"))
        tr_ps, s_top, s_bot = sem("tr_ps"), sem("s_top"), sem("s_bottom")
        hid_ps, hid_sb, sig_sb = sem("hid_ps"), sem("hid_sb"), sem("sig_sb")
        tm_ps, tm_act, tm_dve = sem("tm_ps"), sem("tm_act"), sem("tm_dve")
        order = ((0, "W_r", 0, 64), (2, "W_k", 64, 64), (3, "W_v", 128, 64), (1, "A_w", 192, 64),
                 (4, "A_a", 256, 64), (5, "A_g", 320, 128))
        with nc.Block() as block:
            @block.sync
            def _(sp):
                for half in range(2):
                    rows = slice(64 * half, 64 * half + 64)
                    for _, name, c, n in order:
                        sp.dma_start(WA[rows, c:c + n], A["L0_attn_" + name]).then_inc(w_in, 16)
                    with nc.allow_non_contiguous_dma(reason="six columns"):
                        sp.dma_start(mix[rows, :], A["L0_attn_x_mix"].rearrange("i d -> d i")).then_inc(mix_in, 16)
                sp.wait_ge(z_ok, 1)
                sp.dma_start(BB[0:64, 0:64], A["L0_attn_B_w"]).then_inc(w_in, 16)
                sp.dma_start(BB[64:128, 64:128], A["L0_attn_B_a"]).then_inc(w_in, 16)
                sp.dma_start(BG[:], A["L0_attn_B_g"]).then_inc(w_in, 16)

            @block.gpsimd
            def _(pool):
                nc.gpsimd.memset(BB[:], 0.0).then_inc(z_ok, 1)
                pool.wait_ge(z_ok, 1)
                nc.gpsimd.memset(S[64:128, :, 0:1], 0.0).then_inc(z_ok, 1)
                pool.wait_ge(z_ok, 2)
                pool.wait_ge(x_ready, 1)
                nc.gpsimd.tensor_copy(x2[:, :, 64:128], x2[:, :, 0:64]).then_inc(x_twice, 1)

            @block.vector
            def _(dve):
                link = Chain(dve, chain)
                layernorm_dve(nc, dve, link, K.h[:], x2[:, :, 0:64], tmp[:], st[:], var_ready, std_ready)
                nc.vector.tensor_copy(st[:, 0, :], st[:, 1, :]).then_inc(x_ready, 1)
                dve.wait_ge(mix_in, 32)
                link(nc.vector.tensor_scalar(mix[0:64, :], mix[0:64, :], -1.0, 1.0, ALU.mult, ALU.add))
                dve.wait_ge(w_in, 240)
                for i, _, c, n in order:
                    nc.vector.tensor_scalar(WA[:, c:c + n], WA[:, c:c + n], mix[:, i:i + 1], None,
                                            ALU.mult).then_inc(wmix, 1)
                for g in range(NG):
                    dve.wait_ge(tr_ps, g + 1)
                    c0 = (g % 3) * GRP + 1
                    nc.vector.tensor_copy(S[64:128, g // 3, c0:c0 + GRP], ps[64:128, g, 0:GRP]).then_inc(s_bot, 1)
                for g in range(NG):
                    dve.wait_ge(hid_ps, 2 * g + 1)
                    nc.vector.tensor_copy(H1[64:128, g * GRP:(g + 1) * GRP],
                                          ps[64:128, (2 * g) % 8, 0:GRP]).then_inc(hid_sb, 1)
                for t in range(1, T, 2):
                    dve.wait_ge(tm_ps, t + 1)
                    nc.vector.tensor_copy(TM[:, t, :], ps[0:P, t % 8, 0:384]).then_inc(tm_dve, 1)

            @block.scalar
            def _(act):
                root_act(nc, act, st[:], var_ready, std_ready)
                for g in range(NG):
                    act.wait_ge(tr_ps, g + 1)
                    nc.scalar.copy(S[0:64, g // 3, (g % 3) * GRP:(g % 3 + 1) * GRP],
                                   ps[0:64, g, 0:GRP]).then_inc(s_top, 1)
                for g in range(NG):
                    cols = slice(g * GRP, (g + 1) * GRP)
                    act.wait_ge(hid_ps, 2 * g + 1)
                    nc.scalar.activation(H1[0:64, cols], ps[0:64, (2 * g) % 8, 0:GRP], ACT.Tanh).then_inc(sig_sb, 1)
                    act.wait_ge(hid_ps, 2 * g + 2)
                    nc.scalar.activation(H2[:, cols], ps[:, (2 * g + 1) % 8, 0:GRP], ACT.Sigmoid).then_inc(sig_sb, 1)
                for t in range(0, T, 2):
                    act.wait_ge(tm_ps, t + 1)
                    nc.scalar.copy(TM[:, t, :], ps[0:P, t % 8, 0:384]).then_inc(tm_act, 1)

            @block.tensor
            def _(pe):
                pe.wait_ge(x_ready, 1)
                pe.wait_ge(x_twice, 1)
                transposes(nc, K, lambda t: x2[:, t, :], P, 128, tr_ps)
                pe.wait_ge(wmix, 6)
                pe.wait_ge(z_ok, 2)
                pe.wait_ge(w_in, 240)
                pe.wait_ge(s_top, NG)
                pe.wait_ge(s_bot, NG)
                for g in range(NG):
                    if g >= 4:
                        pe.wait_ge(hid_sb, g - 3)
                        pe.wait_ge(sig_sb, 2 * g - 6)
                    rhs = S[:, g // 3, (g % 3) * GRP:(g % 3 + 1) * GRP]
                    nc.tensor.matmul(ps[:, (2 * g) % 8, 0:GRP], WA[:, 192:320], rhs,
                                     start=True, stop=True).then_inc(hid_ps, 1)
                    nc.tensor.matmul(ps[:, (2 * g + 1) % 8, 0:GRP], WA[:, 320:448], rhs,
                                     start=True, stop=True).then_inc(hid_ps, 1)
                pe.wait_ge(hid_sb, NG)
                pe.wait_ge(sig_sb, 2 * NG)
                for t in range(T):
                    if t >= 8:
                        if t % 2:
                            pe.wait_ge(tm_dve, (t - 8) // 2 + 1)
                        else:
                            pe.wait_ge(tm_act, (t - 8) // 2 + 1)
                    o = ps[0:P, t % 8, :]
                    c = slice(t * P, (t + 1) * P)
                    i = (t % NT) * P
                    nc.tensor.matmul(o[:, 0:192], S[:, t // NT, i:i + P], WA[:, 0:192], start=True, stop=True)
                    nc.tensor.matmul(o[:, 192:256], H2[:, c], BG[:], start=True, stop=True)
                    nc.tensor.matmul(o[:, 256:384], H1[:, c], BB[:], start=True, stop=True).then_inc(tm_ps, 1)


def rwkv_scaled(nc, K, A, TM, QT, Bt, Kt, Y, bonus, F):
    with ExitStack() as ctx:
        sb = lambda n, s: K.sb("rs_" + n, s, ctx=ctx)
        sem = lambda n: K.sem("rs_" + n)
        ps, ident = K.ps, K.ident
        rows = sb("rows", [P, 5, 64])
        rel = sb("rel", [P, 2, P])
        sums = sb("sums", [P, 2])
        kk = sb("kk", [P, T, 64])
        tmp = sb("tmp", [P, T, 64])
        tmp2 = sb("tmp2", [P, T, 64])
        b_ = sb("b", [P, T, 64])
        Rt = sb("Rt", [P, T, 64])
        KK = sb("KK", [P, T, 64])
        E1 = sb("E1", [P, T, 64])
        E2 = sb("E2", [P, T, 64])
        E3 = sb("E3", [P, T, 64])
        st = sb("st", [P, 4, T])
        lm = sb("lm", [64, T, 2])
        c_in, chain, achain = sem("c_in"), sem("chain"), sem("achain")
        biased, gated, nsq, nroot, logw_ok, cum_ps = (sem("biased"), sem("gated"), sem("nsq"), sem("nroot"),
                                                      sem("logw"), sem("cum_ps"))
        e_ok, scaled, tr_ps, tr_act, tr_dve, lm_ps = (sem("exps"), sem("scaled"), sem("tr_ps"), sem("tr_act"),
                                                      sem("tr_dve"), sem("lm_ps"))
        f_sum, f_ok = sem("f_sum"), sem("f_ok")
        flat = lambda a: a.rearrange("p a b -> p (a b)")
        with nc.Block() as block:
            @block.sync
            def _(sp):
                for i, n in enumerate(("b_w", "b_a", "k_k", "k_a", "r_k")):
                    sp.dma_start(rows[:, i, :], row(A["L0_attn_" + n], P)).then_inc(c_in, 16)
                sp.dma_start(rel[:], A["c_rel"]).then_inc(c_in, 16)
                sp.dma_start(sums[:], A["c_sums"]).then_inc(c_in, 16)

            @block.vector
            def _(dve):
                link = Chain(dve, chain)
                tt, stt = nc.vector.tensor_tensor, nc.vector.scalar_tensor_tensor
                dve.wait_ge(c_in, 112)
                tt(TM[:, :, W_], TM[:, :, W_], bc(rows[:, 0], T), ALU.add).then_inc(biased, 1)
                tt(TM[:, :, A_], TM[:, :, A_], bc(rows[:, 1], T), ALU.add).then_inc(biased, 1)
                link(tt(kk[:], TM[:, :, K_], bc(rows[:, 2], T), ALU.mult))
                link(tt(tmp[:], kk[:], kk[:], ALU.mult))
                nc.vector.tensor_reduce(st[:, 0, :], tmp[:], AX.X, ALU.add).then_inc(nsq, 1)
                dve.wait_ge(gated, 2)
                nc.vector.tensor_scalar(TM[:, :, W_], TM[:, :, W_], DECAY, None, ALU.mult).then_inc(logw_ok, 1)
                dve.wait_ge(nroot, 1)
                link(nc.vector.tensor_scalar(st[:, 1, :], st[:, 1, :], 1e-12, None, ALU.max))
                link(nc.vector.reciprocal(st[:, 2, :], st[:, 1, :]))
                link(tt(kk[:], kk[:], bcl(st[:, 2, :], 64), ALU.mult))
                link(tt(b_[:], kk[:], TM[:, :, A_], ALU.mult))
                link(stt(tmp[:], TM[:, :, A_], -1.0, bc(rows[:, 3], T), ALU.add, ALU.mult))
                link(stt(TM[:, :, K_], tmp[:], 1.0, TM[:, :, K_], ALU.add, ALU.mult))
                link(tt(tmp[:], TM[:, :, K_], bc(rows[:, 4], T), ALU.mult))
                link(tt(tmp2[:], tmp[:], TM[:, :, R_], ALU.mult))
                link(nc.vector.tensor_reduce(bonus[:], tmp2[:], AX.X, ALU.add))
                dve.wait_ge(e_ok, 3)
                tt(KK[:], kk[:], E3[:], ALU.mult).then_inc(scaled, 1)
                tt(Rt[:], TM[:, :, R_], E1[:], ALU.mult).then_inc(scaled, 1)
                tt(Bt[:], b_[:], E2[:], ALU.mult).then_inc(scaled, 1)
                tt(Kt[:], TM[:, :, K_], E2[:], ALU.mult).then_inc(scaled, 1)
                dve.wait_ge(scaled, 4)
                nc.vector.tensor_scalar(Y[:, :, 64:128], KK[:], -1.0, None, ALU.mult)
                dve.wait_ge(lm_ps, 1)
                link(nc.vector.tensor_copy(flat(lm[:]), ps[0:64, 6, 0:2 * T]))
                link(nc.vector.tensor_copy(F[:], lm[:, :, 1]))
                for b in range(2):
                    tt(F[:, b * NT:b * NT + NT - 1], lm[:, b * NT:b * NT + NT - 1, 1],
                       lm[:, b * NT + 1:b * NT + NT, 0], ALU.add).then_inc(f_sum, 1)
                for t in range(1, T, 2):
                    dve.wait_ge(tr_ps, t + 1)
                    nc.vector.tensor_copy(QT[:, t].rearrange("p a b -> p (a b)"),
                                          ps[0:64, t % 4, 0:4 * P]).then_inc(tr_dve, 1)

            @block.scalar
            def _(act):
                act.wait_ge(biased, 2)
                nc.scalar.activation(TM[:, :, W_], TM[:, :, W_], ACT.Sigmoid).then_inc(gated, 1)
                nc.scalar.activation(TM[:, :, A_], TM[:, :, A_], ACT.Sigmoid).then_inc(gated, 1)
                act.wait_ge(nsq, 1)
                nc.scalar.activation(st[:, 1, :], st[:, 0, :], ACT.Sqrt).then_inc(nroot, 1)
                act.wait_ge(cum_ps, 6)
                three = lambda a: flat(a[:]).rearrange("p (a b) -> p a b", a=3)
                nc.scalar.activation(three(E1), ps[0:P, 0:3, 0:384], ACT.Exp).then_inc(e_ok, 1)
                nc.scalar.activation(three(E2), ps[0:P, 0:3, 0:384], ACT.Exp, scale=-1.0).then_inc(e_ok, 1)
                nc.scalar.activation(three(E3), ps[0:P, 3:6, 0:384], ACT.Exp).then_inc(e_ok, 1)
                act.wait_ge(f_sum, 2)
                nc.scalar.activation(F[:], F[:], ACT.Exp).then_inc(f_ok, 1)
                for t in range(0, T, 2):
                    act.wait_ge(tr_ps, t + 1)
                    nc.scalar.copy(QT[:, t].rearrange("p a b -> p (a b)"), ps[0:64, t % 4, 0:4 * P]).then_inc(tr_act, 1)

            @block.tensor
            def _(pe):
                pe.wait_ge(c_in, 112)
                pe.wait_ge(logw_ok, 1)
                for m in range(2):
                    for q in range(3):
                        nc.tensor.matmul(ps[0:P, 3 * m + q, 0:384], rel[:, m, :], TM[:, 6 * q:6 * q + 6, W_],
                                         start=True, stop=True).then_inc(cum_ps, 1)
                for t in range(T):
                    ins = nc.tensor.matmul(ps[0:64, 6, 2 * t:2 * t + 2], TM[:, t, W_], sums[:], start=True, stop=True)
                ins.then_inc(lm_ps, 1)
                pe.wait_ge(scaled, 4)
                for t in range(T):
                    if t >= 4:
                        pe.wait_ge(tr_dve if t % 2 else tr_act, (t - 4) // 2 + 1)
                    for j, src in enumerate((KK, Rt, Bt, Kt)):
                        ins = nc.tensor.transpose(ps[0:64, t % 4, j * P:(j + 1) * P], src[:, t, :], ident[0:P, 0:P])
                    ins.then_inc(tr_ps, 1)


def rwkv_chunks(nc, K, A, TM, QT, Bt, Kt, Y, F, O):
    with ExitStack() as ctx:
        sb = lambda n, s: K.sb("rc_" + n, s, ctx=ctx)
        ps, ident = K.ps, K.ident
        sem = lambda n: K.sem("rc_" + n)
        M4 = sb("M4", [P, T, 4, P])
        XX = sb("XX", [P, T, 2, P])
        mask4 = sb("mask4", [P, 4, P])
        lev = sb("lev", [P, 7, P])
        sub = sb("sub", [P, P])
        NL = sb("NL", [P, 2, T, P])
        T1 = sb("T1", [P, NT, 2, P])
        c_in, qk_ps, qk_sb, x0, nl_ok = sem("c_in"), sem("qk_ps"), sem("qk_sb"), sem("x0"), sem("nl")
        t1_ps, t1_sb, dx_ps, dx_ok, chain = sem("t1_ps"), sem("t1_sb"), sem("dx_ps"), sem("dx"), sem("chain")
        flat = lambda a: a.rearrange("p a b -> p (a b)")
        GRPS = T // 2
        N = len(LEVELS) * GRPS
        with nc.Block() as block:
            @block.sync
            def _(sp):
                sp.dma_start(mask4[:], A["c_mask4"]).then_inc(c_in, 16)
                sp.dma_start(lev[:], A["c_levels"]).then_inc(c_in, 16)
                sp.dma_start(sub[:], A["c_sub"]).then_inc(c_in, 16)

            @block.tensor
            def _(pe):
                for t in range(T):
                    if t >= 4:
                        pe.wait_ge(x0, t - 3)
                    bank = 2 * (t % 4)
                    kr = flat(QT[:, t, 0:2, :])
                    nc.tensor.matmul(ps[0:P, bank, 0:2 * P], QT[:, t, 2, :], kr, start=True, stop=True)
                    nc.tensor.matmul(ps[0:P, bank, 2 * P:4 * P], QT[:, t, 3, :], kr, start=True, stop=True)
                    nc.tensor.matmul(ps[0:P, bank + 1, 0:P], QT[:, t, 0, :], QT[:, t, 2, :],
                                     start=True, stop=True).then_inc(qk_ps, 1)
                pe.wait_ge(x0, T)

                def product(n):
                    g, lvl = n % GRPS, n // GRPS
                    pe.wait_ge(nl_ok, lvl + 1)
                    if lvl:
                        pe.wait_ge(dx_ok, n - GRPS + 1)
                    if n >= 4:
                        pe.wait_ge(t1_sb, n - 3)
                    for j in range(2):
                        ins = nc.tensor.matmul(ps[0:P, n % 4, j * P:(j + 1) * P], NL[:, lvl % 2, 2 * g + j, :],
                                               XX[:, 2 * g + j, 0, :], start=True, stop=True)
                    ins.then_inc(t1_ps, 1)

                def update(n):
                    g = n % GRPS
                    pe.wait_ge(t1_sb, n + 1)
                    if n >= 4:
                        pe.wait_ge(dx_ok, n - 3)
                    for j in range(2):
                        t = 2 * g + j
                        nc.tensor.matmul(ps[0:P, 4 + n % 4, 2 * j * P:(2 * j + 1) * P], XX[:, t, 1, :],
                                         T1[:, g, j, :], start=True, stop=True)
                        ins = nc.tensor.matmul(ps[0:P, 4 + n % 4, (2 * j + 1) * P:(2 * j + 2) * P], T1[:, g, j, :],
                                               XX[:, t, 1, :], start=True, stop=True)
                    ins.then_inc(dx_ps, 1)

                for n in range(N + 2):
                    if n < N:
                        product(n)
                    if n >= 2:
                        update(n - 2)

            @block.vector
            def _(dve):
                link = Chain(dve, chain)
                dve.wait_ge(c_in, 48)
                for t in range(T):
                    dve.wait_ge(qk_ps, t + 1)
                    bank = 2 * (t % 4)
                    link(nc.vector.tensor_tensor(flat(M4[:, t]), ps[0:P, bank, 0:4 * P], flat(mask4[:]), ALU.mult))
                    link(nc.vector.tensor_tensor(XX[:, t, 0, :], ps[0:P, bank + 1, 0:P], sub[:], ALU.mult))
                    link(nc.vector.tensor_tensor(XX[:, t, 1, :], M4[:, t, 0, :], lev[:, 0, :], ALU.mult))
                    nc.vector.tensor_tensor(XX[:, t], XX[:, t], bc(ident[0:P, 0:P], 2), ALU.add).then_inc(x0, 1)
                for n in range(N):
                    g = n % GRPS
                    dve.wait_ge(dx_ps, n + 1)
                    if n >= GRPS:
                        dve.wait_ge(dx_ok, n - GRPS + 1)
                    xx = XX[:, 2 * g:2 * g + 2].rearrange("p a b c -> p (a b c)")
                    nc.vector.tensor_tensor(xx, ps[0:P, 4 + n % 4, 0:4 * P], xx, ALU.add).then_inc(dx_ok, 1)

            @block.scalar
            def _(act):
                for n in range(N):
                    act.wait_ge(t1_ps, n + 1)
                    if n >= GRPS:
                        act.wait_ge(dx_ps, n - GRPS + 1)
                    nc.scalar.copy(flat(T1[:, n % GRPS]), ps[0:P, n % 4, 0:2 * P]).then_inc(t1_sb, 1)

            @block.gpsimd
            def _(pool):
                pool.wait_ge(x0, T)
                pool.wait_ge(c_in, 48)
                for lvl in range(len(LEVELS)):
                    if lvl >= 2:
                        pool.wait_ge(t1_ps, (lvl - 1) * GRPS)
                    nc.gpsimd.tensor_tensor(NL[:, lvl % 2], M4[:, :, 0, :], bc(lev[:, lvl + 1, :], T),
                                            ALU.mult).then_inc(nl_ok, 1)
        UZ = sb("UZ", [P, T, 128])
        GI = sb("GI", [64, T, 64])
        HF = sb("HF", [64, T, 64])
        R2 = sb("R2", [64, T, P])
        M = sb("M", [64, T, 64])
        by_ps, by_sb, uz_ps, uz_sb = sem("bv_ps"), sem("bv_sb"), sem("uz_ps"), sem("uz_sb")
        g_ps, g_sb, m_ps, m_sb, o_ps, o_sb = (sem("g_ps"), sem("g_sb"), sem("m_ps"), sem("m_sb"), sem("o_ps"),
                                              sem("o_sb"))
        with nc.Block() as block:
            @block.tensor
            def _(pe):
                for t in range(T):
                    ins = nc.tensor.matmul(ps[0:P, t // 6, (t % 6) * 64:(t % 6) * 64 + 64], M4[:, t, 2, :],
                                           TM[:, t, V_], start=True, stop=True)
                    if t % 6 == 5:
                        ins.then_inc(by_ps, 1)
                for g in range(NG):
                    pe.wait_ge(by_sb, g // 2 + 1)
                    if g >= 5:
                        pe.wait_ge(uz_sb, g - 4)
                    for t in range(3 * g, 3 * g + 3):
                        ins = nc.tensor.matmul(ps[0:P, 3 + g % 5, (t % 3) * 128:(t % 3) * 128 + 128], XX[:, t, 1, :],
                                               Y[:, t, :], start=True, stop=True)
                    ins.then_inc(uz_ps, 1)
                pe.wait_ge(uz_sb, NG)
                for t in range(T):
                    if t >= 4:
                        pe.wait_ge(g_sb, 3 * (t - 3))
                    o = ps[0:64, t % 4, :]
                    z = UZ[:, t, 64:128]
                    nc.tensor.matmul(o[:, 0:64], z, Bt[:, t, :], start=True, stop=True)
                    nc.tensor.matmul(o[:, 64:128], Bt[:, t, :], UZ[:, t, 0:64], start=True, stop=False)
                    nc.tensor.matmul(o[:, 64:128], Kt[:, t, :], TM[:, t, V_], start=False, stop=True)
                    nc.tensor.matmul(o[:, 128:128 + P], z, M4[:, t, 1, :], start=True, stop=True).then_inc(g_ps, 1)
                for c in range(1, NT - 1):
                    for b in range(2):
                        t = b * NT + c
                        pe.wait_ge(m_sb, 2 * c + b - 1)
                        pe.wait_ge(g_sb, 3 * T)
                        nc.tensor.matmul(ps[0:64, 4 + b, 0:64], GI[:, t, :], M[:, t, :],
                                         start=True, stop=True).then_inc(m_ps, 1)
                pe.wait_ge(m_sb, 2 * (NT - 1))
                for g in range(NG):
                    for t in range(3 * g, 3 * g + 3):
                        o = ps[0:P, g, (t % 3) * 64:(t % 3) * 64 + 64]
                        nc.tensor.matmul(o, M4[:, t, 1, :], UZ[:, t, 0:64], start=True, stop=False)
                        ins = nc.tensor.matmul(o, M4[:, t, 3, :], TM[:, t, V_], start=False, stop=(t % NT == 0))
                        if t % NT:
                            ins = nc.tensor.matmul(o, R2[:, t, :], M[:, t, :], start=False, stop=True)
                    ins.then_inc(o_ps, 1)

            @block.scalar
            def _(act):
                for q in range(3):
                    act.wait_ge(by_ps, q + 1)
                    nc.scalar.copy(Y[:, 6 * q:6 * q + 6, 0:64],
                                   ps[0:P, q, 0:384].rearrange("p (a b) -> p a b", a=6)).then_inc(by_sb, 1)
                for g in range(NG):
                    act.wait_ge(uz_ps, g + 1)
                    nc.scalar.copy(flat(UZ[:, 3 * g:3 * g + 3, :]), ps[0:P, 3 + g % 5, 0:384]).then_inc(uz_sb, 1)
                for g in range(NG):
                    act.wait_ge(o_ps, g + 1)
                    nc.scalar.copy(flat(O[:, 3 * g:3 * g + 3, :]), ps[0:P, g, 0:192]).then_inc(o_sb, 1)

            @block.vector
            def _(dve):
                for t in range(T):
                    dve.wait_ge(g_ps, t + 1)
                    o = ps[0:64, t % 4, :]
                    nc.vector.tensor_tensor(GI[:, t, :], o[:, 0:64], ident[0:64, 0:64], ALU.add).then_inc(g_sb, 1)
                    nc.vector.tensor_scalar(HF[:, t, :], o[:, 64:128], F[:, t:t + 1], None, ALU.mult).then_inc(g_sb, 1)
                    nc.vector.tensor_tensor(R2[:, t, :], o[:, 128:128 + P], QT[:, t, 1, :], ALU.add).then_inc(g_sb, 1)
                dve.wait_ge(g_sb, 3 * T)
                for b in range(2):
                    nc.vector.tensor_copy(M[:, b * NT + 1, :], HF[:, b * NT, :]).then_inc(m_sb, 1)
                for c in range(1, NT - 1):
                    for b in range(2):
                        t = b * NT + c
                        dve.wait_ge(m_ps, 2 * c + b - 1)
                        nc.vector.scalar_tensor_tensor(M[:, t + 1, :], ps[0:64, 4 + b, 0:64], F[:, t:t + 1],
                                                       HF[:, t, :], ALU.mult, ALU.add).then_inc(m_sb, 1)


def rwkv_output(nc, K, A, TM, O, bonus):
    with ExitStack() as ctx:
        sb = lambda n, s: K.sb("ro_" + n, s, ctx=ctx)
        sem = lambda n: K.sem("ro_" + n)
        ps = K.ps
        tmp = sb("tmp", [P, T, 64])
        on = sb("on", [P, T, 64])
        st = sb("st", [P, 4, T])
        gn = sb("gn", [P, 2, 64])
        Wo = sb("Wo", [64, 64])
        OT = sb("OT", [64, COLS])
        c_in, chain, var_ready, std_ready = sem("c_in"), sem("chain"), sem("var"), sem("std")
        o_ok, tr_ps, tr_sb, y_ps = sem("o_ok"), sem("tr_ps"), sem("tr_sb"), sem("y_ps")
        with nc.Block() as block:
            @block.sync
            def _(sp):
                sp.dma_start(gn[:, 0, :], row(A["L0_attn_gn_w"], P)).then_inc(c_in, 16)
                sp.dma_start(gn[:, 1, :], row(A["L0_attn_gn_b"], P)).then_inc(c_in, 16)
                sp.dma_start(Wo[:], A["L0_attn_W_o"]).then_inc(c_in, 16)

            @block.vector
            def _(dve):
                link = Chain(dve, chain)
                tt = nc.vector.tensor_tensor
                layernorm_dve(nc, dve, link, O[:], on[:], tmp[:], st[:], var_ready, std_ready, eps=64e-5)
                dve.wait_ge(c_in, 48)
                link(tt(on[:], on[:], bc(gn[:, 0], T), ALU.mult))
                link(tt(on[:], on[:], bc(gn[:, 1], T), ALU.add))
                link(tt(tmp[:], TM[:, :, V_], bcl(bonus[:], 64), ALU.mult))
                link(tt(on[:], on[:], tmp[:], ALU.add))
                tt(on[:], on[:], TM[:, :, G_], ALU.mult).then_inc(o_ok, 1)
                for g in range(NG):
                    dve.wait_ge(y_ps, g + 1)
                    hh = K.h[:, 3 * g:3 * g + 3, :].rearrange("p a b -> p (a b)")
                    tt(hh, ps[0:P, g, 0:192], hh, ALU.add)

            @block.scalar
            def _(act):
                root_act(nc, act, st[:], var_ready, std_ready)
                for g in range(NG):
                    act.wait_ge(tr_ps, g + 1)
                    nc.scalar.copy(OT[:, g * GRP:(g + 1) * GRP], ps[0:64, g, 0:GRP]).then_inc(tr_sb, 1)

            @block.tensor
            def _(pe):
                pe.wait_ge(o_ok, 1)
                transposes(nc, K, lambda t: on[:, t, :], P, 64, tr_ps)
                pe.wait_ge(c_in, 48)
                for g in range(NG):
                    pe.wait_ge(tr_sb, g + 1)
                    for j in range(3):
                        t = 3 * g + j
                        ins = nc.tensor.matmul(ps[0:P, g, j * 64:(j + 1) * 64], OT[:, t * P:(t + 1) * P], Wo[:],
                                               start=True, stop=True)
                    ins.then_inc(y_ps, 1)


def stage_depths(nc, K, A):
    KEEP = SEQ // 2 - 1
    with ExitStack() as ctx:
        sb = lambda n, s: K.sb("md_" + n, s, ctx=ctx)
        sem = lambda n: K.sem("md_" + n)
        ps = K.ps
        xn, tmp, st = sb("xn", [P, T, 64]), sb("tmp", [P, T, 64]), sb("st", [P, 4, T])
        wr = sb("wr", [P, 64])
        br = sb("br", [P, 1])
        before = sb("before", [P, P])
        w1, w2 = sb("w1", [64, 256]), sb("w2", [128, 2, 64])
        b1, b2, ones = sb("b1", [128, 2]), sb("b2", [1, 64]), sb("ones", [1, P])
        wc = sb("wc", [P, T])
        wrow = sb("wrow", [P, B, PADSEQ])
        cnt = sb("cnt", [P, 3, T])
        junk = sb("junk", [P, 3, PADSEQ])
        XT = sb("XT", [64, COLS])
        HT = sb("HT", [128, 2, COLS])
        c_in, chain, var_ready, std_ready = sem("c_in"), sem("chain"), sem("var"), sem("std")
        x_ok, w_ok, tr_ps, tr_sb, row_ps, row_sb = (sem("x_ok"), sem("w_ok"), sem("tr_ps"), sem("tr_sb"),
                                                    sem("row_ps"), sem("row_sb"))
        hid_ps, hid_sb, y_ps, y_sb = sem("hid_ps"), sem("hid_sb"), sem("y_ps"), sem("y_sb")
        with nc.Block() as block:
            @block.sync
            def _(sp):
                sp.dma_start(wr[:], row(A["L0_ffn_wr"].rearrange("d o -> (d o)"), P)).then_inc(c_in, 16)
                sp.dma_start(br[:], row(A["L0_ffn_br"], P)).then_inc(c_in, 16)
                sp.dma_start(before[:], A["c_before"]).then_inc(c_in, 16)
                sp.dma_start(w1[:], A["L0_ffn_w1"]).then_inc(c_in, 16)
                sp.dma_start(w2[:], A["L0_ffn_w2"].rearrange("(k p) d -> p k d", p=128)).then_inc(c_in, 16)
                with nc.allow_non_contiguous_dma(reason="two columns"):
                    sp.dma_start(b1[:], A["L0_ffn_b1"].rearrange("(k p) -> p k", p=128)).then_inc(c_in, 16)
                sp.dma_start(b2[:], row(A["L0_ffn_b2"], 1)).then_inc(c_in, 16)

            @block.vector
            def _(dve):
                link = Chain(dve, chain)
                tt = nc.vector.tensor_tensor
                link(nc.vector.memset(ones[:], 1.0))
                link(nc.vector.memset(cnt[:], 0.0))
                layernorm_dve(nc, dve, link, K.h[:], xn[:], tmp[:], st[:], var_ready, std_ready)
                dve.wait_ge(c_in, 112)
                nc.vector.tensor_copy(st[:, 0, :], st[:, 3, :]).then_inc(x_ok, 1)
                tt(K.h[:], K.h[:], xn[:], ALU.add)
                link(tt(tmp[:], xn[:], bc(wr[:], T), ALU.mult))
                link(nc.vector.tensor_reduce(wc[:], tmp[:], AX.X, ALU.add))
                nc.vector.tensor_scalar(wc[:], wc[:], br[:, 0:1], None, ALU.add).then_inc(w_ok, 1)
                dve.wait_ge(w_ok, 1)
                dve.wait_ge(row_sb, 2)
                link(nc.vector.memset(wrow[:, :, SEQ:PADSEQ], -3e38))
                for t in range(T):
                    b, i = t // NT, t % NT
                    c = i * P
                    if i:
                        nc.vector.tensor_scalar(junk[:, 0, 0:c], wrow[:, b, 0:c], wc[:, t:t + 1], None, ALU.is_ge,
                                                ALU.add, accum_out=cnt[:, 0, t:t + 1])
                    nc.vector.tensor_scalar(junk[:, 1, c:PADSEQ], wrow[:, b, c:PADSEQ], wc[:, t:t + 1], None,
                                            ALU.is_gt, ALU.add, accum_out=cnt[:, 1, t:t + 1])
                    link(nc.vector.scalar_tensor_tensor(junk[:, 2, 0:P], wrow[:, b, c:c + P], wc[:, t:t + 1],
                                                        before[:], ALU.is_equal, ALU.mult,
                                                        accum_out=cnt[:, 2, t:t + 1]))
                link(tt(cnt[:, 0], cnt[:, 0], cnt[:, 1], ALU.add))
                link(tt(cnt[:, 0], cnt[:, 0], cnt[:, 2], ALU.add))
                link(nc.vector.tensor_scalar(cnt[:, 0], cnt[:, 0], float(KEEP), None, ALU.is_lt))
                link(tt(wc[:], wc[:], cnt[:, 0], ALU.mult))
                for g in range(NG):
                    dve.wait_ge(y_ps, g + 1)
                    s = slice(3 * g, 3 * g + 3)
                    link(tt(tmp[:, s], ps[0:P, g, 0:192].rearrange("p (a b) -> p a b", a=3), bcl(wc[:, s], 64),
                            ALU.mult))
                    tt(K.h[:, s], K.h[:, s], tmp[:, s], ALU.add)

            @block.scalar
            def _(act):
                root_act(nc, act, st[:], var_ready, std_ready)
                for g in range(NG):
                    act.wait_ge(tr_ps, g + 1)
                    nc.scalar.copy(XT[:, g * GRP:(g + 1) * GRP], ps[0:64, g, 0:GRP]).then_inc(tr_sb, 1)
                for b in range(B):
                    act.wait_ge(row_ps, 3 * b + 3)
                    nc.scalar.copy(wrow[:, b].rearrange("p (a c) -> p a c", a=3),
                                   ps[0:P, 3 * b:3 * b + 3, 0:GRP]).then_inc(row_sb, 1)
                for n in range(2 * NG):
                    act.wait_ge(hid_ps, n + 1)
                    nc.scalar.activation(HT[:, n % 2, (n // 2) * GRP:(n // 2 + 1) * GRP], ps[:, n % 8, 0:GRP],
                                         ACT.Gelu_apprx_tanh, bias=b1[:, n % 2:n % 2 + 1]).then_inc(hid_sb, 1)

            @block.tensor
            def _(pe):
                pe.wait_ge(x_ok, 1)
                transposes(nc, K, lambda t: xn[:, t, :], P, 64, tr_ps)
                pe.wait_ge(w_ok, 1)
                transposes(nc, K, lambda t: wc[:, t:t + 1].to_broadcast([P, P]), P, P, row_ps,
                           free=lambda g: pe.wait_ge(tr_sb, g + 1))
                pe.wait_ge(row_sb, 2)
                pe.wait_ge(c_in, 112)
                for n in range(2 * NG):
                    if n >= 8:
                        pe.wait_ge(hid_sb, n - 7)
                    nc.tensor.matmul(ps[:, n % 8, 0:GRP], w1[:, (n % 2) * 128:(n % 2) * 128 + 128],
                                     XT[:, (n // 2) * GRP:(n // 2 + 1) * GRP], start=True, stop=True).then_inc(hid_ps, 1)
                pe.wait_ge(hid_sb, 2 * NG)
                for g in range(NG):
                    for j in range(3):
                        c = slice((3 * g + j) * P, (3 * g + j + 1) * P)
                        o = ps[0:P, g, j * 64:(j + 1) * 64]
                        nc.tensor.matmul(o, HT[:, 0, c], w2[:, 0], start=True, stop=False)
                        nc.tensor.matmul(o, HT[:, 1, c], w2[:, 1], start=False, stop=False)
                        ins = nc.tensor.matmul(o, ones[:], b2[:], start=False, stop=True)
                    ins.then_inc(y_ps, 1)


def stage_linear(nc, K, A):
    H = 8
    with ExitStack() as ctx:
        sb = lambda n, s: K.sb("la_" + n, s, ctx=ctx)
        sem = lambda n: K.sem("la_" + n)
        ps = K.ps
        xn, tmp, st = sb("xn", [P, T, 64]), sb("tmp", [P, T, 64]), sb("st", [P, 4, T])
        Win = sb("Win", [64, 3, 64])
        WT = sb("WT", [65, 192])
        XT = sb("XT", [65, COLS])
        qkv = sb("qkv", [P, NT, 3, H, B, 8])
        blk = sb("blk", [P, NT, 3, 128])
        ones = sb("ones", [P, 1])
        rmask = sb("rmask", [P, 1])
        bmask = sb("bmask", [128, 128])
        kmax = sb("kmax", [128, 4])
        qs = sb("qs", [P, 3, NT * H])
        v1 = sb("v1", [P, NT, 129])
        rsum = sb("rsum", [128, 1])
        cx = sb("cx", [128, B, H, 8])
        qT = sb("qT", [128, PADSEQ])
        scratch = nc.dram_tensor("la_scratch", [3, PADSEQ * H, 16], F32, kind="Internal").ap()
        c_in, chain, var_ready, std_ready = sem("c_in"), sem("chain"), sem("var"), sem("std")
        x_ok, wt_ps, wt_sb, tr_ps, tr_sb = sem("x_ok"), sem("wt_ps"), sem("wt_sb"), sem("tr_ps"), sem("tr_sb")
        qkv_ps, qkv_sb, stored, loaded = sem("qkv_ps"), sem("qkv_sb"), sem("stored"), sem("loaded")
        kt_ps, km_ok, km_ps, kd_ok, ke_ok, k_ok = (sem("kt_ps"), sem("km_ok"), sem("km_ps"), sem("kd_ok"),
                                                   sem("ke_ok"), sem("k_ok"))
        qd_ok, qe_ok, q_ok, cx_ps, cx_ok = sem("qd_ok"), sem("qe_ok"), sem("q_ok"), sem("cx_ps"), sem("cx_ok")
        qt_ps, qt_sb, o_ps, ones_ok = sem("qt_ps"), sem("qt_sb"), sem("o_ps"), sem("ones_ok")
        with nc.Block() as block:
            @block.sync
            def _(sp):
                for i, n in enumerate("qkv"):
                    sp.dma_start(Win[:, i], A["L1_attn_W" + n]).then_inc(c_in, 16)
                    sp.dma_start(WT[64:65, 64 * i:64 * i + 64], row(A["L1_attn_b" + n], 1)).then_inc(c_in, 16)
                sp.dma_start(rmask[:], A["c_rowmask"]).then_inc(c_in, 16)
                sp.dma_start(bmask[:], A["c_block16"]).then_inc(c_in, 16)
                sp.wait_ge(qkv_sb, T)
                for a in range(3):
                    sp.dma_start(scratch[a].rearrange("(i p h) e -> p i (h e)", p=P, h=H),
                                 qkv[:, :, a].rearrange("p i h b e -> p i (h b e)")).then_inc(stored, 16)
                sp.wait_ge(stored, 48)
                for a in (1, 0, 2):
                    for g in range(H):
                        sp.dma_start(blk[:, :, a, 16 * g:16 * g + 16],
                                     scratch[a, SEQ * g:SEQ * g + PADSEQ].rearrange("(i p) e -> p i e", p=P)
                                     ).then_inc(loaded, 16)

            @block.gpsimd
            def _(pool):
                nc.gpsimd.memset(XT[64:65, :], 1.0).then_inc(ones_ok, 1)

            @block.vector
            def _(dve):
                link = Chain(dve, chain)
                tt = nc.vector.tensor_tensor
                nc.vector.memset(ones[:], 1.0)
                layernorm_dve(nc, dve, link, K.h[:], xn[:], tmp[:], st[:], var_ready, std_ready)
                nc.vector.tensor_copy(st[:, 0, :], st[:, 3, :]).then_inc(x_ok, 1)
                dve.wait_ge(loaded, 3 * H * 16)
                dve.wait_ge(c_in, 128)
                link(nc.vector.memset(v1[:, :, 128:129], 1.0))
                link(nc.vector.tensor_copy(v1[:, :, 0:128], blk[:, :, 2]))
                dve.wait_ge(kt_ps, 3)
                link(nc.vector.tensor_reduce(kmax[:, 0:2], ps[:, 0:2, 0:GRP], AX.X, ALU.max))
                link(nc.vector.tensor_reduce(kmax[:, 2:3], ps[:, 2, 0:GRP - 1], AX.X, ALU.max))
                nc.vector.tensor_reduce(kmax[:, 3:4], kmax[:, 0:3], AX.X, ALU.max).then_inc(km_ok, 1)
                q4 = blk[:, :, 0].rearrange("p i (g e) -> p i g e", g=H)
                q3 = [blk[:, i, 0].rearrange("p (g e) -> p g e", g=H) for i in range(NT)]
                link(nc.vector.tensor_reduce(qs[:, 0].rearrange("p (i g) -> p i g", g=H), q4, AX.X, ALU.max))
                for i in range(NT):
                    ins = tt(q3[i], q3[i], bcl(qs[:, 0, H * i:H * i + H], 16), ALU.subtract)
                ins.then_inc(qd_ok, 1)
                dve.wait_ge(km_ps, 1)
                tt(blk[:, :, 1], blk[:, :, 1], bc(ps[0:P, 3, 0:128], NT), ALU.subtract).then_inc(kd_ok, 1)
                dve.wait_ge(qe_ok, 1)
                link(nc.vector.tensor_reduce(qs[:, 1].rearrange("p (i g) -> p i g", g=H), q4, AX.X, ALU.add))
                link(nc.vector.reciprocal(qs[:, 2], qs[:, 1]))
                for i in range(NT):
                    ins = tt(q3[i], q3[i], bcl(qs[:, 2, H * i:H * i + H], 16), ALU.mult)
                ins.then_inc(q_ok, 1)
                dve.wait_ge(ke_ok, 1)
                nc.vector.tensor_scalar(blk[:, NT - 1, 1], blk[:, NT - 1, 1], rmask[:, 0:1], None,
                                        ALU.mult).then_inc(k_ok, 1)
                dve.wait_ge(cx_ps, 1)
                link(nc.vector.reciprocal(rsum[:], ps[:, 4, 128:129]))
                link(nc.vector.tensor_scalar(rsum[:], rsum[:], 4.0, None, ALU.mult))
                for b in range(B):
                    src = ps[:, 4, 0:128].rearrange("p (g b e) -> p b g e", g=H, b=B)[:, b]
                    nc.vector.scalar_tensor_tensor(cx[:, b], src, rsum[:, 0:1],
                                                   bmask[:].rearrange("p (g b e) -> p b g e", g=H, b=B)[:, b],
                                                   ALU.mult, ALU.mult).then_inc(cx_ok, 1)
                for g in range(3):
                    dve.wait_ge(o_ps, g + 1)
                    for b in range(B):
                        hh = K.h[:, b * NT + 3 * g:b * NT + 3 * g + 3, :]
                        tt(hh, ps[0:P, 5 + g, 0:384].rearrange("p (i b e) -> p b i e", i=3, b=B)[:, b], hh, ALU.add)

            @block.scalar
            def _(act):
                root_act(nc, act, st[:], var_ready, std_ready)
                act.wait_ge(wt_ps, 1)
                nc.scalar.copy(WT[0:64, :], ps[0:64, 7, 0:192]).then_inc(wt_sb, 1)
                for g in range(NG):
                    act.wait_ge(tr_ps, g + 1)
                    nc.scalar.copy(XT[0:64, g * GRP:(g + 1) * GRP], ps[0:64, g, 0:GRP]).then_inc(tr_sb, 1)
                for t in range(T):
                    act.wait_ge(qkv_ps, t + 1)
                    for a in range(3):
                        ins = nc.scalar.copy(qkv[:, t % NT, a, :, t // NT],
                                             ps[0:P, t % 8, 64 * a:64 * a + 64].rearrange("p (h e) -> p h e", h=H))
                    ins.then_inc(qkv_sb, 1)
                act.wait_ge(qd_ok, 1)
                nc.scalar.activation(blk[:, :, 0], blk[:, :, 0], ACT.Exp).then_inc(qe_ok, 1)
                act.wait_ge(kd_ok, 1)
                nc.scalar.activation(blk[:, :, 1], blk[:, :, 1], ACT.Exp).then_inc(ke_ok, 1)
                for g in range(3):
                    act.wait_ge(qt_ps, g + 1)
                    nc.scalar.copy(qT[:, g * GRP:(g + 1) * GRP], ps[:, g, 0:GRP]).then_inc(qt_sb, 1)

            @block.tensor
            def _(pe):
                pe.wait_ge(c_in, 128)
                for i in range(3):
                    ins = nc.tensor.transpose(ps[0:64, 7, 64 * i:64 * i + 64], Win[:, i], K.ident[0:64, 0:64])
                ins.then_inc(wt_ps, 1)
                pe.wait_ge(x_ok, 1)
                transposes(nc, K, lambda t: xn[:, t, :], P, 64, tr_ps)
                pe.wait_ge(tr_sb, NG)
                pe.wait_ge(wt_sb, 1)
                pe.wait_ge(ones_ok, 1)
                for t in range(T):
                    if t >= 8:
                        pe.wait_ge(qkv_sb, t - 7)
                    nc.tensor.matmul(ps[0:P, t % 8, 0:192], XT[:, t * P:(t + 1) * P], WT[:],
                                     start=True, stop=True).then_inc(qkv_ps, 1)
                pe.wait_ge(qkv_sb, T)
                pe.wait_ge(loaded, 3 * H * 16)

                def nine(a, done):
                    for i in range(NT):
                        ins = nc.tensor.transpose(ps[:, i // 3, (i % 3) * P:(i % 3 + 1) * P], blk[:, i, a, :],
                                                  K.ident[0:P, 0:P])
                        if i % 3 == 2:
                            ins.then_inc(done, 1)

                nine(1, kt_ps)
                pe.wait_ge(km_ok, 1)
                nc.tensor.transpose(ps[0:P, 3, 0:128], kmax[:, 3:4].to_broadcast([128, P]),
                                    K.ident[:]).then_inc(km_ps, 1)
                pe.wait_ge(q_ok, 1)
                nine(0, qt_ps)
                pe.wait_ge(k_ok, 1)
                for i in range(NT):
                    ins = nc.tensor.matmul(ps[:, 4, 0:129], blk[:, i, 1, :], v1[:, i, :], start=(i == 0),
                                           stop=(i == NT - 1))
                ins.then_inc(cx_ps, 1)
                pe.wait_ge(qt_sb, 3)
                pe.wait_ge(cx_ok, B)
                for g in range(3):
                    for i in range(3 * g, 3 * g + 3):
                        ins = nc.tensor.matmul(ps[0:P, 5 + g, (i % 3) * 128:(i % 3) * 128 + 128],
                                               qT[:, i * P:(i + 1) * P], cx[:].rearrange("p b g e -> p (b g e)"),
                                               start=True, stop=True)
                    ins.then_inc(o_ps, 1)


def rms_dve(nc, dve, link, x, out, tmp, st, wrow, var_ready, std_ready, eps=1e-6):
    link(nc.vector.tensor_tensor(tmp, x, x, ALU.mult))
    link(nc.vector.tensor_reduce(st[:, 1, :], tmp, AX.X, ALU.add))
    nc.vector.tensor_scalar(st[:, 1, :], st[:, 1, :], 1.0 / 64, eps, ALU.mult, ALU.add).then_inc(var_ready, 1)
    dve.wait_ge(std_ready, 1)
    link(nc.vector.reciprocal(st[:, 3, :], st[:, 2, :]))
    link(nc.vector.tensor_tensor(out, x, bcl(st[:, 3, :], 64), ALU.mult))
    link(nc.vector.tensor_tensor(out, out, bc(wrow, T), ALU.mult))


def stage_gqa(nc, K, A):
    with ExitStack() as ctx:
        x2 = K.sb("gq_x", [P, T, 64], ctx=ctx)
        gqa_attention(nc, K, A, x2)
        moe_top2(nc, K, A, x2)


def gqa_attention(nc, K, A, x2):
    NH = 4
    with ExitStack() as ctx:
        sb = lambda n, s: K.sb("ga_" + n, s, ctx=ctx)
        sem = lambda n: K.sem("ga_" + n)
        ps = K.ps
        xh, tmp, st, st2 = sb("xh", [P, T, 64]), sb("tmp", [P, T, 64]), sb("st", [P, 4, T]), sb("st2", [P, 4, T])
        lnw = sb("lnw", [P, 64])
        Win = sb("Win", [128, 64])
        wo = sb("wo", [64, 64])
        WT = sb("WT", [64, 192])
        XT = sb("XT", [64, COLS])
        qkv = sb("qkv", [P, T, 128])
        rope = sb("rope", [P, 2, NT, 16])
        rot = sb("rot", [P, T, 6, 16])
        Q4, K4 = sb("Q4", [P, T, NH, 32]), sb("K4", [P, T, NH, 32])
        V1 = sb("V1", [P, T, 2, 17])
        QT, KT = sb("QT", [128, COLS]), sb("KT", [128, COLS])
        neg = sb("neg", [P, P])
        junk = sb("junk", [P, 2, P])
        mx = sb("mx", [P, T * NH, 3])
        mxr = sb("mxr", [P, T * NH])
        PT = sb("PT", [P, 2, 3, GRP])
        Yt = sb("Yt", [P, T, NH, 16])
        yr = sb("yr", [P, 2, NH])
        c_in, chain, var_ready, std_ready = sem("c_in"), sem("chain"), sem("var"), sem("std")
        x_ok, wt_ps, wt_sb, tr_ps, tr_sb = sem("x_ok"), sem("wt_ps"), sem("wt_sb"), sem("tr_ps"), sem("tr_sb")
        qkv_ps, qkv_sb, z_ok, q4_ok, q4_ps, qt_sb, kt_sb = (sem("qkv_ps"), sem("qkv_sb"), sem("zeros"), sem("q4_ok"),
                                                            sem("q4_ps"), sem("qt_sb"), sem("kt_sb"))
        s_ps, max_ok, aug_ok, aug_ps, aug_sb = sem("s_ps"), sem("max_ok"), sem("aug_ok"), sem("aug_ps"), sem("aug_sb")
        st_ps, exp_ok, sel_ok, av_ps, y_ok = sem("st_ps"), sem("exp_ok"), sem("sel_ok"), sem("av_ps"), sem("y_ok")
        yt_ps, yt_sb, o_ps = sem("yt_ps"), sem("yt_sb"), sem("o_ps")
        UNITS = T * NH
        with nc.Block() as block:
            @block.sync
            def _(sp):
                sp.dma_start(lnw[:], row(A["L1_ffn_ln1_w"], P)).then_inc(c_in, 16)
                sp.dma_start(Win[0:64], A["L1_ffn_wq"]).then_inc(c_in, 16)
                sp.dma_start(Win[64:96], A["L1_ffn_wk"]).then_inc(c_in, 16)
                sp.dma_start(Win[96:128], A["L1_ffn_wv"]).then_inc(c_in, 16)
                sp.dma_start(wo[:], A["L1_ffn_wo"]).then_inc(c_in, 16)
                sp.dma_start(rope[:], A["c_rope"]).then_inc(c_in, 16)
                sp.dma_start(neg[:], A["c_negmask"]).then_inc(c_in, 16)

            @block.gpsimd
            def _(pool):
                nc.gpsimd.memset(Q4[:], 0.0).then_inc(z_ok, 1)
                pool.wait_ge(z_ok, 1)
                nc.gpsimd.memset(K4[:], 0.0).then_inc(z_ok, 1)
                pool.wait_ge(z_ok, 2)
                nc.gpsimd.memset(K4[:, :, :, 16:17], 1.0).then_inc(z_ok, 1)
                pool.wait_ge(z_ok, 3)
                nc.gpsimd.memset(V1[:, :, :, 16:17], 1.0).then_inc(z_ok, 1)
                pool.wait_ge(z_ok, 4)
                nc.gpsimd.memset(mx[:], -3e38).then_inc(z_ok, 1)
                for n in range(UNITS):
                    i = n // NH % NT
                    pool.wait_ge(exp_ok, n + 1)
                    d = PT[:, n % 2].rearrange("p a b -> p (a b)")[:, i * P:(i + 1) * P]
                    nc.gpsimd.affine_select(out=d, in_=d, compare_op=ALU.is_ge, fill=0.0, base=0,
                                            pattern=[[1, P]], channel_multiplier=-1).then_inc(sel_ok, 1)

            @block.vector
            def _(dve):
                link = Chain(dve, chain)
                tt = nc.vector.tensor_tensor
                layernorm_dve(nc, dve, link, K.h[:], x2[:], tmp[:], st[:], var_ready, std_ready)
                dve.wait_ge(c_in, 112)
                link(tt(tmp[:], x2[:], x2[:], ALU.mult))
                link(nc.vector.tensor_reduce(st2[:, 1, :], tmp[:], AX.X, ALU.add))
                nc.vector.tensor_scalar(st2[:, 1, :], st2[:, 1, :], 1.0 / 64, 1e-6, ALU.mult,
                                        ALU.add).then_inc(var_ready, 1)
                dve.wait_ge(std_ready, 2)
                link(nc.vector.reciprocal(st2[:, 3, :], st2[:, 2, :]))
                link(tt(xh[:], x2[:], bcl(st2[:, 3, :], 64), ALU.mult))
                tt(xh[:], xh[:], bc(lnw[:], T), ALU.mult).then_inc(x_ok, 1)
                dve.wait_ge(qkv_sb, T)
                dve.wait_ge(z_ok, 5)
                for b in range(B):
                    s = slice(b * NT, b * NT + NT)
                    six = qkv[:, s, 0:96].rearrange("p i (h e) -> p i h e", h=6)
                    hb = lambda a: a.unsqueeze(2).to_broadcast([P, NT, 6, a.shape[2]])
                    tt(rot[:, s, :, 0:8], six[:, :, :, 8:16], hb(rope[:, 1, :, 0:8]), ALU.mult)
                    link(tt(rot[:, s, :, 8:16], six[:, :, :, 0:8], hb(rope[:, 1, :, 8:16]), ALU.mult))
                    link(tt(six, six, hb(rope[:, 0]), ALU.mult))
                    link(tt(six, six, rot[:, s], ALU.add))
                heads = qkv[:].rearrange("p i (h e) -> p i h e", h=8)
                nc.vector.tensor_copy(Q4[:, :, :, 0:16], heads[:, :, 0:4]).then_inc(q4_ok, 1)
                for h in range(NH):
                    nc.vector.tensor_copy(K4[:, :, h, 0:16], heads[:, :, 4 + h // 2]).then_inc(q4_ok, 1)
                nc.vector.tensor_copy(V1[:, :, :, 0:16], heads[:, :, 6:8]).then_inc(q4_ok, 1)
                for g in range(NG):
                    dve.wait_ge(q4_ps, NG + g + 1)
                    nc.vector.tensor_copy(KT[:, g * GRP:(g + 1) * GRP], ps[:, (NG + g) % 8, 0:GRP]).then_inc(kt_sb, 1)
                for n in range(UNITS):
                    i, b0 = n // NH % NT, 3 * (n % 2)
                    dve.wait_ge(s_ps, n + 1)
                    if i // 3:
                        nc.vector.tensor_reduce(mx[:, n, 0:1], ps[0:P, b0:b0 + i // 3, 0:GRP], AX.XY, ALU.max)
                    if i % 3:
                        nc.vector.tensor_reduce(mx[:, n, 1:2], ps[0:P, b0 + i // 3, 0:(i % 3) * P], AX.X, ALU.max)
                    c = (i % 3) * P
                    nc.vector.tensor_tensor_reduce(out=junk[:, n % 2], in0=ps[0:P, b0 + i // 3, c:c + P], in1=neg[:],
                                                   scale=1.0, scalar=-3e38, op0=ALU.add, op1=ALU.max,
                                                   accum_out=mx[:, n, 2:3]).then_inc(max_ok, 1)
                dve.wait_ge(max_ok, UNITS)
                link(nc.vector.tensor_reduce(mxr[:], mx[:], AX.X, ALU.max))
                nc.vector.tensor_scalar(Q4[:, :, :, 16], mxr[:].rearrange("p (t h) -> p t h", h=NH), -1.0, None,
                                        ALU.mult).then_inc(aug_ok, 1)
                for t in range(T):
                    dve.wait_ge(av_ps, NH * (t + 1))
                    y = ps[0:P, 6 + t % 2, 0:NH * 17].rearrange("p (h e) -> p h e", h=NH)
                    link(nc.vector.reciprocal(yr[:, t % 2], y[:, :, 16]))
                    tt(Yt[:, t], y[:, :, 0:16], bcl(yr[:, t % 2], 16), ALU.mult).then_inc(y_ok, 1)
                for g in range(NG):
                    dve.wait_ge(o_ps, g + 1)
                    xx = x2[:, 3 * g:3 * g + 3, :].rearrange("p a b -> p (a b)")
                    tt(xx, ps[0:P, g, 0:192], xx, ALU.add)

            @block.scalar
            def _(act):
                root_act(nc, act, st[:], var_ready, std_ready)
                root_act(nc, act, st2[:], var_ready, std_ready, n=2)
                act.wait_ge(wt_ps, 1)
                nc.scalar.copy(WT[:], ps[0:64, 7, 0:192]).then_inc(wt_sb, 1)
                for g in range(NG):
                    act.wait_ge(tr_ps, g + 1)
                    nc.scalar.copy(XT[:, g * GRP:(g + 1) * GRP], ps[0:64, g, 0:GRP]).then_inc(tr_sb, 1)
                for t in range(T):
                    act.wait_ge(qkv_ps, t + 1)
                    nc.scalar.copy(qkv[:, t], ps[0:P, t % 8, 0:128]).then_inc(qkv_sb, 1)
                for g in range(NG):
                    act.wait_ge(q4_ps, g + 1)
                    nc.scalar.copy(QT[:, g * GRP:(g + 1) * GRP], ps[:, g, 0:GRP]).then_inc(qt_sb, 1)
                for g in range(NG):
                    act.wait_ge(aug_ps, g + 1)
                    nc.scalar.copy(QT[:, g * GRP:(g + 1) * GRP], ps[:, g, 0:GRP]).then_inc(aug_sb, 1)
                for n in range(UNITS):
                    i, b0 = n // NH % NT, 3 * (n % 2)
                    act.wait_ge(st_ps, n + 1)
                    if n >= 2:
                        act.wait_ge(av_ps, n - 1)
                    full, rest = (i + 1) // 3, (i + 1) % 3
                    if full:
                        ins = nc.scalar.activation(PT[:, n % 2, 0:full], ps[0:P, b0:b0 + full, 0:GRP], ACT.Exp,
                                                   scale=0.25)
                    if rest:
                        ins = nc.scalar.activation(PT[:, n % 2, full, 0:rest * P], ps[0:P, b0 + full, 0:rest * P],
                                                   ACT.Exp, scale=0.25)
                    ins.then_inc(exp_ok, 1)
                for g in range(NG):
                    act.wait_ge(yt_ps, g + 1)
                    nc.scalar.copy(XT[:, g * GRP:(g + 1) * GRP], ps[0:64, g, 0:GRP]).then_inc(yt_sb, 1)

            @block.tensor
            def _(pe):
                pe.wait_ge(c_in, 112)
                nc.tensor.transpose(ps[0:64, 7, 0:128], Win[:], K.ident[:])
                nc.tensor.transpose(ps[0:64, 7, 128:192], wo[:], K.ident[0:64, 0:64]).then_inc(wt_ps, 1)
                pe.wait_ge(x_ok, 1)
                transposes(nc, K, lambda t: xh[:, t, :], P, 64, tr_ps)
                pe.wait_ge(tr_sb, NG)
                pe.wait_ge(wt_sb, 1)
                for t in range(T):
                    if t >= 8:
                        pe.wait_ge(qkv_sb, t - 7)
                    nc.tensor.matmul(ps[0:P, t % 8, 0:128], XT[:, t * P:(t + 1) * P], WT[:, 0:128],
                                     start=True, stop=True).then_inc(qkv_ps, 1)
                pe.wait_ge(qkv_sb, T)
                pe.wait_ge(q4_ok, 6)
                pe.wait_ge(z_ok, 5)
                for m in range(2 * NG):
                    if m >= 8:
                        pe.wait_ge(qt_sb, m - 7)
                    for j in range(3):
                        t = 3 * (m % NG) + j
                        ins = nc.tensor.transpose(ps[:, m % 8, j * P:(j + 1) * P],
                                                  (K4 if m // NG else Q4)[:, t].rearrange("p h e -> p (h e)"),
                                                  K.ident[0:P, 0:P])
                    ins.then_inc(q4_ps, 1)
                pe.wait_ge(qt_sb, NG)
                pe.wait_ge(kt_sb, NG)
                for n in range(UNITS):
                    t, h = n // NH, n % NH
                    i, b0 = t % NT, 3 * (n % 2)
                    if n >= 2:
                        pe.wait_ge(max_ok, n - 1)
                    for c in range(i // 3 + 1):
                        w = min(3, i + 1 - 3 * c) * P
                        k0 = (t - i) * P + c * GRP
                        ins = nc.tensor.matmul(ps[0:P, b0 + c, 0:w], QT[32 * h:32 * h + 16, t * P:(t + 1) * P],
                                               KT[32 * h:32 * h + 16, k0:k0 + w], start=True, stop=True)
                    ins.then_inc(s_ps, 1)
                pe.wait_ge(aug_ok, 1)
                transposes(nc, K, lambda t: Q4[:, t].rearrange("p h e -> p (h e)"), P, 128, aug_ps)
                pe.wait_ge(aug_sb, NG)

                def weigh(n):
                    t, h = n // NH, n % NH
                    i = t % NT
                    pe.wait_ge(sel_ok, n + 1)
                    if h == 0 and t >= 2:
                        pe.wait_ge(y_ok, t - 1)
                    for j in range(i + 1):
                        ins = nc.tensor.matmul(ps[0:P, 6 + t % 2, 17 * h:17 * h + 17],
                                               PT[:, n % 2, j // 3, (j % 3) * P:(j % 3 + 1) * P],
                                               V1[:, t - i + j, h // 2, :], start=(j == 0), stop=(j == i))
                    ins.then_inc(av_ps, 1)

                for n in range(UNITS + 1):
                    if n < UNITS:
                        t, h = n // NH, n % NH
                        i = t % NT
                        if n >= 2:
                            pe.wait_ge(exp_ok, n - 1)
                        for j in range(i + 1):
                            k0 = (t - i + j) * P
                            ins = nc.tensor.matmul(ps[0:P, 3 * (n % 2) + j // 3, (j % 3) * P:(j % 3 + 1) * P],
                                                   KT[32 * h:32 * h + 17, k0:k0 + P],
                                                   QT[32 * h:32 * h + 17, t * P:(t + 1) * P], start=True, stop=True)
                        ins.then_inc(st_ps, 1)
                    if n:
                        weigh(n - 1)
                pe.wait_ge(y_ok, T)
                transposes(nc, K, lambda t: Yt[:, t].rearrange("p h e -> p (h e)"), P, 64, yt_ps)
                for g in range(NG):
                    pe.wait_ge(yt_sb, g + 1)
                    for j in range(3):
                        t = 3 * g + j
                        ins = nc.tensor.matmul(ps[0:P, g, j * 64:(j + 1) * 64], XT[:, t * P:(t + 1) * P],
                                               WT[:, 128:192], start=True, stop=True)
                    ins.then_inc(o_ps, 1)


def moe_top2(nc, K, A, x2):
    NE, HID = 8, 170
    HH = HID // 2
    NCH = 2 * NE
    with ExitStack() as ctx:
        sb = lambda n, s: K.sb("mt_" + n, s, ctx=ctx)
        sem = lambda n: K.sem("mt_" + n)
        ps = K.ps
        xf, tmp, st = sb("xf", [P, T, 64]), sb("tmp", [P, T, 64]), sb("st", [P, 4, T])
        lnw = sb("lnw", [P, 64])
        rin = sb("rin", [8, 64])
        rT = sb("rT", [64, 8])
        w1in, w3in, w2in = sb("w1in", [HH, NCH, 64]), sb("w3in", [HH, NCH, 64]), sb("w2in", [64, NE, HID])
        w1T, w3T, w2T = sb("w1T", [64, NCH, HH]), sb("w3T", [64, NCH, HH]), sb("w2T", [HH, NCH, 64])
        XT = sb("XT", [64, COLS])
        lg = sb("lg", [P, T, NE])
        s1 = sb("s1", [P, 4, T])
        big = sb("big", [P, T, NE, NE])
        big2 = sb("big2", [P, T, NE, NE])
        before8 = sb("before8", [P, NE, NE])
        act_sb = sb("act", [HH, 2, GRP])
        HT = sb("HT", [HH, 2, 2, COLS])
        c_in, chain, var_ready, std_ready = sem("c_in"), sem("chain"), sem("var"), sem("std")
        x_ok, w_ps, w_sb, tr_ps, tr_sb = sem("x_ok"), sem("w_ps"), sem("w_sb"), sem("tr_ps"), sem("tr_sb")
        lg_ps, lg_ok, le_ok = sem("lg_ps"), sem("lg_ok"), sem("le_ok")
        up_ps, silu_ok, hid_ok, dn_ps, dn_ok = sem("up_ps"), sem("silu_ok"), sem("hid_ok"), sem("dn_ps"), sem("dn_ok")
        with nc.Block() as block:
            @block.sync
            def _(sp):
                sp.dma_start(w1in[:], A["L1_ffn_w1"].rearrange("e (c p) d -> p (e c) d", p=HH)).then_inc(c_in, 16)
                sp.dma_start(w3in[:], A["L1_ffn_w3"].rearrange("e (c p) d -> p (e c) d", p=HH)).then_inc(c_in, 16)
                sp.dma_start(w2in[:], A["L1_ffn_w2"].rearrange("e d f -> d e f")).then_inc(c_in, 16)
                sp.dma_start(rin[:], A["L1_ffn_router_w"]).then_inc(c_in, 16)
                sp.dma_start(lnw[:], row(A["L1_ffn_ln2_w"], P)).then_inc(c_in, 16)
                sp.dma_start(before8[:], A["c_before8"]).then_inc(c_in, 16)

            @block.vector
            def _(dve):
                link = Chain(dve, chain)
                tt = nc.vector.tensor_tensor
                dve.wait_ge(c_in, 96)
                rms_dve(nc, dve, link, x2[:], xf[:], tmp[:], st[:], lnw[:], var_ready, std_ready)
                nc.vector.tensor_copy(st[:, 0, :], st[:, 3, :]).then_inc(x_ok, 1)
                tt(K.h[:], K.h[:], x2[:], ALU.add)
                dve.wait_ge(lg_ps, 1)
                link(nc.vector.tensor_reduce(s1[:, 0], ps[0:P, 6, 0:T * NE].rearrange("p (t e) -> p t e", e=NE),
                                             AX.X, ALU.max))
                tt(lg[:], ps[0:P, 6, 0:T * NE].rearrange("p (t e) -> p t e", e=NE), bcl(s1[:, 0], NE),
                   ALU.subtract).then_inc(lg_ok, 1)
                dve.wait_ge(le_ok, 1)
                link(nc.vector.tensor_reduce(s1[:, 1], lg[:], AX.X, ALU.add))
                link(nc.vector.reciprocal(s1[:, 1], s1[:, 1]))
                link(tt(lg[:], lg[:], bcl(s1[:, 1], NE), ALU.mult))
                mine = lg[:].unsqueeze(3).to_broadcast([P, T, NE, NE])
                other = lg[:].unsqueeze(2).to_broadcast([P, T, NE, NE])
                f3 = lambda a: a.rearrange("p t a b -> p t (a b)")
                tt(big[:], other, mine, ALU.is_gt)
                link(tt(big2[:], other, mine, ALU.is_equal))
                link(tt(f3(big2[:]), f3(big2[:]), bc(before8[:].rearrange("p a b -> p (a b)"), T), ALU.mult))
                link(tt(big[:], big[:], big2[:], ALU.add))
                link(nc.vector.tensor_reduce(big2[:, :, :, 0], big[:], AX.X, ALU.add))
                link(nc.vector.scalar_tensor_tensor(lg[:], big2[:, :, :, 0], 2.0, lg[:], ALU.is_lt, ALU.mult))
                link(nc.vector.tensor_reduce(s1[:, 2], lg[:], AX.X, ALU.add))
                link(nc.vector.tensor_scalar(s1[:, 2], s1[:, 2], 1e-9, None, ALU.add))
                link(nc.vector.reciprocal(s1[:, 3], s1[:, 2]))
                link(tt(lg[:], lg[:], bcl(s1[:, 3], NE), ALU.mult))
                for e in range(NE + 1):
                    if e < NE:
                        for n in range(12 * e, 12 * e + 12):
                            dve.wait_ge(silu_ok, n + 1)
                            g, c = n % 12 // 2, n % 2
                            if e >= 2:
                                dve.wait_ge(dn_ps, e - 1)
                            tt(HT[:, e % 2, c, g * GRP:(g + 1) * GRP], ps[0:HH, 2 * (n % 2) + 1, 0:GRP],
                               act_sb[:, n % 2], ALU.mult).then_inc(hid_ok, 1)
                    if e:
                        dve.wait_ge(dn_ps, e)
                        link(tt(tmp[:].rearrange("p (a t) d -> p a t d", a=3),
                                ps[0:P, 4:7, 0:384].rearrange("p a (t d) -> p a t d", t=6),
                                lg[:, :, e - 1].rearrange("p (a t) -> p a t", a=3).unsqueeze(3)
                                .to_broadcast([P, 3, 6, 64]), ALU.mult))
                        tt(K.h[:], K.h[:], tmp[:], ALU.add).then_inc(dn_ok, 1)
                        dve.wait_ge(dn_ok, e)

            @block.scalar
            def _(act):
                root_act(nc, act, st[:], var_ready, std_ready)
                for m in range(7):
                    act.wait_ge(w_ps, m + 1)
                    if m < 4:
                        dst = (w1T if m < 2 else w3T)[:, 8 * (m % 2):8 * (m % 2) + 8]
                        for q in range(2):
                            ins = nc.scalar.copy(dst[:, 4 * q:4 * q + 4].rearrange("p a b -> p (a b)"),
                                                 ps[0:64, 2 * (m % 4) + q, 0:4 * HH])
                    elif m < 6:
                        ins = nc.scalar.copy(w2T[:, 8 * (m - 4):8 * (m - 4) + 8].rearrange("p a b -> p (a b)"),
                                             ps[0:HH, m - 4, 0:512])
                    else:
                        ins = nc.scalar.copy(rT[:], ps[0:64, 2, 0:8])
                    ins.then_inc(w_sb, 1)
                for g in range(NG):
                    act.wait_ge(tr_ps, g + 1)
                    nc.scalar.copy(XT[:, g * GRP:(g + 1) * GRP], ps[0:64, g, 0:GRP]).then_inc(tr_sb, 1)
                act.wait_ge(lg_ok, 1)
                nc.scalar.activation(lg[:], lg[:], ACT.Exp).then_inc(le_ok, 1)
                for n in range(12 * NE):
                    act.wait_ge(up_ps, n + 1)
                    if n >= 2:
                        act.wait_ge(hid_ok, n - 1)
                    nc.scalar.activation(act_sb[:, n % 2], ps[0:HH, 2 * (n % 2), 0:GRP], ACT.Silu).then_inc(silu_ok, 1)

            @block.tensor
            def _(pe):
                pe.wait_ge(c_in, 96)
                for m in range(4):
                    win = w1in if m < 2 else w3in
                    for j in range(8):
                        ins = nc.tensor.transpose(ps[0:64, 2 * m + j // 4, (j % 4) * HH:(j % 4 + 1) * HH],
                                                  win[:, 8 * (m % 2) + j, :], K.ident[0:HH, 0:HH])
                    ins.then_inc(w_ps, 1)
                pe.wait_ge(w_sb, 2)
                for m in range(2):
                    for j in range(8):
                        n = 8 * m + j
                        ins = nc.tensor.transpose(ps[0:HH, m, j * 64:(j + 1) * 64],
                                                  w2in[:, n // 2, (n % 2) * HH:(n % 2 + 1) * HH],
                                                  K.ident[0:64, 0:64])
                    ins.then_inc(w_ps, 1)
                nc.tensor.transpose(ps[0:64, 2, 0:8], rin[:], K.ident[0:8, 0:8]).then_inc(w_ps, 1)
                pe.wait_ge(w_sb, 7)
                pe.wait_ge(x_ok, 1)
                transposes(nc, K, lambda t: xf[:, t, :], P, 64, tr_ps)
                pe.wait_ge(tr_sb, NG)
                for t in range(T):
                    ins = nc.tensor.matmul(ps[0:P, 6, t * NE:(t + 1) * NE], XT[:, t * P:(t + 1) * P], rT[:],
                                           start=True, stop=True)
                ins.then_inc(lg_ps, 1)

                def down(e):
                    pe.wait_ge(hid_ok, 12 * (e + 1))
                    if e:
                        pe.wait_ge(dn_ok, e)
                    else:
                        pe.wait_ge(lg_ok, 1)
                    for t in range(T):
                        for c in range(2):
                            ins = nc.tensor.matmul(ps[0:P, 4 + t // 6, (t % 6) * 64:(t % 6) * 64 + 64],
                                                   HT[:, e % 2, c, t * P:(t + 1) * P], w2T[:, 2 * e + c, :],
                                                   start=(c == 0), stop=(c == 1))
                    ins.then_inc(dn_ps, 1)

                for e in range(NE + 1):
                    if e < NE:
                        for n in range(12 * e, 12 * e + 12):
                            g, c = n % 12 // 2, n % 2
                            if n >= 2:
                                pe.wait_ge(hid_ok, n - 1)
                            for q, w in enumerate((w1T, w3T)):
                                ins = nc.tensor.matmul(ps[0:HH, 2 * (n % 2) + q, 0:GRP], w[:, 2 * e + c, :],
                                                       XT[:, g * GRP:(g + 1) * GRP], start=True, stop=True)
                            ins.then_inc(up_ps, 1)
                            if n == 12 * e + 3 and e:
                                down(e - 1)
                    else:
                        down(e - 1)


def stage_pairs(nc, K, A):
    with ExitStack() as ctx:
        Q12 = K.sb("pa_Q12", [P, T, 32, 32], BF16, ctx=ctx)
        K12 = K.sb("pa_K12", [P, T, 32, 32], BF16, ctx=ctx)
        V1 = K.sb("pa_V1", [P, T, 128], ctx=ctx)
        wpT = K.sb("pa_wpT", [64, 64], ctx=ctx)
        pairs_prepare(nc, K, A, Q12, K12, V1, wpT)
        Y = K.sb("pa_Y", [128, 8, COLS], ctx=ctx)
        pairs_attend(nc, K, A, Q12, K12, V1, Y)
        pairs_project(nc, K, A, Y, wpT)


def pairs_prepare(nc, K, A, Q12, K12, V1, wpT):
    with ExitStack() as ctx:
        sb = lambda n, s, dt=F32: K.sb("pp_" + n, s, dt, ctx=ctx)
        sem = lambda n: K.sem("pp_" + n)
        ps = K.ps
        xn, tmp, st = sb("xn", [P, T, 64]), sb("tmp", [P, T, 64]), sb("st", [P, 4, T])
        W3 = sb("W3", [64, 3, 64])
        wp = sb("wp", [64, 64])
        WT = sb("WT", [64, 192])
        XT = sb("XT", [64, COLS])
        qkv = sb("qkv", [P, T, 192])
        sq = sb("sq", [P, T, 128])
        hi, mid, lo = sb("hi", [P, T, 128], BF16), sb("mid", [P, T, 128], BF16), sb("lo", [P, T, 128], BF16)
        pm = sb("pm", [P, T, 64])
        qkw = sb("qkw", [P, 2, 2])
        c_in, chain, var_ready, std_ready = sem("c_in"), sem("chain"), sem("var"), sem("std")
        x_ok, wt_ps, wt_sb, tr_ps, tr_sb = sem("x_ok"), sem("wt_ps"), sem("wt_sb"), sem("tr_ps"), sem("tr_sb")
        qkv_ps, qkv_sb, z_ok, m_ok, r_ok = sem("qkv_ps"), sem("qkv_sb"), sem("zeros"), sem("m_ok"), sem("r_ok")
        with nc.Block() as block:
            @block.sync
            def _(sp):
                sp.dma_start(W3[:], A["L2_attn_w_qkv"].rearrange("(a o) d -> o a d", a=3)).then_inc(c_in, 16)
                sp.dma_start(wp[:], A["L2_attn_w_proj"]).then_inc(c_in, 16)
                sp.dma_start(qkw[:, 0], row(A["L2_attn_qn_w"], P)).then_inc(c_in, 16)
                sp.dma_start(qkw[:, 1], row(A["L2_attn_kn_w"], P)).then_inc(c_in, 16)

            @block.gpsimd
            def _(pool):
                nc.gpsimd.memset(Q12[:, :, :, 12:32], 0.0).then_inc(z_ok, 1)
                pool.wait_ge(z_ok, 1)
                nc.gpsimd.memset(K12[:, :, :, 12:32], 0.0).then_inc(z_ok, 1)
                pool.wait_ge(z_ok, 2)
                nc.gpsimd.memset(V1[:], 1.0).then_inc(z_ok, 1)

            @block.vector
            def _(dve):
                link = Chain(dve, chain)
                tt = nc.vector.tensor_tensor
                layernorm_dve(nc, dve, link, K.h[:], xn[:], tmp[:], st[:], var_ready, std_ready)
                nc.vector.tensor_copy(st[:, 0, :], st[:, 3, :]).then_inc(x_ok, 1)
                dve.wait_ge(c_in, 64)
                dve.wait_ge(qkv_sb, T)
                qk = qkv[:, :, 0:128]
                link(tt(sq[:], qk, qk, ALU.mult))
                link(nc.vector.tensor_reduce(pm[:], sq[:].rearrange("p t (h e) -> p t h e", e=2), AX.X, ALU.add))
                nc.vector.tensor_scalar(pm[:], pm[:], 0.5, 1e-6, ALU.mult, ALU.add).then_inc(m_ok, 1)
                dve.wait_ge(r_ok, 1)
                link(nc.vector.reciprocal(tmp[:], pm[:]))
                link(tt(qk.rearrange("p t (h e) -> p t h e", e=2), qk.rearrange("p t (h e) -> p t h e", e=2),
                        tmp[:].unsqueeze(3).to_broadcast([P, T, 64, 2]), ALU.mult))
                for a in range(2):
                    v = qkv[:, :, 64 * a:64 * a + 64].rearrange("p t (h e) -> p t h e", e=2)
                    for e in range(2):
                        link(nc.vector.tensor_scalar(v[:, :, :, e], v[:, :, :, e], qkw[:, a, e:e + 1], None, ALU.mult))
                link(nc.vector.tensor_copy(hi[:], qk))
                link(tt(sq[:], qk, hi[:], ALU.subtract))
                link(nc.vector.tensor_copy(mid[:], sq[:]))
                link(tt(sq[:], sq[:], mid[:], ALU.subtract))
                link(nc.vector.tensor_copy(lo[:], sq[:]))
                dve.wait_ge(z_ok, 3)
                for dst, off, parts in ((Q12, 0, (hi, hi, mid, mid, hi, lo)), (K12, 64, (hi, mid, hi, mid, lo, hi))):
                    for k, part in enumerate(parts):
                        nc.vector.tensor_copy(dst[:, :, :, 2 * k:2 * k + 2],
                                              part[:, :, off:off + 64].rearrange("p t (h e) -> p t h e", e=2))
                nc.vector.tensor_copy(V1[:, :, 0:96].rearrange("p t (h e) -> p t h e", e=3)[:, :, :, 0:2],
                                      qkv[:, :, 128:192].rearrange("p t (h e) -> p t h e", e=2))

            @block.scalar
            def _(act):
                root_act(nc, act, st[:], var_ready, std_ready)
                act.wait_ge(wt_ps, 1)
                nc.scalar.copy(WT[:], ps[0:64, 7, 0:192]).then_inc(wt_sb, 1)
                nc.scalar.copy(wpT[:], ps[0:64, 7, 192:256]).then_inc(wt_sb, 1)
                for g in range(NG):
                    act.wait_ge(tr_ps, g + 1)
                    nc.scalar.copy(XT[:, g * GRP:(g + 1) * GRP], ps[0:64, g, 0:GRP]).then_inc(tr_sb, 1)
                for t in range(T):
                    act.wait_ge(qkv_ps, t + 1)
                    nc.scalar.copy(qkv[:, t], ps[0:P, t % 8, 0:192]).then_inc(qkv_sb, 1)
                act.wait_ge(m_ok, 1)
                nc.scalar.activation(pm[:], pm[:], ACT.Sqrt).then_inc(r_ok, 1)

            @block.tensor
            def _(pe):
                pe.wait_ge(c_in, 64)
                for i in range(3):
                    nc.tensor.transpose(ps[0:64, 7, 64 * i:64 * i + 64], W3[:, i], K.ident[0:64, 0:64])
                nc.tensor.transpose(ps[0:64, 7, 192:256], wp[:], K.ident[0:64, 0:64]).then_inc(wt_ps, 1)
                pe.wait_ge(x_ok, 1)
                transposes(nc, K, lambda t: xn[:, t, :], P, 64, tr_ps)
                pe.wait_ge(tr_sb, NG)
                pe.wait_ge(wt_sb, 2)
                for t in range(T):
                    if t >= 8:
                        pe.wait_ge(qkv_sb, t - 7)
                    nc.tensor.matmul(ps[0:P, t % 8, 0:192], XT[:, t * P:(t + 1) * P], WT[:],
                                     start=True, stop=True).then_inc(qkv_ps, 1)


def pairs_attend(nc, K, A, Q12, K12, V1, Y):
    SCALE = float(np.float32(1.0 / np.sqrt(2)))
    HG = 8
    units, last_of = [], {}
    for bh in range(B * HG):
        for c in range(3):
            for j in range(3 * c + 3):
                for qp in range(2):
                    units.append((bh, c, j, qp))
            last_of[bh * 3 + c] = len(units) - 1
    per = len(units) // (B * HG)
    diag = [0]
    for bh, c, j, qp in units:
        diag.append(diag[-1] + (j >= 3 * c))
    N = len(units)
    SPLIT = 5
    with ExitStack() as ctx:
        sb = lambda n, s, dt=F32: K.sb("pt_" + n, s, dt, ctx=ctx)
        sem = lambda n: K.sem("pt_" + n)
        ps = K.ps
        identb = sb("identb", [P, P], BF16)
        causal = sb("causal", [P, P])
        QZ = sb("QZ", [128, 2, 4, PADSEQ], BF16)
        KT = sb("KT", [128, 2, PADSEQ], BF16)
        PT = sb("PT", [P, 4, 2, GRP])
        c_in, id_ok, z_ok, trq_ps, trk_ps, q_sb, k_sb = (sem("c_in"), sem("id_ok"), sem("zeros"), sem("trq_ps"),
                                                         sem("trk_ps"), sem("q_sb"), sem("k_sb"))
        s_ps, exp_ok, mask_ok, av_ps, y_sb = sem("s_ps"), sem("exp_ok"), sem("mask_ok"), sem("av_ps"), sem("y_sb")
        with nc.Block() as block:
            @block.sync
            def _(sp):
                sp.dma_start(causal[:], A["c_causal"]).then_inc(c_in, 16)

            @block.gpsimd
            def _(pool):
                nc.gpsimd.memset(QZ[:], 0.0).then_inc(z_ok, 1)

            @block.vector
            def _(dve):
                nc.vector.tensor_copy(identb[:], K.ident[0:P, 0:P]).then_inc(id_ok, 1)

                def bring_q(bh):
                    dve.wait_ge(trq_ps, bh + 1)
                    if bh >= 2:
                        dve.wait_ge(s_ps, per * (bh - 1))
                    for q in range(4):
                        for k, (t0, t1) in enumerate(((0, SPLIT), (SPLIT, NT))):
                            ins = nc.vector.tensor_copy(
                                QZ[32 * q:32 * q + 32, bh % 2, q, t0 * P:t1 * P],
                                ps[32 * q:32 * q + 32, 6 + k, :].bitcast(BF16)[:, 0:(t1 - t0) * P])
                    ins.then_inc(q_sb, 1)

                def bring_k(bh):
                    dve.wait_ge(trk_ps, bh + 1)
                    for k, (t0, t1) in enumerate(((0, SPLIT), (SPLIT, NT))):
                        ins = nc.vector.tensor_copy(KT[:, bh % 2, t0 * P:t1 * P],
                                                    ps[:, 6 + k, :].bitcast(BF16)[:, 0:(t1 - t0) * P])
                    ins.then_inc(k_sb, 1)

                dve.wait_ge(z_ok, 1)
                bring_q(0)
                bring_k(0)
                dve.wait_ge(c_in, 16)
                for n, (bh, c, j, qp) in enumerate(units):
                    if j >= 3 * c:
                        dve.wait_ge(exp_ok, n + 1)
                        d = PT[:, n % 4, :, 0:P]
                        nc.vector.tensor_tensor(d, d, bc(causal[:], 2), ALU.mult).then_inc(mask_ok, 1)
                    if n % per == 12 and bh + 1 < B * HG:
                        bring_q(bh + 1)
                    if n % per == 20 and bh + 1 < B * HG:
                        bring_k(bh + 1)
                    if n == last_of[bh * 3 + c]:
                        dve.wait_ge(av_ps, n + 1)
                        ac = bh * 3 + c
                        col = (bh // HG) * PADSEQ + c * GRP
                        nc.vector.tensor_copy(Y[:, bh % HG, col:col + GRP], ps[:, 4 + ac % 2, 0:GRP]).then_inc(y_sb, 1)

            @block.scalar
            def _(act):
                for n, (bh, c, j, qp) in enumerate(units):
                    w = GRP - max(0, j - 3 * c) * P
                    act.wait_ge(s_ps, n + 1)
                    if n >= 4:
                        act.wait_ge(av_ps, n - 3)
                    b0 = 2 * (n % 2)
                    nc.scalar.activation(PT[:, n % 4, :, 0:w], ps[0:P, b0:b0 + 2, 0:w], ACT.Exp,
                                         scale=SCALE).then_inc(exp_ok, 1)

            @block.tensor
            def _(pe):
                def turn(src, bh, done):
                    for t in range(NT):
                        k, col = (0, t) if t < SPLIT else (1, t - SPLIT)
                        ins = nc.tensor.transpose(
                            ps[:, 6 + k, :].bitcast(BF16)[:, col * P:(col + 1) * P],
                            src[:, (bh // HG) * NT + t, 4 * (bh % HG):4 * (bh % HG) + 4, :].rearrange("p h e -> p (h e)"),
                            identb[:])
                    ins.then_inc(done, 1)

                def weigh(n):
                    bh, c, j, qp = units[n]
                    ac = bh * 3 + c
                    w = GRP - max(0, j - 3 * c) * P
                    pe.wait_ge(exp_ok, n + 1)
                    if j >= 3 * c:
                        pe.wait_ge(mask_ok, diag[n + 1])
                    if j == 0 and ac >= 2:
                        pe.wait_ge(y_sb, ac - 1)
                    for qi in range(2):
                        q = 2 * qp + qi
                        v0 = 3 * (4 * (bh % HG) + q)
                        ins = nc.tensor.matmul(ps[32 * q:32 * q + 32, 4 + ac % 2, GRP - w:GRP],
                                               V1[:, (bh // HG) * NT + j, v0:v0 + 32], PT[:, n % 4, qi, 0:w],
                                               start=(j == 0), stop=(j == 3 * c + 2))
                    ins.then_inc(av_ps, 1)

                pe.wait_ge(id_ok, 1)
                turn(Q12, 0, trq_ps)
                pe.wait_ge(q_sb, 1)
                turn(K12, 0, trk_ps)
                for n in range(N + 4):
                    if n < N:
                        bh, c, j, qp = units[n]
                        if n % per == 0:
                            pe.wait_ge(k_sb, bh + 1)
                        if n >= 2:
                            pe.wait_ge(exp_ok, n - 1)
                        t0 = max(j, 3 * c) * P
                        for qi in range(2):
                            ins = nc.tensor.matmul(ps[0:P, 2 * (n % 2) + qi, 0:(3 * c + 3) * P - t0],
                                                   KT[:, bh % 2, j * P:(j + 1) * P],
                                                   QZ[:, bh % 2, 2 * qp + qi, t0:(3 * c + 3) * P], start=True, stop=True)
                        ins.then_inc(s_ps, 1)
                        if n % per == 12 and bh + 1 < B * HG:
                            pe.wait_ge(k_sb, bh + 1)
                            turn(Q12, bh + 1, trq_ps)
                        if n % per == 20 and bh + 1 < B * HG:
                            pe.wait_ge(q_sb, bh + 2)
                            turn(K12, bh + 1, trk_ps)
                    if n % 2 and n >= 3:
                        for m in (n - 3, n - 2):
                            if m < N:
                                weigh(m)


def pairs_project(nc, K, A, Y, wpT):
    with ExitStack() as ctx:
        sb = lambda n, s, dt=F32: K.sb("po_" + n, s, dt, ctx=ctx)
        sem = lambda n: K.sem("po_" + n)
        ps = K.ps
        Yt = sb("Yt", [P, T, 32, 2])
        rec = sb("rec", [P, 2, 4, 4])
        YT = sb("YT", [64, COLS])
        chain, tr_ps, y_ok, yt_ps, yt_sb, o_ps = (sem("chain"), sem("tr_ps"), sem("y_ok"), sem("yt_ps"),
                                                  sem("yt_sb"), sem("o_ps"))
        N = 2 * T
        with nc.Block() as block:
            @block.tensor
            def _(pe):
                for n in range(N):
                    t = n // 2
                    if n >= 8:
                        pe.wait_ge(y_ok, n - 7)
                    for k in range(4):
                        ins = nc.tensor.transpose(ps[0:P, n % 8, 128 * k:128 * k + 128],
                                                  Y[:, 4 * (n % 2) + k, t * P:(t + 1) * P], K.ident[:])
                    ins.then_inc(tr_ps, 1)
                pe.wait_ge(y_ok, N)
                transposes(nc, K, lambda t: Yt[:, t].rearrange("p h e -> p (h e)"), P, 64, yt_ps)
                for g in range(NG):
                    pe.wait_ge(yt_sb, g + 1)
                    for j in range(3):
                        t = 3 * g + j
                        ins = nc.tensor.matmul(ps[0:P, g, j * 64:(j + 1) * 64], YT[:, t * P:(t + 1) * P], wpT[:],
                                               start=True, stop=True)
                    ins.then_inc(o_ps, 1)

            @block.vector
            def _(dve):
                link = Chain(dve, chain)
                for n in range(N):
                    dve.wait_ge(tr_ps, n + 1)
                    y = ps[0:P, n % 8, :].rearrange("p (k q e) -> p (k q) e", q=4, e=32)
                    r = rec[:, n % 2].rearrange("p k q -> p (k q)")
                    link(nc.vector.reciprocal(r, y[:, :, 2]))
                    nc.vector.tensor_tensor(Yt[:, n // 2, 16 * (n % 2):16 * (n % 2) + 16], y[:, :, 0:2], bcl(r, 2),
                                            ALU.mult).then_inc(y_ok, 1)
                for g in range(NG):
                    dve.wait_ge(o_ps, g + 1)
                    hh = K.h[:, 3 * g:3 * g + 3, :].rearrange("p a b -> p (a b)")
                    nc.vector.tensor_tensor(hh, ps[0:P, g, 0:192], hh, ALU.add)

            @block.scalar
            def _(act):
                for g in range(NG):
                    act.wait_ge(yt_ps, g + 1)
                    nc.scalar.copy(YT[:, g * GRP:(g + 1) * GRP], ps[0:64, g, 0:GRP]).then_inc(yt_sb, 1)


def routed(nc, K, A, pre, E, FF, names, capacity):
    BIG = 1e30
    HID = E * FF
    NCH = HID // 128
    rw, rb, w1n, b1n, w2n, b2n = names
    XR = 96
    RING = 8
    with ExitStack() as ctx:
        sb = lambda n, s, dt=F32: K.sb(pre + n, s, dt, ctx=ctx)
        sem = lambda n: K.sem(pre + n)
        ps = K.ps
        xo, tmp, st = sb("xo", [P, T, XR]), sb("tmp", [P, T, 64]), sb("st", [P, 4, T])
        rwT = sb("rwT", [64, E])
        rin = sb("rin", [E, 64]) if not capacity else None
        rbias = sb("rbias", [P, E])
        first = sb("first", [P, E])
        W1 = sb("W1", [XR, HID])
        W2 = sb("W2", [128, NCH, 64])
        b2 = sb("b2", [XR, 64])
        eye = sb("eye", [XR, E])
        XT = sb("XT", [XR, COLS])
        lg, key = sb("lg", [P, T, E]), sb("key", [P, T, E])
        s1 = sb("s1", [P, 4, T])
        H = sb("H", [128, RING, GRP])
        OT = sb("OT", [64, 2, GRP])
        c_in, wz_ok, chain, var_ready, std_ready = sem("c_in"), sem("wz_ok"), sem("chain"), sem("var"), sem("std")
        x_ok, tr_ps, tr_sb, w1_ok, rw_ps, rw_sb = (sem("x_ok"), sem("tr_ps"), sem("tr_sb"), sem("w1_ok"),
                                                   sem("rw_ps"), sem("rw_sb"))
        lg_ps, one_ok, xo_ps, xo_sb, z_ok = sem("lg_ps"), sem("one_ok"), sem("xo_ps"), sem("xo_sb"), sem("zeros")
        up_ps, re_act, re_dve, dn_ps, dn_sb, bk_ps, bk_ok = (sem("up_ps"), sem("re_act"), sem("re_dve"), sem("dn_ps"),
                                                             sem("dn_sb"), sem("bk_ps"), sem("bk_ok"))
        if capacity:
            tri, onesP = sb("tri", [P, P]), sb("onesP", [P, P])
            rmask, pos = sb("rmask", [P, 1]), sb("pos", [P, T, E])
            run = sb("run", [P, T, E])
            yy, mk, cst = sb("yy", [P, 2, 192]), sb("mk", [P, 2, 192], mybir.dt.uint32), sb("cst", [P, 3, 192])
            e_ok, le_ok, oh_ok, cum_ps = sem("e_ok"), sem("le_ok"), sem("oh_ok"), sem("cum_ps")
        N = NG * NCH
        n_in = 9 if not capacity else 11
        with nc.Block() as block:
            @block.sync
            def _(sp):
                if capacity:
                    sp.dma_start(rwT[:], A[rw]).then_inc(c_in, 16)
                    sp.dma_start(tri[:], A["c_causal"]).then_inc(c_in, 16)
                    sp.dma_start(rmask[:], A["c_rowmask"]).then_inc(c_in, 16)
                else:
                    sp.dma_start(rin[:], A[rw]).then_inc(c_in, 16)
                sp.dma_start(rbias[:], row(A[rb], P)).then_inc(c_in, 16)
                sp.dma_start(first[:], A[f"c_first{E}"]).then_inc(c_in, 16)
                sp.dma_start(W1[0:64].rearrange("d (e f) -> d e f", e=E), A[w1n].rearrange("e d f -> d e f")
                             ).then_inc(c_in, 16)
                sp.dma_start(W2[:], A[w2n].rearrange("e f d -> (e f) d").rearrange("(c p) d -> p c d", p=128)
                             ).then_inc(c_in, 16)
                sp.wait_ge(z_ok, 3)
                sp.dma_start(W1[64:64 + E], row(A[b1n].rearrange("e f -> (e f)"), E)).then_inc(c_in, 16)
                sp.dma_start(b2[64:64 + E], A[b2n]).then_inc(c_in, 16)
                sp.dma_start(eye[64:64 + E], A[f"c_eye{E}"]).then_inc(c_in, 16)
                sp.dma_start(eye[0:E], A[f"c_eye{E}"]).then_inc(c_in, 16)

            @block.gpsimd
            def _(pool):
                nc.gpsimd.memset(xo[:, :, 64:XR], 0.0).then_inc(z_ok, 1)
                pool.wait_ge(z_ok, 1)
                nc.gpsimd.memset(W1[64:XR], 0.0).then_inc(z_ok, 1)
                pool.wait_ge(z_ok, 2)
                nc.gpsimd.memset(b2[64:XR], 0.0).then_inc(z_ok, 1)

            @block.vector
            def _(dve):
                link = Chain(dve, chain)
                tt = nc.vector.tensor_tensor
                layernorm_dve(nc, dve, link, K.h[:], xo[:, :, 0:64], tmp[:], st[:], var_ready, std_ready)
                nc.vector.tensor_copy(st[:, 0, :], st[:, 3, :]).then_inc(x_ok, 1)
                dve.wait_ge(c_in, 16 * n_in)
                w = W1[64:64 + E].rearrange("p (e f) -> p e f", e=E)
                link(tt(w, w, bcl(eye[64:64 + E], FF), ALU.mult))
                link(nc.vector.tensor_scalar(eye[64:64 + E], eye[64:64 + E], -1.0, BIG, ALU.add, ALU.mult))
                tt(w, w, bcl(eye[64:64 + E], FF), ALU.add).then_inc(w1_ok, 1)
                dve.wait_ge(lg_ps, 1)
                per = 512 // E
                for k in range((T + per - 1) // per):
                    t0, t1 = k * per, min(T, (k + 1) * per)
                    link(tt(lg[:, t0:t1], ps[0:P, 6 + k, 0:(t1 - t0) * E].rearrange("p (t e) -> p t e", e=E),
                            bc(rbias[:], t1 - t0), ALU.add))
                link(nc.vector.tensor_reduce(s1[:, 0], lg[:], AX.X, ALU.max))
                if capacity:
                    tt(lg[:], lg[:], bcl(s1[:, 0], E), ALU.subtract).then_inc(e_ok, 1)
                    dve.wait_ge(le_ok, 1)
                    link(nc.vector.tensor_reduce(s1[:, 1], lg[:], AX.X, ALU.add))
                    link(nc.vector.reciprocal(s1[:, 1], s1[:, 1]))
                    link(tt(lg[:], lg[:], bcl(s1[:, 1], E), ALU.mult))
                    link(nc.vector.tensor_reduce(s1[:, 0], lg[:], AX.X, ALU.max))
                link(tt(key[:], lg[:], bcl(s1[:, 0], E), ALU.is_equal))
                link(tt(key[:], key[:], bc(first[:], T), ALU.mult))
                link(nc.vector.tensor_reduce(s1[:, 1], key[:], AX.X, ALU.max))
                tt(xo[:, :, 64:64 + E], key[:], bcl(s1[:, 1], E), ALU.is_equal).then_inc(one_ok, 1)
                if capacity:
                    link(nc.vector.memset(onesP[:], 1.0))
                    dve.wait_ge(one_ok, 1)
                    link(nc.vector.tensor_copy(key[:], xo[:, :, 64:64 + E]))
                    for b in range(B):
                        t = b * NT + NT - 1
                        nc.vector.tensor_scalar(key[:, t], key[:, t], rmask[:, 0:1], None, ALU.mult).then_inc(oh_ok, 1)
                    dve.wait_ge(cum_ps, 1)
                    link(nc.vector.memset(run[:, 0], 0.0))
                    for t in range(1, T):
                        link(tt(run[:, t], ps[0:P, 7, E * (t - 1):E * t], run[:, t - 1], ALU.add))
                    link(tt(pos[:], ps[0:P, 6, 0:T * E].rearrange("p (t e) -> p t e", e=E), run[:], ALU.add))
                    link(tt(pos[:], pos[:], key[:], ALU.mult))
                    link(nc.vector.tensor_reduce(s1[:, 2], pos[:], AX.X, ALU.add))
                    link(nc.vector.tensor_scalar(s1[:, 2], s1[:, 2], float(capacity), None, ALU.is_le))
                    link(tt(s1[:, 3], s1[:, 2], s1[:, 0], ALU.mult))
                    for k, v in enumerate((1e4, -1e4, 0.0)):
                        link(nc.vector.memset(cst[:, k], v))

                def back(g):
                    dve.wait_ge(bk_ps, g + 1)
                    s = slice(3 * g, 3 * g + 3)
                    hh = K.h[:, s].rearrange("p a b -> p (a b)")
                    if not capacity:
                        tt(hh, ps[0:P, 6 + g % 2, 0:192], hh, ALU.add).then_inc(bk_ok, 1)
                        return
                    y = yy[:, g % 2]
                    link(tt(y.rearrange("p (a b) -> p a b", a=3),
                            ps[0:P, 6 + g % 2, 0:192].rearrange("p (a b) -> p a b", a=3), bcl(s1[:, 3, s], 64),
                            ALU.mult))
                    FMAX = 3.4028234663852886e38
                    for k, (op, v) in enumerate(((ALU.is_gt, FMAX), (ALU.is_lt, -FMAX), (ALU.not_equal, None))):
                        if v is None:
                            link(tt(mk[:, g % 2], y, y, op))
                        else:
                            link(nc.vector.tensor_scalar(mk[:, g % 2], y, v, None, op))
                        link(nc.vector.copy_predicated(y, mk[:, g % 2], cst[:, k]))
                    tt(hh, y, hh, ALU.add).then_inc(bk_ok, 1)

                for g in range(NG):
                    for c in range(NCH):
                        n = g * NCH + c
                        if n % 2:
                            dve.wait_ge(up_ps, n + 1)
                            if n >= RING:
                                dve.wait_ge(dn_ps, n - RING + 1)
                            nc.vector.tensor_scalar(H[:, n % RING], ps[:, n % 4, 0:GRP], 0.0, None,
                                                    ALU.max).then_inc(re_dve, 1)
                    if g:
                        back(g - 1)
                back(NG - 1)

            @block.scalar
            def _(act):
                root_act(nc, act, st[:], var_ready, std_ready)
                for g in range(NG):
                    act.wait_ge(tr_ps, g + 1)
                    nc.scalar.copy(XT[0:64, g * GRP:(g + 1) * GRP], ps[0:64, g, 0:GRP]).then_inc(tr_sb, 1)
                if not capacity:
                    act.wait_ge(rw_ps, 1)
                    nc.scalar.copy(rwT[:], ps[0:64, 6, 0:E]).then_inc(rw_sb, 1)
                else:
                    act.wait_ge(e_ok, 1)
                    nc.scalar.activation(lg[:], lg[:], ACT.Exp).then_inc(le_ok, 1)
                for g in range(NG):
                    act.wait_ge(xo_ps, g + 1)
                    nc.scalar.copy(XT[:, g * GRP:(g + 1) * GRP], ps[0:XR, g, 0:GRP]).then_inc(xo_sb, 1)

                def out(g):
                    act.wait_ge(dn_ps, (g + 1) * NCH)
                    act.wait_ge(bk_ok, g) if g else None
                    nc.scalar.activation(OT[:, g % 2], ps[0:64, 4 + g % 2, 0:GRP],
                                         ACT.Copy if capacity else ACT.Relu).then_inc(dn_sb, 1)

                for g in range(NG):
                    for c in range(0, NCH, 2):
                        n = g * NCH + c
                        act.wait_ge(up_ps, n + 1)
                        if n >= RING:
                            act.wait_ge(dn_ps, n - RING + 1)
                        nc.scalar.activation(H[:, n % RING], ps[:, n % 4, 0:GRP], ACT.Relu).then_inc(re_act, 1)
                    if g:
                        out(g - 1)
                out(NG - 1)

            @block.tensor
            def _(pe):
                pe.wait_ge(x_ok, 1)
                transposes(nc, K, lambda t: xo[:, t, 0:64], P, 64, tr_ps)
                pe.wait_ge(c_in, 16 * n_in)
                if not capacity:
                    nc.tensor.transpose(ps[0:64, 6, 0:E], rin[:], K.ident[0:E, 0:E]).then_inc(rw_ps, 1)
                    pe.wait_ge(rw_sb, 1)
                pe.wait_ge(tr_sb, NG)
                per = 512 // E
                for t in range(T):
                    ins = nc.tensor.matmul(ps[0:P, 6 + t // per, (t % per) * E:(t % per + 1) * E],
                                           XT[0:64, t * P:(t + 1) * P], rwT[:], start=True, stop=True)
                ins.then_inc(lg_ps, 1)
                pe.wait_ge(one_ok, 1)
                pe.wait_ge(z_ok, 3)
                transposes(nc, K, lambda t: xo[:, t, :], P, XR, xo_ps)
                if capacity:
                    pe.wait_ge(oh_ok, 2)
                    k2 = key[:].rearrange("p t e -> p (t e)")
                    nc.tensor.matmul(ps[0:P, 6, 0:T * E], tri[:], k2, start=True, stop=True)
                    nc.tensor.matmul(ps[0:P, 7, 0:T * E], onesP[:], k2, start=True, stop=True).then_inc(cum_ps, 1)
                pe.wait_ge(w1_ok, 1)
                pe.wait_ge(xo_sb, NG)

                def down(n):
                    g, c = n // NCH, n % NCH
                    pe.wait_ge(re_dve if n % 2 else re_act, n // 2 + 1)
                    if c == 0 and g >= 2:
                        pe.wait_ge(dn_sb, g - 1)
                    o = ps[0:64, 4 + g % 2, 0:GRP]
                    if c == 0:
                        nc.tensor.matmul(o, b2[64:XR], XT[64:XR, g * GRP:(g + 1) * GRP], start=True, stop=False)
                    nc.tensor.matmul(o, W2[:, c], H[:, n % RING], start=False, stop=(c == NCH - 1)).then_inc(dn_ps, 1)

                def turn(g):
                    pe.wait_ge(dn_sb, g + 1)
                    if g >= 2:
                        pe.wait_ge(bk_ok, g - 1)
                    for j in range(3):
                        ins = nc.tensor.transpose(ps[0:P, 6 + g % 2, 64 * j:64 * j + 64],
                                                  OT[:, g % 2, j * P:(j + 1) * P], K.ident[0:64, 0:64])
                    ins.then_inc(bk_ps, 1)

                for n in range(N + 3):
                    if n < N:
                        g, c = n // NCH, n % NCH
                        if n >= 4:
                            pe.wait_ge(re_dve if n % 2 else re_act, (n - 4) // 2 + 1)
                        nc.tensor.matmul(ps[:, n % 4, 0:GRP], W1[:, c * 128:(c + 1) * 128],
                                         XT[:, g * GRP:(g + 1) * GRP], start=True, stop=True).then_inc(up_ps, 1)
                    if n >= 3:
                        down(n - 3)
                        if (n - 3) % NCH == NCH - 1 and (n - 3) // NCH:
                            turn((n - 3) // NCH - 1)
                turn(NG - 1)


def stage_switch(nc, K, A):
    routed(nc, K, A, "sw_", 32, 16, ["L2_ffn_" + n for n in ("router_w", "router_b", "W1", "b1", "W2", "b2")], None)


def stage_capacity(nc, K, A):
    slots = -(-5 * B * SEQ // (4 * 8))
    routed(nc, K, A, "cp_", 8, 256, ["L3_ffn_" + n for n in ("gate_w", "gate_b", "w1", "b1", "w2", "b2")], slots)


NSEL = 255
SELP = 256


def stage_distance(nc, K, A):
    with ExitStack() as ctx:
        sb = lambda n, s, dt=F32: K.sb("ds_" + n, s, dt, ctx=ctx)
        xn = sb("xn", [P, T, 128])
        SelT = sb("SelT", [128, 2, PADSEQ])
        fT = sb("fT", [65, 64])
        acc = sb("acc", [128, B, 2, 64])
        with ExitStack() as inner:
            si = lambda n, s, dt=F32: K.sb("di_" + n, s, dt, ctx=inner)
            QH = si("QH", [128, 8, SELP])
            KH, NK = si("KH", [128, 8, SELP]), si("NK", [128, 8, SELP])
            VR = si("VR", [128, B, 4, 8, 65])
            KS = si("KS", [128, B, 4, 4])
            distance_prepare(nc, K, A, xn, SelT, fT, QH, KH, NK, VR, KS)
            distance_attend(nc, K, A, QH, KH, NK, VR, KS, acc)
        distance_output(nc, K, A, xn, SelT, fT, acc)


def distance_prepare(nc, K, A, xn, SelT, fT, QH, KH, NK, VR, KS):
    with ExitStack() as ctx:
        sb = lambda n, s, dt=F32: K.sb("dp_" + n, s, dt, ctx=ctx)
        sem = lambda n: K.sem("dp_" + n)
        ps = K.ps
        tmp, st = sb("tmp", [P, T, 64]), sb("st", [P, 4, T])
        ai, ci = sb("ai", [P, NSEL], I32), sb("ci", [128, 2], I32)
        af, cf = sb("af", [P, SELP]), sb("cf", [128, 2])
        tok, tokrow = sb("tok", [P, NT]), sb("tokrow", [128, PADSEQ])
        Sel = sb("Sel", [P, NT, SELP])
        wq, wv, fo = sb("wq", [128, 4, 65]), sb("wv", [128, 4, 65]), sb("fo", [64, 65])
        WqT, WvT = sb("WqT", [65, 512]), sb("WvT", [65, 512])
        wk = sb("wk", [128, 4])
        half = sb("half", [128, 2])
        wkT = sb("wkT", [64, 8])
        kh = sb("kh", [128, 2, 4])
        XG2 = sb("XG2", [128, B, SELP])
        XG1 = sb("XG1", [65, B, SELP])
        XD = sb("XD", [65, B, 4, 128])
        c_in, z_ok, chain, var_ready, std_ready = sem("c_in"), sem("zeros"), sem("chain"), sem("var"), sem("std")
        x_ok, sel_ok, w_ps, w_sb, g_ps, g_sb, xd_ok = (sem("x_ok"), sem("sel_ok"), sem("w_ps"), sem("w_sb"),
                                                       sem("g_ps"), sem("g_sb"), sem("xd_ok"))
        q_ps, q_sb, v_ps, v_sb, ks_ps = sem("q_ps"), sem("q_sb"), sem("v_ps"), sem("v_sb"), sem("ks_ps")
        with nc.Block() as block:
            @block.sync
            def _(sp):
                sp.dma_start(ai[:], row(A["L3_attn_a2a"], P)).then_inc(c_in, 16)
                sp.dma_start(ci[:, 0:1], A["L3_attn_a2a"][0:128].unsqueeze(1)).then_inc(c_in, 16)
                sp.dma_start(ci[0:127, 1:2], A["L3_attn_a2a"][128:NSEL].unsqueeze(1)).then_inc(c_in, 16)
                sp.dma_start(tok[:], A["c_token"]).then_inc(c_in, 16)
                sp.dma_start(tokrow[:], row(A["c_tokenrow"], 128)).then_inc(c_in, 16)
                sp.dma_start(wq[:], A["L3_attn_wq"].rearrange("(k p) d -> p k d", p=128)).then_inc(c_in, 16)
                sp.dma_start(wv[:], A["L3_attn_wv"].rearrange("(k p) d -> p k d", p=128)).then_inc(c_in, 16)
                sp.dma_start(fo[:], A["L3_attn_fanout_w"]).then_inc(c_in, 16)
                with nc.allow_non_contiguous_dma(reason="four columns"):
                    for h in range(2):
                        sp.dma_start(wk[64 * h:64 * h + 64],
                                     A["L3_attn_wk"].rearrange("(p h) c -> h c p", h=2)[h]).then_inc(c_in, 16)
                    sp.dma_start(wkT[:], A["L3_attn_wk"].rearrange("h c -> c h")).then_inc(c_in, 16)
                sp.dma_start(half[:], A["c_half"]).then_inc(c_in, 16)

            @block.gpsimd
            def _(pool):
                nc.gpsimd.memset(XG1[64:65], 1.0).then_inc(z_ok, 1)
                pool.wait_ge(z_ok, 1)
                nc.gpsimd.memset(XG1[64:65, :, NSEL:SELP], 0.0).then_inc(z_ok, 1)

            @block.vector
            def _(dve):
                link = Chain(dve, chain)
                tt = nc.vector.tensor_tensor
                link(nc.vector.memset(af[:], -1.0))
                link(nc.vector.memset(cf[:], -1.0))
                dve.wait_ge(c_in, 192)
                link(nc.vector.tensor_copy(af[:, 0:NSEL], ai[:]))
                link(nc.vector.tensor_copy(cf[:, 0:1], ci[:, 0:1]))
                link(nc.vector.tensor_copy(cf[0:127, 1:2], ci[0:127, 1:2]))
                for i in range(NT):
                    nc.vector.tensor_scalar(Sel[:, i], af[:], tok[:, i:i + 1], None, ALU.is_equal).then_inc(sel_ok, 1)
                for k in range(2):
                    nc.vector.tensor_scalar(SelT[:, k], tokrow[:], cf[:, k:k + 1], None, ALU.is_equal)
                layernorm_dve(nc, dve, link, K.h[:], xn[:, :, 0:64], tmp[:], st[:], var_ready, std_ready)
                nc.vector.tensor_copy(xn[:, :, 64:128], xn[:, :, 0:64]).then_inc(x_ok, 1)
                for b in range(B):
                    dve.wait_ge(g_ps, b + 1)
                    link(nc.vector.tensor_copy(XG2[:, b], ps[:, 2 + b, 0:SELP]))
                    nc.vector.tensor_copy(XG1[0:64, b], XG2[0:64, b]).then_inc(g_sb, 1)
                dve.wait_ge(z_ok, 2)
                dve.wait_ge(g_sb, 2)
                for b in range(B):
                    nc.vector.tensor_copy(
                        XD[:, b].rearrange("p k (q h m) -> p (k q) h m", q=4, h=2),
                        XG1[:, b].rearrange("p (a m) -> p a m", m=16).unsqueeze(2).to_broadcast([65, 16, 2, 16])
                    ).then_inc(xd_ok, 1)
                for u in range(8):
                    link(nc.vector.tensor_scalar(KH[:, u], XG2[:, u // 4], wk[:, u % 4:u % 4 + 1], None, ALU.mult))
                link(nc.vector.tensor_scalar(NK[:], KH[:], -1.0, None, ALU.mult))
                for b in range(B):
                    for k in range(4):
                        n = 4 * b + k
                        if n == 0:
                            dve.wait_ge(ks_ps, 1)
                        ks = ps[:, 0, 8 * n:8 * n + 8].rearrange("p (a h) -> p a h", h=2)
                        for h in range(2):
                            link(nc.vector.tensor_scalar(kh[:, h], ks[:, :, h], half[:, h:h + 1], -0.125, ALU.mult,
                                                         ALU.mult))
                        link(tt(KS[:, b, k], kh[:, 0], kh[:, 1], ALU.add))
                        nc.vector.tensor_copy(VR[:, b, k, :, 64].rearrange("p (a h) -> p a h", h=2), bc(half[:], 4))
                        dve.wait_ge(v_ps, n + 1)
                        for hp in range(4):
                            ins = tt(VR[:, b, k, 2 * hp:2 * hp + 2, 0:64],
                                     ps[:, 4 + n % 4, 128 * hp:128 * hp + 128].rearrange("p (h w) -> p h w", h=2),
                                     bcl(half[:], 64), ALU.mult)
                        ins.then_inc(v_sb, 1)

            @block.scalar
            def _(act):
                root_act(nc, act, st[:], var_ready, std_ready)
                act.wait_ge(w_ps, 1)
                nc.scalar.copy(WqT[:], ps[0:65, 0, :]).then_inc(w_sb, 1)
                nc.scalar.copy(WvT[:], ps[0:65, 1, :]).then_inc(w_sb, 1)
                nc.scalar.copy(fT[:], ps[0:65, 7, 0:64]).then_inc(w_sb, 1)
                for u in range(8):
                    act.wait_ge(q_ps, u + 1)
                    nc.scalar.copy(QH[:, u], ps[:, u % 4, 0:SELP]).then_inc(q_sb, 1)

            @block.tensor
            def _(pe):
                pe.wait_ge(c_in, 192)
                for i, w in enumerate((wq, wv)):
                    for k in range(4):
                        nc.tensor.transpose(ps[0:65, i, 128 * k:128 * k + 128], w[:, k], K.ident[:])
                nc.tensor.transpose(ps[0:65, 7, 0:64], fo[:], K.ident[0:64, 0:64]).then_inc(w_ps, 1)
                pe.wait_ge(sel_ok, NT)
                pe.wait_ge(x_ok, 1)
                for b in range(B):
                    for i in range(NT):
                        ins = nc.tensor.matmul(ps[:, 2 + b, 0:SELP], xn[:, b * NT + i, :], Sel[:, i],
                                               start=(i == 0), stop=(i == NT - 1))
                    ins.then_inc(g_ps, 1)
                pe.wait_ge(xd_ok, 2)
                pe.wait_ge(w_sb, 3)
                for u in range(8):
                    if u >= 4:
                        pe.wait_ge(q_sb, u - 3)
                    nc.tensor.matmul(ps[:, u % 4, 0:SELP], WqT[:, 128 * (u % 4):128 * (u % 4) + 128], XG1[:, u // 4],
                                     start=True, stop=True).then_inc(q_ps, 1)
                pe.wait_ge(q_sb, 8)
                for n in range(8):
                    ins = nc.tensor.matmul(ps[:, 0, 8 * n:8 * n + 8], XD[0:64, n // 4, n % 4], wkT[:],
                                           start=True, stop=True)
                ins.then_inc(ks_ps, 1)
                for n in range(8):
                    if n >= 4:
                        pe.wait_ge(v_sb, n - 3)
                    nc.tensor.matmul(ps[:, 4 + n % 4, :], XD[:, n // 4, n % 4], WvT[:],
                                     start=True, stop=True).then_inc(v_ps, 1)


def distance_attend(nc, K, A, QH, KH, NK, VR, KS, acc):
    RING = 16
    ACT_SHARE = (3, 6, 9)
    items = []
    for u in range(8):
        for k in range(4):
            for i in range(64):
                q, m = i % 4, i // 4
                if 64 * k + 16 * q + m < NSEL:
                    items.append((u, k, q, m))
    mine = [n % 10 in ACT_SHARE for n in range(len(items))]
    before = [0]
    for a in mine:
        before.append(before[-1] + a)
    end = {}
    for n, (u, k, q, m) in enumerate(items):
        end[4 * u + k] = n + 1
    with ExitStack() as ctx:
        sb = lambda n, s, dt=F32: K.sb("da_" + n, s, dt, ctx=ctx)
        sem = lambda n: K.sem("da_" + n)
        ps = K.ps
        win = sb("win", [128, 47])
        own = sb("own", [128, 2, 128])
        AD = sb("AD", [128, RING, SELP])
        PP = sb("PP", [128, 8, SELP])
        rec = sb("rec", [128, 2, 2])
        c_in, ad_act, ad_dve, red_ps, exp_ok, av_ps, av_sb, chain = (
            sem("c_in"), sem("ad_act"), sem("ad_dve"), sem("red_ps"), sem("exp_ok"), sem("av_ps"), sem("av_sb"),
            sem("chain"))
        with nc.Block() as block:
            @block.sync
            def _(sp):
                sp.dma_start(win[:], A["c_window"]).then_inc(c_in, 16)
                sp.dma_start(own[:], A["c_own"]).then_inc(c_in, 16)

            @block.vector
            def _(dve):
                link = Chain(dve, chain)

                def gather(u):
                    b = u // 4
                    for d in range(2):
                        dve.wait_ge(av_ps, 2 * u + d + 1)
                        o = ps[:, 4 + (2 * u + d) % 4, 0:130].rearrange("p (h w) -> p h w", h=2)
                        link(nc.vector.reciprocal(rec[:, d], o[:, :, 64]))
                        for h in range(2):
                            if u % 4 == 0 and h == 0:
                                ins = nc.vector.tensor_scalar(acc[:, b, d], o[:, h, 0:64], rec[:, d, h:h + 1], None,
                                                              ALU.mult)
                            else:
                                ins = nc.vector.scalar_tensor_tensor(acc[:, b, d], o[:, h, 0:64], rec[:, d, h:h + 1],
                                                                     acc[:, b, d], ALU.mult, ALU.add)
                            if h == 0:
                                link(ins)
                        ins.then_inc(av_sb, 1)
                    dve.wait_ge(av_sb, 2 * u + 2)

                for n, (u, k, q, m) in enumerate(items):
                    if not mine[n]:
                        if n >= RING:
                            dve.wait_ge(red_ps, n - RING + 1)
                        s = 64 * k + 16 * q + m
                        nc.vector.tensor_scalar(AD[:, n % RING], QH[:, u], KH[:, u, s:s + 1], 0.0, ALU.subtract,
                                                ALU.max).then_inc(ad_dve, 1)
                    if k == 1 and u and n + 1 == end[4 * u + 1]:
                        gather(u - 1)
                gather(7)

            @block.scalar
            def _(act):
                def exps(e):
                    act.wait_ge(red_ps, end[e])
                    if e >= 8:
                        act.wait_ge(av_ps, 2 * (e // 4 - 1))
                    nc.scalar.activation(PP[:, e % 8], ps[:, e % 4, 0:SELP], ACT.Exp, scale=-0.125,
                                         bias=KS[:, e // 16, e % 4, e // 4 % 4:e // 4 % 4 + 1]).then_inc(exp_ok, 1)

                for n, (u, k, q, m) in enumerate(items):
                    if mine[n]:
                        if n >= RING:
                            act.wait_ge(red_ps, n - RING + 1)
                        s = 64 * k + 16 * q + m
                        nc.scalar.activation(AD[:, n % RING], QH[:, u], ACT.Relu,
                                             bias=NK[:, u, s:s + 1]).then_inc(ad_act, 1)
                    e = 4 * u + k
                    if e and n == end[e - 1] + 20:
                        exps(e - 1)
                exps(31)

            @block.tensor
            def _(pe):
                pe.wait_ge(c_in, 32)

                def weigh(u):
                    pe.wait_ge(exp_ok, 4 * u + 4)
                    for d in range(2):
                        if u >= 2:
                            pe.wait_ge(av_sb, 2 * u + d - 3)
                        for k in range(4):
                            ins = nc.tensor.matmul(ps[:, 4 + (2 * u + d) % 4, 0:130],
                                                   PP[:, (4 * u + k) % 8, 128 * d:128 * d + 128],
                                                   VR[:, u // 4, k, 2 * (u % 4):2 * (u % 4) + 2, :]
                                                   .rearrange("p h w -> p (h w)"), start=(k == 0), stop=(k == 3))
                        ins.then_inc(av_ps, 1)

                for n, (u, k, q, m) in enumerate(items):
                    if mine[n]:
                        pe.wait_ge(ad_act, before[n + 1])
                    else:
                        pe.wait_ge(ad_dve, n + 1 - before[n + 1])
                    e = 4 * u + k
                    if m == 0 and q == 0 and e >= 4:
                        pe.wait_ge(exp_ok, e - 3)
                    if m == 0 and q == 0:
                        nc.tensor.matmul(ps[:, e % 4, 0:SELP], own[:, k // 3], QH[:, u], start=True, stop=False,
                                         skip_group_check=True)
                    last = m == (14 if (k, q) == (3, 3) else 15)
                    nc.tensor.matmul(ps[32 * q:32 * q + 32, e % 4, 0:SELP], win[:, 15 - m:47 - m], AD[:, n % RING],
                                     start=False, stop=last, skip_group_check=True).then_inc(red_ps, 1)
                    if u and n + 1 == end[4 * u]:
                        weigh(u - 1)
                weigh(7)


def distance_output(nc, K, A, xn, SelT, fT, acc):
    with ExitStack() as ctx:
        sb = lambda n, s, dt=F32: K.sb("dq_" + n, s, dt, ctx=ctx)
        sem = lambda n: K.sem("dq_" + n)
        ps = K.ps
        sig, y = sb("sig", [P, T, 64]), sb("y", [P, T, 64])
        YT = sb("YT", [65, COLS])
        s_ps, sig_ok, y_ok, tr_ps, tr_sb, o_ps, one_ok = (sem("s_ps"), sem("sig_ok"), sem("y_ok"), sem("tr_ps"),
                                                          sem("tr_sb"), sem("o_ps"), sem("one_ok"))
        x_ok = sem("x_ok")
        flat = lambda a, g: a[:, 3 * g:3 * g + 3].rearrange("p a b -> p (a b)")
        with nc.Block() as block:
            @block.gpsimd
            def _(pool):
                nc.gpsimd.memset(YT[64:65], 1.0).then_inc(one_ok, 1)

            @block.tensor
            def _(pe):
                for g in range(NG):
                    for t in range(3 * g, 3 * g + 3):
                        i = (t % NT) * P
                        for k in range(2):
                            ins = nc.tensor.matmul(ps[0:P, g, (t % 3) * 64:(t % 3) * 64 + 64], SelT[:, k, i:i + P],
                                                   acc[:, t // NT, k], start=(k == 0), stop=(k == 1))
                    ins.then_inc(s_ps, 1)
                pe.wait_ge(y_ok, NG)
                transposes(nc, K, lambda t: y[:, t], P, 64, tr_ps)
                pe.wait_ge(one_ok, 1)
                for g in range(NG):
                    pe.wait_ge(tr_sb, g + 1)
                    for j in range(3):
                        t = 3 * g + j
                        ins = nc.tensor.matmul(ps[0:P, g, j * 64:(j + 1) * 64], YT[:, t * P:(t + 1) * P], fT[:],
                                               start=True, stop=True)
                    ins.then_inc(o_ps, 1)

            @block.scalar
            def _(act):
                for g in range(NG):
                    act.wait_ge(s_ps, g + 1)
                    nc.scalar.activation(flat(sig, g), ps[0:P, g, 0:192], ACT.Sigmoid, scale=1.702).then_inc(sig_ok, 1)
                for g in range(NG):
                    act.wait_ge(tr_ps, g + 1)
                    nc.scalar.copy(YT[0:64, g * GRP:(g + 1) * GRP], ps[0:64, g, 0:GRP]).then_inc(tr_sb, 1)

            @block.vector
            def _(dve):
                nc.vector.tensor_tensor(K.h[:], K.h[:], xn[:, :, 0:64], ALU.add).then_inc(x_ok, 1)
                for g in range(NG):
                    dve.wait_ge(sig_ok, g + 1)
                    nc.vector.tensor_tensor(flat(y, g), ps[0:P, g, 0:192], flat(sig, g), ALU.mult).then_inc(y_ok, 1)
                dve.wait_ge(x_ok, 1)
                for g in range(NG):
                    dve.wait_ge(o_ps, g + 1)
                    nc.vector.tensor_tensor(flat(K.h, g), ps[0:P, g, 0:192], flat(K.h, g), ALU.add)


STAGES = [stage_embed, stage_rwkv, stage_depths, stage_linear, stage_gqa, stage_pairs, stage_switch, stage_distance,
          stage_capacity]


def program(nc, A, out, stages):
    with ExitStack() as ctx:
        K = Core(nc, A, ctx)
        for stage in stages:
            stage(nc, K, A)
            if stage in (stage_linear, stage_pairs):
                K.recycle_semaphores()
        written = K.written
        with nc.Block() as block:
            @block.sync
            def _(sp):
                for b in range(B):
                    sp.dma_start(out[b, 0:8 * P, :].rearrange("(t p) d -> p t d", p=P),
                                 K.h[:, b * NT:b * NT + 8, :]).then_inc(written, 16)
                    sp.dma_start(out[b, 8 * P:SEQ, :], K.h[0:P - 1, b * NT + 8, :]).then_inc(written, 16)
                sp.wait_ge(written, 64)


def kernel(**inputs):
    import numpy as _np
    import concourse.bacc as _bacc
    from concourse import mybir as _mybir
    from concourse.bass_utils import run_bass_kernel_spmd as _run

    nc = _bacc.Bacc("TRN2", target_bir_lowering=False, num_devices=1)
    arrays, args = {}, {}
    for name, a in list(inputs.items()) + list(constants().items()):
        a = _np.ascontiguousarray(a)
        arrays[f"in_{name}_dram"] = a
        args[name] = nc.dram_tensor(f"in_{name}_dram", a.shape, _mybir.dt.from_np(a.dtype), kind="ExternalInput").ap()
    out = nc.dram_tensor("out_0_dram", (B, SEQ, D), F32, kind="ExternalOutput").ap()
    program(nc, args, out, STAGES)
    r = _run(nc, [arrays], core_ids=[0])
    return r.results[0]["out_0_dram"]
```

```python
from contextlib import ExitStack

import numpy as np

import concourse.bass as bass
from concourse import mybir

ALU = mybir.AluOpType
ACT = mybir.ActivationFunctionType
F32 = mybir.dt.float32
I32 = mybir.dt.int32
BF16 = mybir.dt.bfloat16
AX = mybir.AxisListType

B = 2
D = 64
SEQ = 1025
P = 114
NT = 9
T = B * NT
PADSEQ = P * NT
COLS = B * PADSEQ
GRP = 3 * P
NG = T // 3
LAST = P - 2
DECAY = -0.6065306597126334
MID = 56
LEVELS = (2, 4, 8, 16, 32, 64)


class Chain:

    def __init__(self, eng, sem):
        self.eng, self.sem, self.n = eng, sem, 0

    def __call__(self, ins):
        self.n += 1
        ins.then_inc(self.sem, 1)
        self.eng.wait_ge(self.sem, self.n)


def constants():
    c = {}
    ident = np.eye(128, dtype=np.float32)
    c["c_ident"] = ident
    c["c_ident2"] = np.concatenate([np.eye(64), np.eye(64)]).astype(np.float32)
    dft = np.zeros((128, 9, 16), np.float64)
    for slot in range(18):
        f, imag = slot % 9, slot // 9
        ang = 2 * np.pi * f * np.arange(16) / 16
        row = (-np.sin(ang) if imag else np.cos(ang)) / 4.0
        dft[(slot % 2) * 64:(slot % 2) * 64 + 64, slot // 2, :] = row
    c["c_dft"] = dft.astype(np.float32)
    s = np.arange(P)[:, None]
    t = np.arange(P)[None, :]
    mid = (s <= MID).astype(np.float64)
    rel = np.stack([(s <= t) - mid, (s < t) - mid], 1)
    c["c_rel"] = rel.astype(np.float32)
    c["c_sums"] = np.concatenate([s <= MID, s > MID], 1).astype(np.float32)
    c["c_mask4"] = np.stack([-(s < t).astype(float), (s <= t), -(s < t).astype(float), (s <= t)], 1).astype(np.float32)
    lev = []
    for l in (1,) + LEVELS:
        lev.append(((s // (2 * l)) == (t // (2 * l))) & ((s // l) % 2 == 0) & ((t // l) % 2 == 1))
    c["c_levels"] = np.stack(lev, 1).astype(np.float32)
    c["c_sub"] = -lev[0].T.astype(np.float32)
    c["c_before"] = (t < s).astype(np.float32)
    rm = np.ones((P, 1), np.float32)
    rm[P - 1] = 0.0
    c["c_rowmask"] = rm
    blk = np.arange(128)
    c["c_block16"] = ((blk[:, None] // 16) == (blk[None, :] // 16)).astype(np.float32)
    inv = 1.0 / 10000.0 ** (np.arange(0, 16, 2, dtype=np.float32) / 16)
    freqs = np.outer(np.arange(PADSEQ, dtype=np.float32), inv)
    cos, sin = np.cos(freqs), np.sin(freqs)
    rope = np.stack([np.concatenate([cos, cos], 1), np.concatenate([-sin, sin], 1)], 1)
    c["c_rope"] = np.ascontiguousarray(rope.reshape(NT, P, 2, 16).transpose(1, 2, 0, 3)).astype(np.float32)
    c["c_negmask"] = np.where(t > s, np.float32(-1e30), np.float32(0))
    e = np.arange(8)
    c["c_before8"] = np.tile((e[None, :] < e[:, None]).astype(np.float32).reshape(1, 8, 8), (P, 1, 1))
    c["c_causal"] = (t >= s).astype(np.float32)
    for n in (8, 32):
        c[f"c_eye{n}"] = np.eye(n, dtype=np.float32)
        c[f"c_first{n}"] = np.tile(np.arange(n, 0, -1, dtype=np.float32)[None, :], (P, 1))
    c["c_token"] = np.ascontiguousarray(np.arange(PADSEQ, dtype=np.float32).reshape(NT, P).T)
    c["c_tokenrow"] = np.arange(PADSEQ, dtype=np.float32)
    half = (np.arange(128) // 16) % 2
    c["c_half"] = np.stack([half == 0, half == 1], 1).astype(np.float32)
    win = np.zeros((128, 47), np.float32)
    win[:64, 15] = 2.0
    win[64:, 31] = 2.0
    c["c_window"] = win
    own = -((np.arange(128)[:, None] // 64) == half[None, :]).astype(np.float32)
    c["c_own"] = np.stack([own, np.where(np.isin(np.arange(128), (111, 127)), 0, own)], 1).astype(np.float32)
    ex = np.zeros((96, 8 * 170), np.float32)
    for k in range(24):
        ex[k, (k % 8) * 170:(k % 8 + 1) * 170] = 1.0
    c["c_expand"] = ex
    return c


def bc(ap, n):
    return ap.unsqueeze(1).to_broadcast([ap.shape[0], n, ap.shape[1]])


def bcl(ap, w):
    return ap.unsqueeze(2).to_broadcast([ap.shape[0], ap.shape[1], w])


class Core:

    def __init__(self, nc, A, ctx):
        self.nc, self.A, self.ctx = nc, A, ctx
        self.ps = ctx.enter_context(nc.psum_tensor("ps", [128, 8, 512], F32))
        self.h = self.sb("h", [P, T, D])
        self.ident = self.sb("ident", [128, 128])
        self.written = nc.alloc_semaphore(name="out_written")
        self.sems = []

    def sb(self, name, shape, dt=F32, ctx=None):
        return (ctx or self.ctx).enter_context(self.nc.sbuf_tensor(name, shape, dt))

    def sem(self, name):
        self.sems.append(self.nc.alloc_semaphore(name=name))
        return self.sems[-1]

    def recycle_semaphores(self):
        with self.nc.Block() as block:
            @block.gpsimd
            def _(pool):
                self.nc.clear_and_free_semaphores(self.sems)
        self.sems = []


def row(ap, n):
    return ap.unsqueeze(0).to_broadcast([n, ap.shape[0]])


def transposes(nc, K, src, rows, cols, done, free=None):
    for g in range(NG):
        if free is not None:
            free(g)
        for j in range(3):
            ins = nc.tensor.transpose(K.ps[0:cols, g, j * rows:(j + 1) * rows], src(3 * g + j),
                                      K.ident[0:rows, 0:rows])
        ins.then_inc(done, 1)


def layernorm_dve(nc, dve, link, x, out, tmp, st, var_ready, std_ready, eps=1e-5):
    w = x.shape[2]
    link(nc.vector.tensor_reduce(st[:, 0, :], x, AX.X, ALU.add))
    link(nc.vector.tensor_scalar(st[:, 0, :], st[:, 0, :], 1.0 / w, None, ALU.mult))
    link(nc.vector.tensor_tensor(out, x, bcl(st[:, 0, :], w), ALU.subtract))
    link(nc.vector.tensor_tensor(tmp, out, out, ALU.mult))
    link(nc.vector.tensor_reduce(st[:, 1, :], tmp, AX.X, ALU.add))
    nc.vector.tensor_scalar(st[:, 1, :], st[:, 1, :], 1.0 / w, eps, ALU.mult, ALU.add).then_inc(var_ready, 1)
    dve.wait_ge(std_ready, 1)
    link(nc.vector.reciprocal(st[:, 3, :], st[:, 2, :]))
    link(nc.vector.tensor_tensor(out, out, bcl(st[:, 3, :], w), ALU.mult))


def root_act(nc, act, st, var_ready, std_ready, n=1):
    act.wait_ge(var_ready, n)
    nc.scalar.activation(st[:, 2, :], st[:, 1, :], ACT.Sqrt).then_inc(std_ready, 1)


def stage_embed(nc, K, A):
    with ExitStack() as ctx:
        sb = lambda n, s: K.sb("em_" + n, s, ctx=ctx)
        sem = lambda n: K.sem("em_" + n)
        W = sb("W", [64, 1152])
        WT = sb("WT", [128, 9, 64])
        id2 = sb("id2", [128, 64])
        dft = sb("dft", [128, 9, 16])
        kron = sb("kron", [128, 9, 16, 64])
        Wc = sb("Wc", [128, 8, 64])
        xs = sb("xs", [128, 2, 68, 64])
        XT = sb("XT", [64, COLS])
        w_in, id_in, x_in, cls_in = sem("w_in"), sem("id_in"), [sem("x_in0"), sem("x_in1")], sem("cls_in")
        wt_ps, wt_sb, kron_ok, wc_ps, wc_sb = sem("wt_ps"), sem("wt_sb"), sem("kron_ok"), sem("wc_ps"), sem("wc_sb")
        emb_ps, emb_sb, tr_ps, h_ok = sem("emb_ps"), sem("emb_sb"), sem("tr_ps"), sem("h_ok")
        ps = K.ps
        x = A["x"]
        with nc.Block() as block:
            @block.sync
            def _(sp):
                sp.dma_start(W[:], A["L0_tok_W"]).then_inc(w_in, 16)
                sp.dma_start(K.ident[:], A["c_ident"]).then_inc(id_in, 16)
                sp.dma_start(id2[:], A["c_ident2"]).then_inc(id_in, 16)
                sp.dma_start(dft[:], A["c_dft"]).then_inc(id_in, 16)
                for b in range(2):
                    v = x[b].rearrange("c (t p) v -> p c t v", p=2)
                    for par in range(2):
                        sp.dma_start(xs[64 * par:64 * par + 64, b, 0:64, :], v[par]).then_inc(x_in[b], 16)
                        sp.dma_start(xs[64 * par:64 * par + 64, b, 64:68, :],
                                     x[b, :, 127:128, :].to_broadcast([64, 4, 64])).then_inc(x_in[b], 16)
                    sp.dma_start(XT[:, b * PADSEQ:b * PADSEQ + 1],
                                 A["cls_tok"][0, 0, :].unsqueeze(1)).then_inc(cls_in, 16)

            @block.vector
            def _(dve):
                dve.wait_ge(id_in, 48)
                for k in range(9):
                    nc.vector.tensor_tensor(kron[:, k], bc(id2[:], 16), bcl(dft[:, k, :], 64),
                                            ALU.mult).then_inc(kron_ok, 1)
                for b in range(2):
                    nc.vector.memset(XT[:, b * PADSEQ + SEQ:(b + 1) * PADSEQ], 0.0).then_inc(emb_sb, 1)
                for q in range(4):
                    dve.wait_ge(emb_ps, q + 1)
                    c0 = (q // 2) * PADSEQ + 1 + 512 * (q % 2)
                    nc.vector.tensor_copy(XT[:, c0:c0 + 512], ps[0:64, 4 + q, :]).then_inc(emb_sb, 1)
                for g in range(NG):
                    dve.wait_ge(tr_ps, g + 1)
                    nc.vector.tensor_copy(K.h[:, 3 * g:3 * g + 3, :].rearrange("p a b -> p (a b)"),
                                          ps[0:P, g, 0:192]).then_inc(h_ok, 1)

            @block.scalar
            def _(act):
                act.wait_ge(wt_ps, 1)
                nc.scalar.copy(WT[:, 0:8, :].rearrange("p a b -> p (a b)"), ps[:, 0, :]).then_inc(wt_sb, 1)
                nc.scalar.copy(WT[:, 8, :], ps[:, 1, 0:64]).then_inc(wt_sb, 1)
                act.wait_ge(wc_ps, 1)
                nc.scalar.copy(Wc[:].rearrange("p a b -> p (a b)"), ps[:, 2, :]).then_inc(wc_sb, 1)

            @block.tensor
            def _(pe):
                pe.wait_ge(w_in, 16)
                pe.wait_ge(id_in, 48)
                for k in range(9):
                    ins = nc.tensor.transpose(ps[:, k // 8, (k % 8) * 64:(k % 8) * 64 + 64],
                                              W[:, k * 128:(k + 1) * 128], K.ident[0:64, 0:64])
                ins.then_inc(wt_ps, 1)
                pe.wait_ge(wt_sb, 2)
                pe.wait_ge(kron_ok, 9)
                for j in range(8):
                    for k in range(9):
                        ins = nc.tensor.matmul(ps[:, 2, j * 64:(j + 1) * 64],
                                               kron[:, k, 2 * j:2 * j + 2, :].rearrange("p a b -> p (a b)"),
                                               WT[:, k, :], start=(k == 0), stop=(k == 8))
                ins.then_inc(wc_ps, 1)
                pe.wait_ge(wc_sb, 1)
                for b in range(2):
                    pe.wait_ge(x_in[b], 64)
                    for half in range(2):
                        for j in range(8):
                            ins = nc.tensor.matmul(
                                ps[0:64, 4 + 2 * b + half, :], Wc[:, j, :],
                                xs[:, b, j:j + 61:4, 32 * half:32 * half + 32].rearrange("p n v -> p v n"),
                                start=(j == 0), stop=(j == 7))
                        ins.then_inc(emb_ps, 1)
                pe.wait_ge(emb_sb, 6)
                pe.wait_ge(cls_in, 32)
                for g in range(NG):
                    for j in range(3):
                        t = 3 * g + j
                        ins = nc.tensor.transpose(ps[0:P, g, j * 64:(j + 1) * 64], XT[:, t * P:(t + 1) * P],
                                                  K.ident[0:64, 0:64])
                    ins.then_inc(tr_ps, 1)


def stage_rwkv(nc, K, A):
    outer = ExitStack()
    with outer:
        sb = lambda n, s: K.sb("rw_" + n, s, ctx=outer)
        TM = sb("TM", [P, T, 384])
        rwkv_projections(nc, K, A, TM)
        QT = sb("QT", [64, T, 4, P])
        Bt = sb("Bt", [P, T, 64])
        Kt = sb("Kt", [P, T, 64])
        Y = sb("Y", [P, T, 128])
        bonus = sb("bonus", [P, T])
        F = sb("F", [64, T])
        rwkv_scaled(nc, K, A, TM, QT, Bt, Kt, Y, bonus, F)
        O = sb("O", [P, T, 64])
        rwkv_chunks(nc, K, A, TM, QT, Bt, Kt, Y, F, O)
        rwkv_output(nc, K, A, TM, O, bonus)


R_, K_, V_, G_, W_, A_ = (slice(64 * i, 64 * i + 64) for i in range(6))


def rwkv_projections(nc, K, A, TM):
    with ExitStack() as ctx:
        sb = lambda n, s: K.sb("rp_" + n, s, ctx=ctx)
        sem = lambda n: K.sem("rp_" + n)
        ps, ident = K.ps, K.ident
        x2 = sb("x2", [P, T, 128])
        tmp = sb("tmp", [P, T, 64])
        st = sb("st", [P, 4, T])
        S = sb("S", [128, 2, PADSEQ + 1])
        mix = sb("mix", [128, 6])
        WA = sb("WA", [128, 512])
        BB = sb("BB", [128, 128])
        BG = sb("BG", [128, 64])
        H1 = sb("H1", [128, COLS])
        H2 = sb("H2", [128, COLS])
        w_in, mix_in, z_ok, wmix = sem("w_in"), sem("mix_in"), sem("zeros"), sem("wmix")
        chain, var_ready, std_ready, x_ready, x_twice = (sem("chain"), sem("var"), sem("std"), sem("x"), sem("x_twice"))
        tr_ps, s_top, s_bot = sem("tr_ps"), sem("s_top"), sem("s_bottom")
        hid_ps, hid_sb, sig_sb = sem("hid_ps"), sem("hid_sb"), sem("sig_sb")
        tm_ps, tm_act, tm_dve = sem("tm_ps"), sem("tm_act"), sem("tm_dve")
        order = ((0, "W_r", 0, 64), (2, "W_k", 64, 64), (3, "W_v", 128, 64), (1, "A_w", 192, 64),
                 (4, "A_a", 256, 64), (5, "A_g", 320, 128))
        with nc.Block() as block:
            @block.sync
            def _(sp):
                for half in range(2):
                    rows = slice(64 * half, 64 * half + 64)
                    for _, name, c, n in order:
                        sp.dma_start(WA[rows, c:c + n], A["L0_attn_" + name]).then_inc(w_in, 16)
                    with nc.allow_non_contiguous_dma(reason="six columns"):
                        sp.dma_start(mix[rows, :], A["L0_attn_x_mix"].rearrange("i d -> d i")).then_inc(mix_in, 16)
                sp.wait_ge(z_ok, 1)
                sp.dma_start(BB[0:64, 0:64], A["L0_attn_B_w"]).then_inc(w_in, 16)
                sp.dma_start(BB[64:128, 64:128], A["L0_attn_B_a"]).then_inc(w_in, 16)
                sp.dma_start(BG[:], A["L0_attn_B_g"]).then_inc(w_in, 16)

            @block.gpsimd
            def _(pool):
                nc.gpsimd.memset(BB[:], 0.0).then_inc(z_ok, 1)
                pool.wait_ge(z_ok, 1)
                nc.gpsimd.memset(S[64:128, :, 0:1], 0.0).then_inc(z_ok, 1)
                pool.wait_ge(z_ok, 2)
                pool.wait_ge(x_ready, 1)
                nc.gpsimd.tensor_copy(x2[:, :, 64:128], x2[:, :, 0:64]).then_inc(x_twice, 1)

            @block.vector
            def _(dve):
                link = Chain(dve, chain)
                layernorm_dve(nc, dve, link, K.h[:], x2[:, :, 0:64], tmp[:], st[:], var_ready, std_ready)
                nc.vector.tensor_copy(st[:, 0, :], st[:, 1, :]).then_inc(x_ready, 1)
                dve.wait_ge(mix_in, 32)
                link(nc.vector.tensor_scalar(mix[0:64, :], mix[0:64, :], -1.0, 1.0, ALU.mult, ALU.add))
                dve.wait_ge(w_in, 240)
                for i, _, c, n in order:
                    nc.vector.tensor_scalar(WA[:, c:c + n], WA[:, c:c + n], mix[:, i:i + 1], None,
                                            ALU.mult).then_inc(wmix, 1)
                for g in range(NG):
                    dve.wait_ge(tr_ps, g + 1)
                    c0 = (g % 3) * GRP + 1
                    nc.vector.tensor_copy(S[64:128, g // 3, c0:c0 + GRP], ps[64:128, g, 0:GRP]).then_inc(s_bot, 1)
                for g in range(NG):
                    dve.wait_ge(hid_ps, 2 * g + 1)
                    nc.vector.tensor_copy(H1[64:128, g * GRP:(g + 1) * GRP],
                                          ps[64:128, (2 * g) % 8, 0:GRP]).then_inc(hid_sb, 1)
                for t in range(1, T, 2):
                    dve.wait_ge(tm_ps, t + 1)
                    nc.vector.tensor_copy(TM[:, t, :], ps[0:P, t % 8, 0:384]).then_inc(tm_dve, 1)

            @block.scalar
            def _(act):
                root_act(nc, act, st[:], var_ready, std_ready)
                for g in range(NG):
                    act.wait_ge(tr_ps, g + 1)
                    nc.scalar.copy(S[0:64, g // 3, (g % 3) * GRP:(g % 3 + 1) * GRP],
                                   ps[0:64, g, 0:GRP]).then_inc(s_top, 1)
                for g in range(NG):
                    cols = slice(g * GRP, (g + 1) * GRP)
                    act.wait_ge(hid_ps, 2 * g + 1)
                    nc.scalar.activation(H1[0:64, cols], ps[0:64, (2 * g) % 8, 0:GRP], ACT.Tanh).then_inc(sig_sb, 1)
                    act.wait_ge(hid_ps, 2 * g + 2)
                    nc.scalar.activation(H2[:, cols], ps[:, (2 * g + 1) % 8, 0:GRP], ACT.Sigmoid).then_inc(sig_sb, 1)
                for t in range(0, T, 2):
                    act.wait_ge(tm_ps, t + 1)
                    nc.scalar.copy(TM[:, t, :], ps[0:P, t % 8, 0:384]).then_inc(tm_act, 1)

            @block.tensor
            def _(pe):
                pe.wait_ge(x_ready, 1)
                pe.wait_ge(x_twice, 1)
                transposes(nc, K, lambda t: x2[:, t, :], P, 128, tr_ps)
                pe.wait_ge(wmix, 6)
                pe.wait_ge(z_ok, 2)
                pe.wait_ge(w_in, 240)
                pe.wait_ge(s_top, NG)
                pe.wait_ge(s_bot, NG)
                for g in range(NG):
                    if g >= 4:
                        pe.wait_ge(hid_sb, g - 3)
                        pe.wait_ge(sig_sb, 2 * g - 6)
                    rhs = S[:, g // 3, (g % 3) * GRP:(g % 3 + 1) * GRP]
                    nc.tensor.matmul(ps[:, (2 * g) % 8, 0:GRP], WA[:, 192:320], rhs,
                                     start=True, stop=True).then_inc(hid_ps, 1)
                    nc.tensor.matmul(ps[:, (2 * g + 1) % 8, 0:GRP], WA[:, 320:448], rhs,
                                     start=True, stop=True).then_inc(hid_ps, 1)
                pe.wait_ge(hid_sb, NG)
                pe.wait_ge(sig_sb, 2 * NG)
                for t in range(T):
                    if t >= 8:
                        if t % 2:
                            pe.wait_ge(tm_dve, (t - 8) // 2 + 1)
                        else:
                            pe.wait_ge(tm_act, (t - 8) // 2 + 1)
                    o = ps[0:P, t % 8, :]
                    c = slice(t * P, (t + 1) * P)
                    i = (t % NT) * P
                    nc.tensor.matmul(o[:, 0:192], S[:, t // NT, i:i + P], WA[:, 0:192], start=True, stop=True)
                    nc.tensor.matmul(o[:, 192:256], H2[:, c], BG[:], start=True, stop=True)
                    nc.tensor.matmul(o[:, 256:384], H1[:, c], BB[:], start=True, stop=True).then_inc(tm_ps, 1)


def rwkv_scaled(nc, K, A, TM, QT, Bt, Kt, Y, bonus, F):
    with ExitStack() as ctx:
        sb = lambda n, s: K.sb("rs_" + n, s, ctx=ctx)
        sem = lambda n: K.sem("rs_" + n)
        ps, ident = K.ps, K.ident
        rows = sb("rows", [P, 5, 64])
        rel = sb("rel", [P, 2, P])
        sums = sb("sums", [P, 2])
        kk = sb("kk", [P, T, 64])
        tmp = sb("tmp", [P, T, 64])
        tmp2 = sb("tmp2", [P, T, 64])
        b_ = sb("b", [P, T, 64])
        Rt = sb("Rt", [P, T, 64])
        KK = sb("KK", [P, T, 64])
        E1 = sb("E1", [P, T, 64])
        E2 = sb("E2", [P, T, 64])
        E3 = sb("E3", [P, T, 64])
        st = sb("st", [P, 4, T])
        lm = sb("lm", [64, T, 2])
        c_in, chain, achain = sem("c_in"), sem("chain"), sem("achain")
        biased, gated, nsq, nroot, logw_ok, cum_ps = (sem("biased"), sem("gated"), sem("nsq"), sem("nroot"),
                                                      sem("logw"), sem("cum_ps"))
        e_ok, scaled, tr_ps, tr_act, tr_dve, lm_ps = (sem("exps"), sem("scaled"), sem("tr_ps"), sem("tr_act"),
                                                      sem("tr_dve"), sem("lm_ps"))
        f_sum, f_ok = sem("f_sum"), sem("f_ok")
        flat = lambda a: a.rearrange("p a b -> p (a b)")
        with nc.Block() as block:
            @block.sync
            def _(sp):
                for i, n in enumerate(("b_w", "b_a", "k_k", "k_a", "r_k")):
                    sp.dma_start(rows[:, i, :], row(A["L0_attn_" + n], P)).then_inc(c_in, 16)
                sp.dma_start(rel[:], A["c_rel"]).then_inc(c_in, 16)
                sp.dma_start(sums[:], A["c_sums"]).then_inc(c_in, 16)

            @block.vector
            def _(dve):
                link = Chain(dve, chain)
                tt, stt = nc.vector.tensor_tensor, nc.vector.scalar_tensor_tensor
                dve.wait_ge(c_in, 112)
                tt(TM[:, :, W_], TM[:, :, W_], bc(rows[:, 0], T), ALU.add).then_inc(biased, 1)
                tt(TM[:, :, A_], TM[:, :, A_], bc(rows[:, 1], T), ALU.add).then_inc(biased, 1)
                link(tt(kk[:], TM[:, :, K_], bc(rows[:, 2], T), ALU.mult))
                link(tt(tmp[:], kk[:], kk[:], ALU.mult))
                nc.vector.tensor_reduce(st[:, 0, :], tmp[:], AX.X, ALU.add).then_inc(nsq, 1)
                dve.wait_ge(gated, 2)
                nc.vector.tensor_scalar(TM[:, :, W_], TM[:, :, W_], DECAY, None, ALU.mult).then_inc(logw_ok, 1)
                dve.wait_ge(nroot, 1)
                link(nc.vector.tensor_scalar(st[:, 1, :], st[:, 1, :], 1e-12, None, ALU.max))
                link(nc.vector.reciprocal(st[:, 2, :], st[:, 1, :]))
                link(tt(kk[:], kk[:], bcl(st[:, 2, :], 64), ALU.mult))
                link(tt(b_[:], kk[:], TM[:, :, A_], ALU.mult))
                link(stt(tmp[:], TM[:, :, A_], -1.0, bc(rows[:, 3], T), ALU.add, ALU.mult))
                link(stt(TM[:, :, K_], tmp[:], 1.0, TM[:, :, K_], ALU.add, ALU.mult))
                link(tt(tmp[:], TM[:, :, K_], bc(rows[:, 4], T), ALU.mult))
                link(tt(tmp2[:], tmp[:], TM[:, :, R_], ALU.mult))
                link(nc.vector.tensor_reduce(bonus[:], tmp2[:], AX.X, ALU.add))
                dve.wait_ge(e_ok, 3)
                tt(KK[:], kk[:], E3[:], ALU.mult).then_inc(scaled, 1)
                tt(Rt[:], TM[:, :, R_], E1[:], ALU.mult).then_inc(scaled, 1)
                tt(Bt[:], b_[:], E2[:], ALU.mult).then_inc(scaled, 1)
                tt(Kt[:], TM[:, :, K_], E2[:], ALU.mult).then_inc(scaled, 1)
                dve.wait_ge(scaled, 4)
                nc.vector.tensor_scalar(Y[:, :, 64:128], KK[:], -1.0, None, ALU.mult)
                dve.wait_ge(lm_ps, 1)
                link(nc.vector.tensor_copy(flat(lm[:]), ps[0:64, 6, 0:2 * T]))
                link(nc.vector.tensor_copy(F[:], lm[:, :, 1]))
                for b in range(2):
                    tt(F[:, b * NT:b * NT + NT - 1], lm[:, b * NT:b * NT + NT - 1, 1],
                       lm[:, b * NT + 1:b * NT + NT, 0], ALU.add).then_inc(f_sum, 1)
                for t in range(1, T, 2):
                    dve.wait_ge(tr_ps, t + 1)
                    nc.vector.tensor_copy(QT[:, t].rearrange("p a b -> p (a b)"),
                                          ps[0:64, t % 4, 0:4 * P]).then_inc(tr_dve, 1)

            @block.scalar
            def _(act):
                act.wait_ge(biased, 2)
                nc.scalar.activation(TM[:, :, W_], TM[:, :, W_], ACT.Sigmoid).then_inc(gated, 1)
                nc.scalar.activation(TM[:, :, A_], TM[:, :, A_], ACT.Sigmoid).then_inc(gated, 1)
                act.wait_ge(nsq, 1)
                nc.scalar.activation(st[:, 1, :], st[:, 0, :], ACT.Sqrt).then_inc(nroot, 1)
                act.wait_ge(cum_ps, 6)
                three = lambda a: flat(a[:]).rearrange("p (a b) -> p a b", a=3)
                nc.scalar.activation(three(E1), ps[0:P, 0:3, 0:384], ACT.Exp).then_inc(e_ok, 1)
                nc.scalar.activation(three(E2), ps[0:P, 0:3, 0:384], ACT.Exp, scale=-1.0).then_inc(e_ok, 1)
                nc.scalar.activation(three(E3), ps[0:P, 3:6, 0:384], ACT.Exp).then_inc(e_ok, 1)
                act.wait_ge(f_sum, 2)
                nc.scalar.activation(F[:], F[:], ACT.Exp).then_inc(f_ok, 1)
                for t in range(0, T, 2):
                    act.wait_ge(tr_ps, t + 1)
                    nc.scalar.copy(QT[:, t].rearrange("p a b -> p (a b)"), ps[0:64, t % 4, 0:4 * P]).then_inc(tr_act, 1)

            @block.tensor
            def _(pe):
                pe.wait_ge(c_in, 112)
                pe.wait_ge(logw_ok, 1)
                for m in range(2):
                    for q in range(3):
                        nc.tensor.matmul(ps[0:P, 3 * m + q, 0:384], rel[:, m, :], TM[:, 6 * q:6 * q + 6, W_],
                                         start=True, stop=True).then_inc(cum_ps, 1)
                for t in range(T):
                    ins = nc.tensor.matmul(ps[0:64, 6, 2 * t:2 * t + 2], TM[:, t, W_], sums[:], start=True, stop=True)
                ins.then_inc(lm_ps, 1)
                pe.wait_ge(scaled, 4)
                for t in range(T):
                    if t >= 4:
                        pe.wait_ge(tr_dve if t % 2 else tr_act, (t - 4) // 2 + 1)
                    for j, src in enumerate((KK, Rt, Bt, Kt)):
                        ins = nc.tensor.transpose(ps[0:64, t % 4, j * P:(j + 1) * P], src[:, t, :], ident[0:P, 0:P])
                    ins.then_inc(tr_ps, 1)


def rwkv_chunks(nc, K, A, TM, QT, Bt, Kt, Y, F, O):
    with ExitStack() as ctx:
        sb = lambda n, s: K.sb("rc_" + n, s, ctx=ctx)
        ps, ident = K.ps, K.ident
        sem = lambda n: K.sem("rc_" + n)
        M4 = sb("M4", [P, T, 4, P])
        XX = sb("XX", [P, T, 2, P])
        mask4 = sb("mask4", [P, 4, P])
        lev = sb("lev", [P, 7, P])
        sub = sb("sub", [P, P])
        NL = sb("NL", [P, 2, T, P])
        T1 = sb("T1", [P, NT, 2, P])
        c_in, qk_ps, qk_sb, x0, nl_ok = sem("c_in"), sem("qk_ps"), sem("qk_sb"), sem("x0"), sem("nl")
        t1_ps, t1_sb, dx_ps, dx_ok, chain = sem("t1_ps"), sem("t1_sb"), sem("dx_ps"), sem("dx"), sem("chain")
        flat = lambda a: a.rearrange("p a b -> p (a b)")
        GRPS = T // 2
        N = len(LEVELS) * GRPS
        with nc.Block() as block:
            @block.sync
            def _(sp):
                sp.dma_start(mask4[:], A["c_mask4"]).then_inc(c_in, 16)
                sp.dma_start(lev[:], A["c_levels"]).then_inc(c_in, 16)
                sp.dma_start(sub[:], A["c_sub"]).then_inc(c_in, 16)

            @block.tensor
            def _(pe):
                for t in range(T):
                    if t >= 4:
                        pe.wait_ge(x0, t - 3)
                    bank = 2 * (t % 4)
                    kr = flat(QT[:, t, 0:2, :])
                    nc.tensor.matmul(ps[0:P, bank, 0:2 * P], QT[:, t, 2, :], kr, start=True, stop=True)
                    nc.tensor.matmul(ps[0:P, bank, 2 * P:4 * P], QT[:, t, 3, :], kr, start=True, stop=True)
                    nc.tensor.matmul(ps[0:P, bank + 1, 0:P], QT[:, t, 0, :], QT[:, t, 2, :],
                                     start=True, stop=True).then_inc(qk_ps, 1)
                pe.wait_ge(x0, T)

                def product(n):
                    g, lvl = n % GRPS, n // GRPS
                    pe.wait_ge(nl_ok, lvl + 1)
                    if lvl:
                        pe.wait_ge(dx_ok, n - GRPS + 1)
                    if n >= 4:
                        pe.wait_ge(t1_sb, n - 3)
                    for j in range(2):
                        ins = nc.tensor.matmul(ps[0:P, n % 4, j * P:(j + 1) * P], NL[:, lvl % 2, 2 * g + j, :],
                                               XX[:, 2 * g + j, 0, :], start=True, stop=True)
                    ins.then_inc(t1_ps, 1)

                def update(n):
                    g = n % GRPS
                    pe.wait_ge(t1_sb, n + 1)
                    if n >= 4:
                        pe.wait_ge(dx_ok, n - 3)
                    for j in range(2):
                        t = 2 * g + j
                        nc.tensor.matmul(ps[0:P, 4 + n % 4, 2 * j * P:(2 * j + 1) * P], XX[:, t, 1, :],
                                         T1[:, g, j, :], start=True, stop=True)
                        ins = nc.tensor.matmul(ps[0:P, 4 + n % 4, (2 * j + 1) * P:(2 * j + 2) * P], T1[:, g, j, :],
                                               XX[:, t, 1, :], start=True, stop=True)
                    ins.then_inc(dx_ps, 1)

                for n in range(N + 2):
                    if n < N:
                        product(n)
                    if n >= 2:
                        update(n - 2)

            @block.vector
            def _(dve):
                link = Chain(dve, chain)
                dve.wait_ge(c_in, 48)
                for t in range(T):
                    dve.wait_ge(qk_ps, t + 1)
                    bank = 2 * (t % 4)
                    link(nc.vector.tensor_tensor(flat(M4[:, t]), ps[0:P, bank, 0:4 * P], flat(mask4[:]), ALU.mult))
                    link(nc.vector.tensor_tensor(XX[:, t, 0, :], ps[0:P, bank + 1, 0:P], sub[:], ALU.mult))
                    link(nc.vector.tensor_tensor(XX[:, t, 1, :], M4[:, t, 0, :], lev[:, 0, :], ALU.mult))
                    nc.vector.tensor_tensor(XX[:, t], XX[:, t], bc(ident[0:P, 0:P], 2), ALU.add).then_inc(x0, 1)
                for n in range(N):
                    g = n % GRPS
                    dve.wait_ge(dx_ps, n + 1)
                    if n >= GRPS:
                        dve.wait_ge(dx_ok, n - GRPS + 1)
                    xx = XX[:, 2 * g:2 * g + 2].rearrange("p a b c -> p (a b c)")
                    nc.vector.tensor_tensor(xx, ps[0:P, 4 + n % 4, 0:4 * P], xx, ALU.add).then_inc(dx_ok, 1)

            @block.scalar
            def _(act):
                for n in range(N):
                    act.wait_ge(t1_ps, n + 1)
                    if n >= GRPS:
                        act.wait_ge(dx_ps, n - GRPS + 1)
                    nc.scalar.copy(flat(T1[:, n % GRPS]), ps[0:P, n % 4, 0:2 * P]).then_inc(t1_sb, 1)

            @block.gpsimd
            def _(pool):
                pool.wait_ge(x0, T)
                pool.wait_ge(c_in, 48)
                for lvl in range(len(LEVELS)):
                    if lvl >= 2:
                        pool.wait_ge(t1_ps, (lvl - 1) * GRPS)
                    nc.gpsimd.tensor_tensor(NL[:, lvl % 2], M4[:, :, 0, :], bc(lev[:, lvl + 1, :], T),
                                            ALU.mult).then_inc(nl_ok, 1)
        UZ = sb("UZ", [P, T, 128])
        GI = sb("GI", [64, T, 64])
        HF = sb("HF", [64, T, 64])
        R2 = sb("R2", [64, T, P])
        M = sb("M", [64, T, 64])
        by_ps, by_sb, uz_ps, uz_sb = sem("bv_ps"), sem("bv_sb"), sem("uz_ps"), sem("uz_sb")
        g_ps, g_sb, m_ps, m_sb, o_ps, o_sb = (sem("g_ps"), sem("g_sb"), sem("m_ps"), sem("m_sb"), sem("o_ps"),
                                              sem("o_sb"))
        with nc.Block() as block:
            @block.tensor
            def _(pe):
                for t in range(T):
                    ins = nc.tensor.matmul(ps[0:P, t // 6, (t % 6) * 64:(t % 6) * 64 + 64], M4[:, t, 2, :],
                                           TM[:, t, V_], start=True, stop=True)
                    if t % 6 == 5:
                        ins.then_inc(by_ps, 1)
                for g in range(NG):
                    pe.wait_ge(by_sb, g // 2 + 1)
                    if g >= 5:
                        pe.wait_ge(uz_sb, g - 4)
                    for t in range(3 * g, 3 * g + 3):
                        ins = nc.tensor.matmul(ps[0:P, 3 + g % 5, (t % 3) * 128:(t % 3) * 128 + 128], XX[:, t, 1, :],
                                               Y[:, t, :], start=True, stop=True)
                    ins.then_inc(uz_ps, 1)
                pe.wait_ge(uz_sb, NG)
                for t in range(T):
                    if t >= 4:
                        pe.wait_ge(g_sb, 3 * (t - 3))
                    o = ps[0:64, t % 4, :]
                    z = UZ[:, t, 64:128]
                    nc.tensor.matmul(o[:, 0:64], z, Bt[:, t, :], start=True, stop=True)
                    nc.tensor.matmul(o[:, 64:128], Bt[:, t, :], UZ[:, t, 0:64], start=True, stop=False)
                    nc.tensor.matmul(o[:, 64:128], Kt[:, t, :], TM[:, t, V_], start=False, stop=True)
                    nc.tensor.matmul(o[:, 128:128 + P], z, M4[:, t, 1, :], start=True, stop=True).then_inc(g_ps, 1)
                for c in range(1, NT - 1):
                    for b in range(2):
                        t = b * NT + c
                        pe.wait_ge(m_sb, 2 * c + b - 1)
                        pe.wait_ge(g_sb, 3 * T)
                        nc.tensor.matmul(ps[0:64, 4 + b, 0:64], GI[:, t, :], M[:, t, :],
                                         start=True, stop=True).then_inc(m_ps, 1)
                pe.wait_ge(m_sb, 2 * (NT - 1))
                for g in range(NG):
                    for t in range(3 * g, 3 * g + 3):
                        o = ps[0:P, g, (t % 3) * 64:(t % 3) * 64 + 64]
                        nc.tensor.matmul(o, M4[:, t, 1, :], UZ[:, t, 0:64], start=True, stop=False)
                        ins = nc.tensor.matmul(o, M4[:, t, 3, :], TM[:, t, V_], start=False, stop=(t % NT == 0))
                        if t % NT:
                            ins = nc.tensor.matmul(o, R2[:, t, :], M[:, t, :], start=False, stop=True)
                    ins.then_inc(o_ps, 1)

            @block.scalar
            def _(act):
                for q in range(3):
                    act.wait_ge(by_ps, q + 1)
                    nc.scalar.copy(Y[:, 6 * q:6 * q + 6, 0:64],
                                   ps[0:P, q, 0:384].rearrange("p (a b) -> p a b", a=6)).then_inc(by_sb, 1)
                for g in range(NG):
                    act.wait_ge(uz_ps, g + 1)
                    nc.scalar.copy(flat(UZ[:, 3 * g:3 * g + 3, :]), ps[0:P, 3 + g % 5, 0:384]).then_inc(uz_sb, 1)
                for g in range(NG):
                    act.wait_ge(o_ps, g + 1)
                    nc.scalar.copy(flat(O[:, 3 * g:3 * g + 3, :]), ps[0:P, g, 0:192]).then_inc(o_sb, 1)

            @block.vector
            def _(dve):
                for t in range(T):
                    dve.wait_ge(g_ps, t + 1)
                    o = ps[0:64, t % 4, :]
                    nc.vector.tensor_tensor(GI[:, t, :], o[:, 0:64], ident[0:64, 0:64], ALU.add).then_inc(g_sb, 1)
                    nc.vector.tensor_scalar(HF[:, t, :], o[:, 64:128], F[:, t:t + 1], None, ALU.mult).then_inc(g_sb, 1)
                    nc.vector.tensor_tensor(R2[:, t, :], o[:, 128:128 + P], QT[:, t, 1, :], ALU.add).then_inc(g_sb, 1)
                dve.wait_ge(g_sb, 3 * T)
                for b in range(2):
                    nc.vector.tensor_copy(M[:, b * NT + 1, :], HF[:, b * NT, :]).then_inc(m_sb, 1)
                for c in range(1, NT - 1):
                    for b in range(2):
                        t = b * NT + c
                        dve.wait_ge(m_ps, 2 * c + b - 1)
                        nc.vector.scalar_tensor_tensor(M[:, t + 1, :], ps[0:64, 4 + b, 0:64], F[:, t:t + 1],
                                                       HF[:, t, :], ALU.mult, ALU.add).then_inc(m_sb, 1)


def rwkv_output(nc, K, A, TM, O, bonus):
    with ExitStack() as ctx:
        sb = lambda n, s: K.sb("ro_" + n, s, ctx=ctx)
        sem = lambda n: K.sem("ro_" + n)
        ps = K.ps
        tmp = sb("tmp", [P, T, 64])
        on = sb("on", [P, T, 64])
        st = sb("st", [P, 4, T])
        gn = sb("gn", [P, 2, 64])
        Wo = sb("Wo", [64, 64])
        OT = sb("OT", [64, COLS])
        c_in, chain, var_ready, std_ready = sem("c_in"), sem("chain"), sem("var"), sem("std")
        o_ok, tr_ps, tr_sb, y_ps = sem("o_ok"), sem("tr_ps"), sem("tr_sb"), sem("y_ps")
        with nc.Block() as block:
            @block.sync
            def _(sp):
                sp.dma_start(gn[:, 0, :], row(A["L0_attn_gn_w"], P)).then_inc(c_in, 16)
                sp.dma_start(gn[:, 1, :], row(A["L0_attn_gn_b"], P)).then_inc(c_in, 16)
                sp.dma_start(Wo[:], A["L0_attn_W_o"]).then_inc(c_in, 16)

            @block.vector
            def _(dve):
                link = Chain(dve, chain)
                tt = nc.vector.tensor_tensor
                layernorm_dve(nc, dve, link, O[:], on[:], tmp[:], st[:], var_ready, std_ready, eps=64e-5)
                dve.wait_ge(c_in, 48)
                link(tt(on[:], on[:], bc(gn[:, 0], T), ALU.mult))
                link(tt(on[:], on[:], bc(gn[:, 1], T), ALU.add))
                link(tt(tmp[:], TM[:, :, V_], bcl(bonus[:], 64), ALU.mult))
                link(tt(on[:], on[:], tmp[:], ALU.add))
                tt(on[:], on[:], TM[:, :, G_], ALU.mult).then_inc(o_ok, 1)
                for g in range(NG):
                    dve.wait_ge(y_ps, g + 1)
                    hh = K.h[:, 3 * g:3 * g + 3, :].rearrange("p a b -> p (a b)")
                    tt(hh, ps[0:P, g, 0:192], hh, ALU.add)

            @block.scalar
            def _(act):
                root_act(nc, act, st[:], var_ready, std_ready)
                for g in range(NG):
                    act.wait_ge(tr_ps, g + 1)
                    nc.scalar.copy(OT[:, g * GRP:(g + 1) * GRP], ps[0:64, g, 0:GRP]).then_inc(tr_sb, 1)

            @block.tensor
            def _(pe):
                pe.wait_ge(o_ok, 1)
                transposes(nc, K, lambda t: on[:, t, :], P, 64, tr_ps)
                pe.wait_ge(c_in, 48)
                for g in range(NG):
                    pe.wait_ge(tr_sb, g + 1)
                    for j in range(3):
                        t = 3 * g + j
                        ins = nc.tensor.matmul(ps[0:P, g, j * 64:(j + 1) * 64], OT[:, t * P:(t + 1) * P], Wo[:],
                                               start=True, stop=True)
                    ins.then_inc(y_ps, 1)


def stage_depths(nc, K, A):
    KEEP = SEQ // 2 - 1
    with ExitStack() as ctx:
        sb = lambda n, s: K.sb("md_" + n, s, ctx=ctx)
        sem = lambda n: K.sem("md_" + n)
        ps = K.ps
        xn, tmp, st = sb("xn", [P, T, 64]), sb("tmp", [P, T, 64]), sb("st", [P, 4, T])
        wr = sb("wr", [P, 64])
        br = sb("br", [P, 1])
        before = sb("before", [P, P])
        w1, w2 = sb("w1", [64, 256]), sb("w2", [128, 2, 64])
        b1, b2, ones = sb("b1", [128, 2]), sb("b2", [1, 64]), sb("ones", [1, P])
        wc = sb("wc", [P, T])
        wrow = sb("wrow", [P, B, PADSEQ])
        cnt = sb("cnt", [P, 3, T])
        junk = sb("junk", [P, 3, PADSEQ])
        XT = sb("XT", [64, COLS])
        HT = sb("HT", [128, 2, COLS])
        c_in, chain, var_ready, std_ready = sem("c_in"), sem("chain"), sem("var"), sem("std")
        x_ok, w_ok, tr_ps, tr_sb, row_ps, row_sb = (sem("x_ok"), sem("w_ok"), sem("tr_ps"), sem("tr_sb"),
                                                    sem("row_ps"), sem("row_sb"))
        hid_ps, hid_sb, y_ps, y_sb = sem("hid_ps"), sem("hid_sb"), sem("y_ps"), sem("y_sb")
        with nc.Block() as block:
            @block.sync
            def _(sp):
                sp.dma_start(wr[:], row(A["L0_ffn_wr"].rearrange("d o -> (d o)"), P)).then_inc(c_in, 16)
                sp.dma_start(br[:], row(A["L0_ffn_br"], P)).then_inc(c_in, 16)
                sp.dma_start(before[:], A["c_before"]).then_inc(c_in, 16)
                sp.dma_start(w1[:], A["L0_ffn_w1"]).then_inc(c_in, 16)
                sp.dma_start(w2[:], A["L0_ffn_w2"].rearrange("(k p) d -> p k d", p=128)).then_inc(c_in, 16)
                with nc.allow_non_contiguous_dma(reason="two columns"):
                    sp.dma_start(b1[:], A["L0_ffn_b1"].rearrange("(k p) -> p k", p=128)).then_inc(c_in, 16)
                sp.dma_start(b2[:], row(A["L0_ffn_b2"], 1)).then_inc(c_in, 16)

            @block.vector
            def _(dve):
                link = Chain(dve, chain)
                tt = nc.vector.tensor_tensor
                link(nc.vector.memset(ones[:], 1.0))
                link(nc.vector.memset(cnt[:], 0.0))
                layernorm_dve(nc, dve, link, K.h[:], xn[:], tmp[:], st[:], var_ready, std_ready)
                dve.wait_ge(c_in, 112)
                nc.vector.tensor_copy(st[:, 0, :], st[:, 3, :]).then_inc(x_ok, 1)
                tt(K.h[:], K.h[:], xn[:], ALU.add)
                link(tt(tmp[:], xn[:], bc(wr[:], T), ALU.mult))
                link(nc.vector.tensor_reduce(wc[:], tmp[:], AX.X, ALU.add))
                nc.vector.tensor_scalar(wc[:], wc[:], br[:, 0:1], None, ALU.add).then_inc(w_ok, 1)
                dve.wait_ge(w_ok, 1)
                dve.wait_ge(row_sb, 2)
                link(nc.vector.memset(wrow[:, :, SEQ:PADSEQ], -3e38))
                for t in range(T):
                    b, i = t // NT, t % NT
                    c = i * P
                    if i:
                        nc.vector.tensor_scalar(junk[:, 0, 0:c], wrow[:, b, 0:c], wc[:, t:t + 1], None, ALU.is_ge,
                                                ALU.add, accum_out=cnt[:, 0, t:t + 1])
                    nc.vector.tensor_scalar(junk[:, 1, c:PADSEQ], wrow[:, b, c:PADSEQ], wc[:, t:t + 1], None,
                                            ALU.is_gt, ALU.add, accum_out=cnt[:, 1, t:t + 1])
                    link(nc.vector.scalar_tensor_tensor(junk[:, 2, 0:P], wrow[:, b, c:c + P], wc[:, t:t + 1],
                                                        before[:], ALU.is_equal, ALU.mult,
                                                        accum_out=cnt[:, 2, t:t + 1]))
                link(tt(cnt[:, 0], cnt[:, 0], cnt[:, 1], ALU.add))
                link(tt(cnt[:, 0], cnt[:, 0], cnt[:, 2], ALU.add))
                link(nc.vector.tensor_scalar(cnt[:, 0], cnt[:, 0], float(KEEP), None, ALU.is_lt))
                link(tt(wc[:], wc[:], cnt[:, 0], ALU.mult))
                for g in range(NG):
                    dve.wait_ge(y_ps, g + 1)
                    s = slice(3 * g, 3 * g + 3)
                    link(tt(tmp[:, s], ps[0:P, g, 0:192].rearrange("p (a b) -> p a b", a=3), bcl(wc[:, s], 64),
                            ALU.mult))
                    tt(K.h[:, s], K.h[:, s], tmp[:, s], ALU.add)

            @block.scalar
            def _(act):
                root_act(nc, act, st[:], var_ready, std_ready)
                for g in range(NG):
                    act.wait_ge(tr_ps, g + 1)
                    nc.scalar.copy(XT[:, g * GRP:(g + 1) * GRP], ps[0:64, g, 0:GRP]).then_inc(tr_sb, 1)
                for b in range(B):
                    act.wait_ge(row_ps, 3 * b + 3)
                    nc.scalar.copy(wrow[:, b].rearrange("p (a c) -> p a c", a=3),
                                   ps[0:P, 3 * b:3 * b + 3, 0:GRP]).then_inc(row_sb, 1)
                for n in range(2 * NG):
                    act.wait_ge(hid_ps, n + 1)
                    nc.scalar.activation(HT[:, n % 2, (n // 2) * GRP:(n // 2 + 1) * GRP], ps[:, n % 8, 0:GRP],
                                         ACT.Gelu_apprx_tanh, bias=b1[:, n % 2:n % 2 + 1]).then_inc(hid_sb, 1)

            @block.tensor
            def _(pe):
                pe.wait_ge(x_ok, 1)
                transposes(nc, K, lambda t: xn[:, t, :], P, 64, tr_ps)
                pe.wait_ge(w_ok, 1)
                transposes(nc, K, lambda t: wc[:, t:t + 1].to_broadcast([P, P]), P, P, row_ps,
                           free=lambda g: pe.wait_ge(tr_sb, g + 1))
                pe.wait_ge(row_sb, 2)
                pe.wait_ge(c_in, 112)
                for n in range(2 * NG):
                    if n >= 8:
                        pe.wait_ge(hid_sb, n - 7)
                    nc.tensor.matmul(ps[:, n % 8, 0:GRP], w1[:, (n % 2) * 128:(n % 2) * 128 + 128],
                                     XT[:, (n // 2) * GRP:(n // 2 + 1) * GRP], start=True, stop=True).then_inc(hid_ps, 1)
                pe.wait_ge(hid_sb, 2 * NG)
                for g in range(NG):
                    for j in range(3):
                        c = slice((3 * g + j) * P, (3 * g + j + 1) * P)
                        o = ps[0:P, g, j * 64:(j + 1) * 64]
                        nc.tensor.matmul(o, HT[:, 0, c], w2[:, 0], start=True, stop=False)
                        nc.tensor.matmul(o, HT[:, 1, c], w2[:, 1], start=False, stop=False)
                        ins = nc.tensor.matmul(o, ones[:], b2[:], start=False, stop=True)
                    ins.then_inc(y_ps, 1)


def stage_linear(nc, K, A):
    H = 8
    with ExitStack() as ctx:
        sb = lambda n, s: K.sb("la_" + n, s, ctx=ctx)
        sem = lambda n: K.sem("la_" + n)
        ps = K.ps
        xn, tmp, st = sb("xn", [P, T, 64]), sb("tmp", [P, T, 64]), sb("st", [P, 4, T])
        Win = sb("Win", [64, 3, 64])
        WT = sb("WT", [65, 192])
        XT = sb("XT", [65, COLS])
        qkv = sb("qkv", [P, NT, 3, H, B, 8])
        blk = sb("blk", [P, NT, 3, 128])
        ones = sb("ones", [P, 1])
        rmask = sb("rmask", [P, 1])
        bmask = sb("bmask", [128, 128])
        kmax = sb("kmax", [128, 4])
        qs = sb("qs", [P, 3, NT * H])
        v1 = sb("v1", [P, NT, 129])
        rsum = sb("rsum", [128, 1])
        cx = sb("cx", [128, B, H, 8])
        qT = sb("qT", [128, PADSEQ])
        scratch = nc.dram_tensor("la_scratch", [3, PADSEQ * H, 16], F32, kind="Internal").ap()
        c_in, chain, var_ready, std_ready = sem("c_in"), sem("chain"), sem("var"), sem("std")
        x_ok, wt_ps, wt_sb, tr_ps, tr_sb = sem("x_ok"), sem("wt_ps"), sem("wt_sb"), sem("tr_ps"), sem("tr_sb")
        qkv_ps, qkv_sb, stored, loaded = sem("qkv_ps"), sem("qkv_sb"), sem("stored"), sem("loaded")
        kt_ps, km_ok, km_ps, kd_ok, ke_ok, k_ok = (sem("kt_ps"), sem("km_ok"), sem("km_ps"), sem("kd_ok"),
                                                   sem("ke_ok"), sem("k_ok"))
        qd_ok, qe_ok, q_ok, cx_ps, cx_ok = sem("qd_ok"), sem("qe_ok"), sem("q_ok"), sem("cx_ps"), sem("cx_ok")
        qt_ps, qt_sb, o_ps, ones_ok = sem("qt_ps"), sem("qt_sb"), sem("o_ps"), sem("ones_ok")
        with nc.Block() as block:
            @block.sync
            def _(sp):
                for i, n in enumerate("qkv"):
                    sp.dma_start(Win[:, i], A["L1_attn_W" + n]).then_inc(c_in, 16)
                    sp.dma_start(WT[64:65, 64 * i:64 * i + 64], row(A["L1_attn_b" + n], 1)).then_inc(c_in, 16)
                sp.dma_start(rmask[:], A["c_rowmask"]).then_inc(c_in, 16)
                sp.dma_start(bmask[:], A["c_block16"]).then_inc(c_in, 16)
                sp.wait_ge(qkv_sb, T)
                for a in range(3):
                    sp.dma_start(scratch[a].rearrange("(i p h) e -> p i (h e)", p=P, h=H),
                                 qkv[:, :, a].rearrange("p i h b e -> p i (h b e)")).then_inc(stored, 16)
                sp.wait_ge(stored, 48)
                for a in (1, 0, 2):
                    for g in range(H):
                        sp.dma_start(blk[:, :, a, 16 * g:16 * g + 16],
                                     scratch[a, SEQ * g:SEQ * g + PADSEQ].rearrange("(i p) e -> p i e", p=P)
                                     ).then_inc(loaded, 16)

            @block.gpsimd
            def _(pool):
                nc.gpsimd.memset(XT[64:65, :], 1.0).then_inc(ones_ok, 1)

            @block.vector
            def _(dve):
                link = Chain(dve, chain)
                tt = nc.vector.tensor_tensor
                nc.vector.memset(ones[:], 1.0)
                layernorm_dve(nc, dve, link, K.h[:], xn[:], tmp[:], st[:], var_ready, std_ready)
                nc.vector.tensor_copy(st[:, 0, :], st[:, 3, :]).then_inc(x_ok, 1)
                dve.wait_ge(loaded, 3 * H * 16)
                dve.wait_ge(c_in, 128)
                link(nc.vector.memset(v1[:, :, 128:129], 1.0))
                link(nc.vector.tensor_copy(v1[:, :, 0:128], blk[:, :, 2]))
                dve.wait_ge(kt_ps, 3)
                link(nc.vector.tensor_reduce(kmax[:, 0:2], ps[:, 0:2, 0:GRP], AX.X, ALU.max))
                link(nc.vector.tensor_reduce(kmax[:, 2:3], ps[:, 2, 0:GRP - 1], AX.X, ALU.max))
                nc.vector.tensor_reduce(kmax[:, 3:4], kmax[:, 0:3], AX.X, ALU.max).then_inc(km_ok, 1)
                q4 = blk[:, :, 0].rearrange("p i (g e) -> p i g e", g=H)
                q3 = [blk[:, i, 0].rearrange("p (g e) -> p g e", g=H) for i in range(NT)]
                link(nc.vector.tensor_reduce(qs[:, 0].rearrange("p (i g) -> p i g", g=H), q4, AX.X, ALU.max))
                for i in range(NT):
                    ins = tt(q3[i], q3[i], bcl(qs[:, 0, H * i:H * i + H], 16), ALU.subtract)
                ins.then_inc(qd_ok, 1)
                dve.wait_ge(km_ps, 1)
                tt(blk[:, :, 1], blk[:, :, 1], bc(ps[0:P, 3, 0:128], NT), ALU.subtract).then_inc(kd_ok, 1)
                dve.wait_ge(qe_ok, 1)
                link(nc.vector.tensor_reduce(qs[:, 1].rearrange("p (i g) -> p i g", g=H), q4, AX.X, ALU.add))
                link(nc.vector.reciprocal(qs[:, 2], qs[:, 1]))
                for i in range(NT):
                    ins = tt(q3[i], q3[i], bcl(qs[:, 2, H * i:H * i + H], 16), ALU.mult)
                ins.then_inc(q_ok, 1)
                dve.wait_ge(ke_ok, 1)
                nc.vector.tensor_scalar(blk[:, NT - 1, 1], blk[:, NT - 1, 1], rmask[:, 0:1], None,
                                        ALU.mult).then_inc(k_ok, 1)
                dve.wait_ge(cx_ps, 1)
                link(nc.vector.reciprocal(rsum[:], ps[:, 4, 128:129]))
                link(nc.vector.tensor_scalar(rsum[:], rsum[:], 4.0, None, ALU.mult))
                for b in range(B):
                    src = ps[:, 4, 0:128].rearrange("p (g b e) -> p b g e", g=H, b=B)[:, b]
                    nc.vector.scalar_tensor_tensor(cx[:, b], src, rsum[:, 0:1],
                                                   bmask[:].rearrange("p (g b e) -> p b g e", g=H, b=B)[:, b],
                                                   ALU.mult, ALU.mult).then_inc(cx_ok, 1)
                for g in range(3):
                    dve.wait_ge(o_ps, g + 1)
                    for b in range(B):
                        hh = K.h[:, b * NT + 3 * g:b * NT + 3 * g + 3, :]
                        tt(hh, ps[0:P, 5 + g, 0:384].rearrange("p (i b e) -> p b i e", i=3, b=B)[:, b], hh, ALU.add)

            @block.scalar
            def _(act):
                root_act(nc, act, st[:], var_ready, std_ready)
                act.wait_ge(wt_ps, 1)
                nc.scalar.copy(WT[0:64, :], ps[0:64, 7, 0:192]).then_inc(wt_sb, 1)
                for g in range(NG):
                    act.wait_ge(tr_ps, g + 1)
                    nc.scalar.copy(XT[0:64, g * GRP:(g + 1) * GRP], ps[0:64, g, 0:GRP]).then_inc(tr_sb, 1)
                for t in range(T):
                    act.wait_ge(qkv_ps, t + 1)
                    for a in range(3):
                        ins = nc.scalar.copy(qkv[:, t % NT, a, :, t // NT],
                                             ps[0:P, t % 8, 64 * a:64 * a + 64].rearrange("p (h e) -> p h e", h=H))
                    ins.then_inc(qkv_sb, 1)
                act.wait_ge(qd_ok, 1)
                nc.scalar.activation(blk[:, :, 0], blk[:, :, 0], ACT.Exp).then_inc(qe_ok, 1)
                act.wait_ge(kd_ok, 1)
                nc.scalar.activation(blk[:, :, 1], blk[:, :, 1], ACT.Exp).then_inc(ke_ok, 1)
                for g in range(3):
                    act.wait_ge(qt_ps, g + 1)
                    nc.scalar.copy(qT[:, g * GRP:(g + 1) * GRP], ps[:, g, 0:GRP]).then_inc(qt_sb, 1)

            @block.tensor
            def _(pe):
                pe.wait_ge(c_in, 128)
                for i in range(3):
                    ins = nc.tensor.transpose(ps[0:64, 7, 64 * i:64 * i + 64], Win[:, i], K.ident[0:64, 0:64])
                ins.then_inc(wt_ps, 1)
                pe.wait_ge(x_ok, 1)
                transposes(nc, K, lambda t: xn[:, t, :], P, 64, tr_ps)
                pe.wait_ge(tr_sb, NG)
                pe.wait_ge(wt_sb, 1)
                pe.wait_ge(ones_ok, 1)
                for t in range(T):
                    if t >= 8:
                        pe.wait_ge(qkv_sb, t - 7)
                    nc.tensor.matmul(ps[0:P, t % 8, 0:192], XT[:, t * P:(t + 1) * P], WT[:],
                                     start=True, stop=True).then_inc(qkv_ps, 1)
                pe.wait_ge(qkv_sb, T)
                pe.wait_ge(loaded, 3 * H * 16)

                def nine(a, done):
                    for i in range(NT):
                        ins = nc.tensor.transpose(ps[:, i // 3, (i % 3) * P:(i % 3 + 1) * P], blk[:, i, a, :],
                                                  K.ident[0:P, 0:P])
                        if i % 3 == 2:
                            ins.then_inc(done, 1)

                nine(1, kt_ps)
                pe.wait_ge(km_ok, 1)
                nc.tensor.transpose(ps[0:P, 3, 0:128], kmax[:, 3:4].to_broadcast([128, P]),
                                    K.ident[:]).then_inc(km_ps, 1)
                pe.wait_ge(q_ok, 1)
                nine(0, qt_ps)
                pe.wait_ge(k_ok, 1)
                for i in range(NT):
                    ins = nc.tensor.matmul(ps[:, 4, 0:129], blk[:, i, 1, :], v1[:, i, :], start=(i == 0),
                                           stop=(i == NT - 1))
                ins.then_inc(cx_ps, 1)
                pe.wait_ge(qt_sb, 3)
                pe.wait_ge(cx_ok, B)
                for g in range(3):
                    for i in range(3 * g, 3 * g + 3):
                        ins = nc.tensor.matmul(ps[0:P, 5 + g, (i % 3) * 128:(i % 3) * 128 + 128],
                                               qT[:, i * P:(i + 1) * P], cx[:].rearrange("p b g e -> p (b g e)"),
                                               start=True, stop=True)
                    ins.then_inc(o_ps, 1)


def rms_dve(nc, dve, link, x, out, tmp, st, wrow, var_ready, std_ready, eps=1e-6):
    link(nc.vector.tensor_tensor(tmp, x, x, ALU.mult))
    link(nc.vector.tensor_reduce(st[:, 1, :], tmp, AX.X, ALU.add))
    nc.vector.tensor_scalar(st[:, 1, :], st[:, 1, :], 1.0 / 64, eps, ALU.mult, ALU.add).then_inc(var_ready, 1)
    dve.wait_ge(std_ready, 1)
    link(nc.vector.reciprocal(st[:, 3, :], st[:, 2, :]))
    link(nc.vector.tensor_tensor(out, x, bcl(st[:, 3, :], 64), ALU.mult))
    link(nc.vector.tensor_tensor(out, out, bc(wrow, T), ALU.mult))


def stage_gqa(nc, K, A):
    with ExitStack() as ctx:
        x2 = K.sb("gq_x", [P, T, 64], ctx=ctx)
        gqa_attention(nc, K, A, x2)
        moe_top2(nc, K, A, x2)


def split3(nc, link, src, hi, mid, lo, tmp):
    link(nc.vector.tensor_copy(hi, src))
    link(nc.vector.tensor_tensor(tmp, src, hi, ALU.subtract))
    link(nc.vector.tensor_copy(mid, tmp))
    link(nc.vector.tensor_tensor(tmp, tmp, mid, ALU.subtract))
    link(nc.vector.tensor_copy(lo, tmp))


PARTS = ((0, 0), (0, 1), (1, 0), (1, 1), (0, 2), (2, 0))


def gqa_attention(nc, K, A, x2):
    with ExitStack() as ctx:
        QT = K.sb("gq_QT", [99, 4, COLS], BF16, ctx=ctx)
        KT = K.sb("gq_KT", [99, 2, COLS], BF16, ctx=ctx)
        V1 = K.sb("gq_V1", [P, T, 2, 32], ctx=ctx)
        WoT = K.sb("gq_WoT", [64, 64], ctx=ctx)
        with ExitStack() as inner:
            Q6 = K.sb("gq_Q6", [P, T, 4, 99], BF16, ctx=inner)
            gqa_prepare(nc, K, A, x2, Q6, QT, KT, V1, WoT)
            gqa_maxima(nc, K, A, Q6, QT, KT)
        gqa_attend(nc, K, A, QT, KT, V1, WoT, x2)


def gqa_prepare(nc, K, A, x2, Q6, QT, KT, V1, WoT):
    with ExitStack() as ctx:
        sb = lambda n, s, dt=F32: K.sb("ga_" + n, s, dt, ctx=ctx)
        sem = lambda n: K.sem("ga_" + n)
        ps = K.ps
        xh, tmp, st, st2 = sb("xh", [P, T, 64]), sb("tmp", [P, T, 64]), sb("st", [P, 4, T]), sb("st2", [P, 4, T])
        lnw = sb("lnw", [P, 64])
        Win = sb("Win", [128, 64])
        wo = sb("wo", [64, 64])
        WT = sb("WT", [64, 128])
        XT = sb("XT", [64, COLS])
        qkv = sb("qkv", [P, T, 128])
        rope = sb("rope", [P, 2, NT, 16])
        rot = sb("rot", [P, T, 96])
        part = sb("part", [P, 3, T, 96], BF16)
        K6 = sb("K6", [P, T, 2, 99], BF16)
        identb = sb("identb", [P, P], BF16)
        c_in, chain, var_ready, std_ready = sem("c_in"), sem("chain"), sem("var"), sem("std")
        x_ok, wt_ps, wt_sb, tr_ps, tr_sb = sem("x_ok"), sem("wt_ps"), sem("wt_sb"), sem("tr_ps"), sem("tr_sb")
        qkv_ps, qkv_sb, z_ok, q6_ok, k6_ok, t_ps, t_act, t_dve = (
            sem("qkv_ps"), sem("qkv_sb"), sem("zeros"), sem("q6_ok"), sem("k6_ok"), sem("t_ps"), sem("t_act"),
            sem("t_dve"))
        NTR = 6 * NG
        with nc.Block() as block:
            @block.sync
            def _(sp):
                sp.dma_start(lnw[:], row(A["L1_ffn_ln1_w"], P)).then_inc(c_in, 16)
                sp.dma_start(Win[0:64], A["L1_ffn_wq"]).then_inc(c_in, 16)
                sp.dma_start(Win[64:96], A["L1_ffn_wk"]).then_inc(c_in, 16)
                sp.dma_start(Win[96:128], A["L1_ffn_wv"]).then_inc(c_in, 16)
                sp.dma_start(wo[:], A["L1_ffn_wo"]).then_inc(c_in, 16)
                sp.dma_start(rope[:], A["c_rope"]).then_inc(c_in, 16)

            @block.gpsimd
            def _(pool):
                nc.gpsimd.memset(K6[:, :, :, 96:99], 1.0).then_inc(z_ok, 1)
                pool.wait_ge(z_ok, 1)
                nc.gpsimd.memset(Q6[:, :, :, 96:99], 0.0).then_inc(z_ok, 1)
                pool.wait_ge(z_ok, 2)
                nc.gpsimd.memset(V1[:], 1.0).then_inc(z_ok, 1)

            @block.vector
            def _(dve):
                link = Chain(dve, chain)
                tt = nc.vector.tensor_tensor
                link(nc.vector.tensor_copy(identb[:], K.ident[0:P, 0:P]))
                layernorm_dve(nc, dve, link, K.h[:], x2[:], tmp[:], st[:], var_ready, std_ready)
                dve.wait_ge(c_in, 96)
                link(tt(tmp[:], x2[:], x2[:], ALU.mult))
                link(nc.vector.tensor_reduce(st2[:, 1, :], tmp[:], AX.X, ALU.add))
                nc.vector.tensor_scalar(st2[:, 1, :], st2[:, 1, :], 1.0 / 64, 1e-6, ALU.mult,
                                        ALU.add).then_inc(var_ready, 1)
                dve.wait_ge(std_ready, 2)
                link(nc.vector.reciprocal(st2[:, 3, :], st2[:, 2, :]))
                link(tt(xh[:], x2[:], bcl(st2[:, 3, :], 64), ALU.mult))
                tt(xh[:], xh[:], bc(lnw[:], T), ALU.mult).then_inc(x_ok, 1)
                dve.wait_ge(qkv_sb, T)
                for b in range(B):
                    s = slice(b * NT, b * NT + NT)
                    six = qkv[:, s, 0:96].rearrange("p i (h e) -> p i h e", h=6)
                    rt = rot[:, s].rearrange("p i (h e) -> p i h e", h=6)
                    hb = lambda a: a.unsqueeze(2).to_broadcast([P, NT, 6, a.shape[2]])
                    tt(rt[:, :, :, 0:8], six[:, :, :, 8:16], hb(rope[:, 1, :, 0:8]), ALU.mult)
                    link(tt(rt[:, :, :, 8:16], six[:, :, :, 0:8], hb(rope[:, 1, :, 8:16]), ALU.mult))
                    link(tt(six, six, hb(rope[:, 0]), ALU.mult))
                    link(tt(six, six, rt, ALU.add))
                split3(nc, link, qkv[:, :, 0:96], part[:, 0], part[:, 1], part[:, 2], rot[:])
                dve.wait_ge(z_ok, 3)
                for k, (a, b) in enumerate(PARTS):
                    nc.vector.tensor_copy(Q6[:, :, :, 16 * k:16 * k + 16],
                                          part[:, a, :, 0:64].rearrange("p t (h e) -> p t h e", h=4)).then_inc(q6_ok, 1)
                for k, (a, b) in enumerate(PARTS):
                    nc.vector.tensor_copy(K6[:, :, :, 16 * k:16 * k + 16],
                                          part[:, b, :, 64:96].rearrange("p t (h e) -> p t h e", h=2)).then_inc(k6_ok, 1)
                nc.vector.tensor_copy(V1[:, :, :, 0:16], qkv[:, :, 96:128].rearrange("p t (h e) -> p t h e", h=2))
                for n in range(1, NTR, 2):
                    dst = QT[:, n // NG] if n < 4 * NG else KT[:, n // NG - 4]
                    c = n % NG * GRP
                    dve.wait_ge(t_ps, n + 1)
                    nc.vector.tensor_copy(dst[:, c:c + GRP], ps[0:99, n % 8, :].bitcast(BF16)[:, 0:GRP]
                                          ).then_inc(t_dve, 1)

            @block.scalar
            def _(act):
                root_act(nc, act, st[:], var_ready, std_ready)
                root_act(nc, act, st2[:], var_ready, std_ready, n=2)
                act.wait_ge(wt_ps, 1)
                nc.scalar.copy(WT[:], ps[0:64, 7, 0:128]).then_inc(wt_sb, 1)
                nc.scalar.copy(WoT[:], ps[0:64, 7, 128:192]).then_inc(wt_sb, 1)
                for g in range(NG):
                    act.wait_ge(tr_ps, g + 1)
                    nc.scalar.copy(XT[:, g * GRP:(g + 1) * GRP], ps[0:64, g, 0:GRP]).then_inc(tr_sb, 1)
                for t in range(T):
                    act.wait_ge(qkv_ps, t + 1)
                    nc.scalar.copy(qkv[:, t], ps[0:P, t % 8, 0:128]).then_inc(qkv_sb, 1)
                for n in range(0, NTR, 2):
                    dst = QT[:, n // NG] if n < 4 * NG else KT[:, n // NG - 4]
                    c = n % NG * GRP
                    act.wait_ge(t_ps, n + 1)
                    nc.scalar.copy(dst[:, c:c + GRP], ps[0:99, n % 8, :].bitcast(BF16)[:, 0:GRP]).then_inc(t_act, 1)

            @block.tensor
            def _(pe):
                pe.wait_ge(c_in, 96)
                nc.tensor.transpose(ps[0:64, 7, 0:128], Win[:], K.ident[:])
                nc.tensor.transpose(ps[0:64, 7, 128:192], wo[:], K.ident[0:64, 0:64]).then_inc(wt_ps, 1)
                pe.wait_ge(x_ok, 1)
                transposes(nc, K, lambda t: xh[:, t, :], P, 64, tr_ps)
                pe.wait_ge(tr_sb, NG)
                pe.wait_ge(wt_sb, 2)
                for t in range(T):
                    if t >= 8:
                        pe.wait_ge(qkv_sb, t - 7)
                    nc.tensor.matmul(ps[0:P, t % 8, 0:128], XT[:, t * P:(t + 1) * P], WT[:],
                                     start=True, stop=True).then_inc(qkv_ps, 1)
                pe.wait_ge(qkv_sb, T)
                pe.wait_ge(q6_ok, 6)
                for n in range(NTR):
                    h, g = n // NG, n % NG
                    if h == 4 and g == 0:
                        pe.wait_ge(k6_ok, 6)
                    if n >= 8:
                        pe.wait_ge(t_dve if n % 2 else t_act, (n - 8) // 2 + 1)
                    for j in range(3):
                        src = Q6[:, 3 * g + j, h] if h < 4 else K6[:, 3 * g + j, h - 4]
                        ins = nc.tensor.transpose(ps[0:99, n % 8, :].bitcast(BF16)[:, j * P:(j + 1) * P], src, identb[:])
                    ins.then_inc(t_ps, 1)


def gqa_maxima(nc, K, A, Q6, QT, KT):
    NH = 4
    with ExitStack() as ctx:
        sb = lambda n, s, dt=F32: K.sb("gm_" + n, s, dt, ctx=ctx)
        sem = lambda n: K.sem("gm_" + n)
        ps = K.ps
        neg = sb("neg", [P, P])
        junk = sb("junk", [P, 2, P])
        mx = sb("mx", [P, T * NH, 3])
        mxr, mxt = sb("mxr", [P, T * NH]), sb("mxt", [P, T * NH])
        m3 = sb("m3", [P, 3, T * NH], BF16)
        identb = sb("identb", [P, P], BF16)
        c_in, z_ok, chain, s_ps, max_ok, aug_ok, t_ps, t_act, t_dve = (
            sem("c_in"), sem("zeros"), sem("chain"), sem("s_ps"), sem("max_ok"), sem("aug_ok"), sem("t_ps"),
            sem("t_act"), sem("t_dve"))
        UNITS = T * NH
        with nc.Block() as block:
            @block.sync
            def _(sp):
                sp.dma_start(neg[:], A["c_negmask"]).then_inc(c_in, 16)

            @block.gpsimd
            def _(pool):
                nc.gpsimd.memset(mx[:], -3e38).then_inc(z_ok, 1)

            @block.vector
            def _(dve):
                link = Chain(dve, chain)
                link(nc.vector.tensor_copy(identb[:], K.ident[0:P, 0:P]))
                dve.wait_ge(c_in, 16)
                dve.wait_ge(z_ok, 1)
                for n in range(UNITS):
                    i, b0 = n // NH % NT, 3 * (n % 2)
                    dve.wait_ge(s_ps, n + 1)
                    if i // 3:
                        nc.vector.tensor_reduce(mx[:, n, 0:1], ps[0:P, b0:b0 + i // 3, 0:GRP], AX.XY, ALU.max)
                    if i % 3:
                        nc.vector.tensor_reduce(mx[:, n, 1:2], ps[0:P, b0 + i // 3, 0:(i % 3) * P], AX.X, ALU.max)
                    c = (i % 3) * P
                    nc.vector.tensor_tensor_reduce(out=junk[:, n % 2], in0=ps[0:P, b0 + i // 3, c:c + P], in1=neg[:],
                                                   scale=1.0, scalar=-3e38, op0=ALU.add, op1=ALU.max,
                                                   accum_out=mx[:, n, 2:3]).then_inc(max_ok, 1)
                dve.wait_ge(max_ok, UNITS)
                link(nc.vector.tensor_reduce(mxr[:], mx[:], AX.X, ALU.max))
                link(nc.vector.tensor_scalar(mxr[:], mxr[:], -1.0, None, ALU.mult))
                split3(nc, link, mxr[:], m3[:, 0], m3[:, 1], m3[:, 2], mxt[:])
                for k in range(3):
                    nc.vector.tensor_copy(Q6[:, :, :, 96 + k], m3[:, k].rearrange("p (t h) -> p t h", h=NH)
                                          ).then_inc(aug_ok, 1)
                for n in range(1, NH * NG, 2):
                    c = n % NG * GRP
                    dve.wait_ge(t_ps, n + 1)
                    nc.vector.tensor_copy(QT[:, n // NG, c:c + GRP], ps[0:99, n % 8, :].bitcast(BF16)[:, 0:GRP]
                                          ).then_inc(t_dve, 1)

            @block.scalar
            def _(act):
                for n in range(0, NH * NG, 2):
                    c = n % NG * GRP
                    act.wait_ge(t_ps, n + 1)
                    nc.scalar.copy(QT[:, n // NG, c:c + GRP], ps[0:99, n % 8, :].bitcast(BF16)[:, 0:GRP]
                                   ).then_inc(t_act, 1)

            @block.tensor
            def _(pe):
                for n in range(UNITS):
                    t, h = n // NH, n % NH
                    i, b0 = t % NT, 3 * (n % 2)
                    if n >= 2:
                        pe.wait_ge(max_ok, n - 1)
                    for c in range(i // 3 + 1):
                        w = min(3, i + 1 - 3 * c) * P
                        k0 = (t - i) * P + c * GRP
                        ins = nc.tensor.matmul(ps[0:P, b0 + c, 0:w], QT[0:96, h, t * P:(t + 1) * P],
                                               KT[0:96, h // 2, k0:k0 + w], start=True, stop=True)
                    ins.then_inc(s_ps, 1)
                pe.wait_ge(aug_ok, 3)
                for n in range(NH * NG):
                    h, g = n // NG, n % NG
                    if n >= 8:
                        pe.wait_ge(t_dve if n % 2 else t_act, (n - 8) // 2 + 1)
                    for j in range(3):
                        ins = nc.tensor.transpose(ps[0:99, n % 8, :].bitcast(BF16)[:, j * P:(j + 1) * P],
                                                  Q6[:, 3 * g + j, h], identb[:])
                    ins.then_inc(t_ps, 1)


def gqa_attend(nc, K, A, QT, KT, V1, WoT, x2):
    units, last_of = [], {}
    for b in range(B):
        for c in range(3):
            for j in range(3 * c + 3):
                for hp in range(2):
                    units.append((b, c, j, hp))
            last_of[3 * b + c] = len(units) - 1
    diag = [0]
    for b, c, j, hp in units:
        diag.append(diag[-1] + (j >= 3 * c))
    N = len(units)
    with ExitStack() as ctx:
        sb = lambda n, s, dt=F32: K.sb("gt_" + n, s, dt, ctx=ctx)
        sem = lambda n: K.sem("gt_" + n)
        ps = K.ps
        PT = sb("PT", [P, 4, 2, GRP])
        Y = sb("Y", [128, 2, GRP])
        Yt = sb("Yt", [P, T, 4, 16])
        rec = sb("rec", [P, 2, 3, 4])
        YT = sb("YT", [64, COLS])
        s_ps, exp_ok, mask_ok, av_ps, y_sb, yt_ps, y_ok = (sem("s_ps"), sem("exp_ok"), sem("mask_ok"), sem("av_ps"),
                                                           sem("y_sb"), sem("yt_ps"), sem("y_ok"))
        tr_ps, tr_sb, o_ps, chain = sem("tr_ps"), sem("tr_sb"), sem("o_ps"), sem("chain")
        with nc.Block() as block:
            @block.gpsimd
            def _(pool):
                for n, (b, c, j, hp) in enumerate(units):
                    if j >= 3 * c:
                        pool.wait_ge(exp_ok, n + 1)
                        d = PT[:, n % 4, :, 0:P]
                        nc.gpsimd.affine_select(out=d, in_=d, compare_op=ALU.is_ge, fill=0.0, base=0,
                                                pattern=[[0, 2], [1, P]], channel_multiplier=-1).then_inc(mask_ok, 1)

            @block.vector
            def _(dve):
                link = Chain(dve, chain)

                def normalise(a):
                    dve.wait_ge(yt_ps, a + 1)
                    y = ps[0:P, 6 + a % 2, 0:384].rearrange("p (k h e) -> p (k h) e", h=4, e=32)
                    r = rec[:, a % 2].rearrange("p k h -> p (k h)")
                    link(nc.vector.reciprocal(r, y[:, :, 16]))
                    nc.vector.tensor_tensor(Yt[:, 3 * a:3 * a + 3].rearrange("p t h e -> p (t h) e"), y[:, :, 0:16],
                                            bcl(r, 16), ALU.mult).then_inc(y_ok, 1)

                for a in range(NG):
                    dve.wait_ge(av_ps, last_of[a] + 1)
                    if a >= 2:
                        dve.wait_ge(yt_ps, a - 1)
                    nc.vector.tensor_copy(Y[:, a % 2], ps[:, 4 + a % 2, 0:GRP]).then_inc(y_sb, 1)
                    if a:
                        normalise(a - 1)
                normalise(NG - 1)
                for g in range(NG):
                    dve.wait_ge(o_ps, g + 1)
                    xx = x2[:, 3 * g:3 * g + 3, :].rearrange("p a b -> p (a b)")
                    nc.vector.tensor_tensor(xx, ps[0:P, g, 0:192], xx, ALU.add)

            @block.scalar
            def _(act):
                for n, (b, c, j, hp) in enumerate(units):
                    w = GRP - max(0, j - 3 * c) * P
                    act.wait_ge(s_ps, n + 1)
                    if n >= 4:
                        act.wait_ge(av_ps, n - 3)
                    b0 = 2 * (n % 2)
                    nc.scalar.activation(PT[:, n % 4, :, 0:w], ps[0:P, b0:b0 + 2, 0:w], ACT.Exp,
                                         scale=0.25).then_inc(exp_ok, 1)
                for g in range(NG):
                    act.wait_ge(tr_ps, g + 1)
                    nc.scalar.copy(YT[:, g * GRP:(g + 1) * GRP], ps[0:64, g, 0:GRP]).then_inc(tr_sb, 1)

            @block.tensor
            def _(pe):
                def weigh(n):
                    b, c, j, hp = units[n]
                    a = 3 * b + c
                    w = GRP - max(0, j - 3 * c) * P
                    pe.wait_ge(exp_ok, n + 1)
                    if j >= 3 * c:
                        pe.wait_ge(mask_ok, diag[n + 1])
                    if j == 0 and a >= 2:
                        pe.wait_ge(y_sb, a - 1)
                    for hi in range(2):
                        h = 2 * hp + hi
                        ins = nc.tensor.matmul(ps[32 * h:32 * h + 32, 4 + a % 2, GRP - w:GRP], V1[:, b * NT + j, hp],
                                               PT[:, n % 4, hi, 0:w], start=(j == 0), stop=(j == 3 * c + 2))
                    ins.then_inc(av_ps, 1)

                def turn(a):
                    pe.wait_ge(y_sb, a + 1)
                    if a >= 2:
                        pe.wait_ge(y_ok, a - 1)
                    for k in range(3):
                        ins = nc.tensor.transpose(ps[0:P, 6 + a % 2, 128 * k:128 * k + 128],
                                                  Y[:, a % 2, k * P:(k + 1) * P], K.ident[:])
                    ins.then_inc(yt_ps, 1)

                for n in range(N + 4):
                    if n < N:
                        b, c, j, hp = units[n]
                        if n >= 2:
                            pe.wait_ge(exp_ok, n - 1)
                        t0 = b * PADSEQ + max(j, 3 * c) * P
                        t1 = b * PADSEQ + (3 * c + 3) * P
                        k0 = b * PADSEQ + j * P
                        for hi in range(2):
                            ins = nc.tensor.matmul(ps[0:P, 2 * (n % 2) + hi, 0:t1 - t0], KT[:, hp, k0:k0 + P],
                                                   QT[:, 2 * hp + hi, t0:t1], start=True, stop=True)
                        ins.then_inc(s_ps, 1)
                    if n % 2 and n >= 3:
                        for m in (n - 3, n - 2):
                            if m < N:
                                weigh(m)
                    for a in range(NG):
                        if n == min(last_of[a] + 6, N + 3):
                            turn(a)
                pe.wait_ge(y_ok, NG)
                transposes(nc, K, lambda t: Yt[:, t].rearrange("p h e -> p (h e)"), P, 64, tr_ps)
                for g in range(NG):
                    pe.wait_ge(tr_sb, g + 1)
                    for j in range(3):
                        t = 3 * g + j
                        ins = nc.tensor.matmul(ps[0:P, g, j * 64:(j + 1) * 64], YT[:, t * P:(t + 1) * P], WoT[:],
                                               start=True, stop=True)
                    ins.then_inc(o_ps, 1)


def moe_top2(nc, K, A, x2):
    NE, FF = 8, 170
    HID = NE * FF
    NCH = -(-HID // 128)
    rows = [min(128, HID - 128 * c) for c in range(NCH)]
    KW = 96
    with ExitStack() as ctx:
        sb = lambda n, s, dt=F32: K.sb("mt_" + n, s, dt, ctx=ctx)
        sem = lambda n: K.sem("mt_" + n)
        ps = K.ps
        xf, tmp, st = sb("xf", [P, T, 128]), sb("tmp", [P, T, 64]), sb("st", [P, 4, T])
        lnw = sb("lnw", [P, 64])
        rin, rT = sb("rin", [8, 64]), sb("rT", [64, 8])
        win = sb("win", [128, 2, NCH, 128])
        w2in = sb("w2in", [64, HID])
        wf = sb("wf", [128, 2, HID])
        wt = sb("wt", [128, 2, HID])
        wp = sb("wp", [128, 3, 2, HID], BF16)
        w2T = sb("w2T", [128, NCH, 64])
        exf, ex = sb("exf", [KW, HID]), sb("ex", [KW, HID], BF16)
        XA = sb("XA", [64, COLS])
        X1, X3 = sb("X1", [128, COLS], BF16), sb("X3", [128, COLS], BF16)
        xt, xm = sb("xt", [128, 2, GRP]), sb("xm", [64, 2, GRP], BF16)
        lg, lt = sb("lg", [P, T, NE]), sb("lt", [P, T, NE])
        lp = sb("lp", [P, T, KW], BF16)
        WT = sb("WT", [KW, COLS], BF16)
        s1 = sb("s1", [P, 4, T])
        big, big2 = sb("big", [P, T, NE, NE]), sb("big2", [P, T, NE, NE])
        before8 = sb("before8", [P, NE, NE])
        identb = sb("identb", [P, P], BF16)
        act_sb, prod = sb("act", [128, 2, GRP]), sb("prod", [128, 2, GRP])
        H = sb("H", [128, 4, GRP])
        OT = sb("OT", [64, 2, GRP])
        w_in, c_in, chain, var_ready, std_ready, pch = (sem("w_in"), sem("c_in"), sem("chain"), sem("var"),
                                                        sem("std"), sem("pool_chain"))
        x_ok, w_ps, w_sb, wp_ok, tr_ps, xa_sb, x_parts = (sem("x_ok"), sem("w_ps"), sem("w_sb"), sem("wp_ok"),
                                                          sem("tr_ps"), sem("xa_sb"), sem("x_parts"))
        lg_ps, lg_ok, le_ok, lp_ok, wt_ps, wt_sb = (sem("lg_ps"), sem("lg_ok"), sem("le_ok"), sem("lp_ok"),
                                                    sem("wt_ps"), sem("wt_sb"))
        up_ps, silu_ok, hid_ok, dn_ps, dn_sb, bk_ps, bk_ok = (sem("up_ps"), sem("silu_ok"), sem("hid_ok"),
                                                              sem("dn_ps"), sem("dn_sb"), sem("bk_ps"), sem("bk_ok"))
        N = NG * NCH
        with nc.Block() as block:
            @block.sync
            def _(sp):
                for i, name in enumerate(("w1", "w3")):
                    w = A["L1_ffn_" + name].rearrange("e f d -> (e f) d")
                    for half in range(2):
                        cols = slice(64 * half, 64 * half + 64)
                        sp.dma_start(win[:, i, 0:NCH - 1, cols],
                                     w[0:128 * (NCH - 1)].rearrange("(c p) d -> p c d", p=128)).then_inc(w_in, 16)
                        sp.dma_start(win[0:rows[-1], i, NCH - 1, cols], w[128 * (NCH - 1):HID]).then_inc(w_in, 16)
                sp.dma_start(w2in[:].rearrange("d (e f) -> d e f", e=NE),
                             A["L1_ffn_w2"].rearrange("e d f -> d e f")).then_inc(w_in, 16)
                sp.dma_start(rin[:], A["L1_ffn_router_w"]).then_inc(w_in, 16)
                sp.dma_start(lnw[:], row(A["L1_ffn_ln2_w"], P)).then_inc(c_in, 16)
                sp.dma_start(before8[:], A["c_before8"]).then_inc(c_in, 16)
                sp.dma_start(exf[:], A["c_expand"]).then_inc(c_in, 16)

            @block.gpsimd
            def _(pool):
                link = Chain(pool, pch)
                link(nc.gpsimd.memset(lp[:], 0.0))
                pool.wait_ge(c_in, 48)
                link(nc.gpsimd.tensor_copy(ex[:], exf[:]))
                pool.wait_ge(w_sb, 2 * 3)
                for i in range(2):
                    link(nc.gpsimd.tensor_copy(wp[:, 0, i], wf[:, i]))
                    link(nc.gpsimd.tensor_tensor(wt[:, i], wf[:, i], wp[:, 0, i], ALU.subtract))
                    link(nc.gpsimd.tensor_copy(wp[:, 1, i], wt[:, i]))
                    link(nc.gpsimd.tensor_tensor(wt[64:128, i], wt[64:128, i], wp[64:128, 1, i], ALU.subtract))
                    link(nc.gpsimd.tensor_copy(wp[64:128, 2, i], wt[64:128, i]))
                    link(nc.gpsimd.tensor_copy(wp[0:64, 2, i], wp[0:64, 0, i]))
                nc.gpsimd.memset(wt[0:1, 0, 0:1], 0.0).then_inc(wp_ok, 1)

            @block.vector
            def _(dve):
                link = Chain(dve, chain)
                tt = nc.vector.tensor_tensor
                link(nc.vector.tensor_copy(identb[:], K.ident[0:P, 0:P]))
                dve.wait_ge(c_in, 48)
                rms_dve(nc, dve, link, x2[:], xf[:, :, 0:64], tmp[:], st[:], lnw[:], var_ready, std_ready)
                nc.vector.tensor_copy(xf[:, :, 64:128], xf[:, :, 0:64]).then_inc(x_ok, 1)
                tt(K.h[:], K.h[:], x2[:], ALU.add)
                for g in range(NG):
                    c = slice(g * GRP, (g + 1) * GRP)
                    dve.wait_ge(xa_sb, 3 * (g + 1))
                    t_, m_ = xt[:, g % 2], xm[:, g % 2]
                    tt(t_[0:64], ps[0:64, g, 0:GRP], X1[0:64, c], ALU.subtract)
                    link(tt(t_[64:128], ps[64:128, g, 0:GRP], X3[64:128, c], ALU.subtract))
                    nc.vector.tensor_copy(X1[64:128, c], t_[64:128])
                    link(nc.vector.tensor_copy(m_, t_[0:64]))
                    link(tt(X3[0:64, c], t_[0:64], m_, ALU.subtract))
                nc.vector.tensor_copy(st[:, 0, :], st[:, 3, :]).then_inc(x_parts, 1)
                dve.wait_ge(lg_ps, 1)
                link(nc.vector.tensor_reduce(s1[:, 0], ps[0:P, 6, 0:T * NE].rearrange("p (t e) -> p t e", e=NE),
                                             AX.X, ALU.max))
                tt(lg[:], ps[0:P, 6, 0:T * NE].rearrange("p (t e) -> p t e", e=NE), bcl(s1[:, 0], NE),
                   ALU.subtract).then_inc(lg_ok, 1)
                dve.wait_ge(le_ok, 1)
                link(nc.vector.tensor_reduce(s1[:, 1], lg[:], AX.X, ALU.add))
                link(nc.vector.reciprocal(s1[:, 1], s1[:, 1]))
                link(tt(lg[:], lg[:], bcl(s1[:, 1], NE), ALU.mult))
                mine = lg[:].unsqueeze(3).to_broadcast([P, T, NE, NE])
                other = lg[:].unsqueeze(2).to_broadcast([P, T, NE, NE])
                f3 = lambda a: a.rearrange("p t a b -> p t (a b)")
                tt(big[:], other, mine, ALU.is_gt)
                link(tt(big2[:], other, mine, ALU.is_equal))
                link(tt(f3(big2[:]), f3(big2[:]), bc(before8[:].rearrange("p a b -> p (a b)"), T), ALU.mult))
                link(tt(big[:], big[:], big2[:], ALU.add))
                link(nc.vector.tensor_reduce(big2[:, :, :, 0], big[:], AX.X, ALU.add))
                link(nc.vector.scalar_tensor_tensor(lg[:], big2[:, :, :, 0], 2.0, lg[:], ALU.is_lt, ALU.mult))
                link(nc.vector.tensor_reduce(s1[:, 2], lg[:], AX.X, ALU.add))
                link(nc.vector.tensor_scalar(s1[:, 2], s1[:, 2], 1e-9, None, ALU.add))
                link(nc.vector.reciprocal(s1[:, 3], s1[:, 2]))
                link(tt(lg[:], lg[:], bcl(s1[:, 3], NE), ALU.mult))
                dve.wait_ge(pch, 1)
                split3(nc, link, lg[:], lp[:, :, 0:8], lp[:, :, 8:16], lp[:, :, 16:24], lt[:])
                nc.vector.tensor_copy(st[:, 0, :], st[:, 3, :]).then_inc(lp_ok, 1)

                def back(g):
                    dve.wait_ge(bk_ps, g + 1)
                    hh = K.h[:, 3 * g:3 * g + 3].rearrange("p a b -> p (a b)")
                    tt(hh, ps[0:P, 7, 0:192], hh, ALU.add).then_inc(bk_ok, 1)

                for n in range(N):
                    g, c = n // NCH, n % NCH
                    r = rows[c]
                    b0 = 3 * (n % 2)
                    dve.wait_ge(silu_ok, n + 1)
                    if n >= 4:
                        dve.wait_ge(dn_ps, n - 3)
                    link(tt(prod[0:r, n % 2], ps[0:r, b0 + 1, 0:GRP], act_sb[0:r, n % 2], ALU.mult))
                    tt(H[0:r, n % 4], ps[0:r, b0 + 2, 0:GRP], prod[0:r, n % 2], ALU.mult).then_inc(hid_ok, 1)
                    if g and c == 5:
                        back(g - 1)
                back(NG - 1)

            @block.scalar
            def _(act):
                for m in range(6):
                    act.wait_ge(w_ps, m + 1)
                    w = min(512, HID - 512 * (m % 3))
                    nc.scalar.copy(wf[:, m // 3, 512 * (m % 3):512 * (m % 3) + w], ps[:, m, 0:w]).then_inc(w_sb, 1)
                act.wait_ge(w_ps, 7)
                nc.scalar.copy(w2T[:, 0:8].rearrange("p a b -> p (a b)"), ps[:, 6, :])
                nc.scalar.copy(w2T[:, 8:10].rearrange("p a b -> p (a b)"), ps[:, 7, 0:128])
                nc.scalar.copy(w2T[0:rows[-1], 10], ps[0:rows[-1], 7, 128:192])
                nc.scalar.copy(rT[:], ps[0:64, 7, 192:200]).then_inc(w_sb, 1)
                root_act(nc, act, st[:], var_ready, std_ready)
                for g in range(NG):
                    c = slice(g * GRP, (g + 1) * GRP)
                    act.wait_ge(tr_ps, g + 1)
                    nc.scalar.copy(X1[0:64, c], ps[0:64, g, 0:GRP]).then_inc(xa_sb, 1)
                    nc.scalar.copy(X3[64:128, c], ps[64:128, g, 0:GRP]).then_inc(xa_sb, 1)
                    nc.scalar.copy(XA[:, c], ps[0:64, g, 0:GRP]).then_inc(xa_sb, 1)
                act.wait_ge(lg_ok, 1)
                nc.scalar.activation(lg[:], lg[:], ACT.Exp).then_inc(le_ok, 1)
                for g in range(NG):
                    act.wait_ge(wt_ps, g + 1)
                    nc.scalar.copy(WT[:, g * GRP:(g + 1) * GRP],
                                   ps[0:KW, g, :].bitcast(BF16)[:, 0:GRP]).then_inc(wt_sb, 1)

                def out(g):
                    act.wait_ge(dn_ps, (g + 1) * NCH)
                    if g >= 2:
                        act.wait_ge(bk_ps, g - 1)
                    nc.scalar.copy(OT[:, g % 2], ps[0:64, 6, 0:GRP]).then_inc(dn_sb, 1)

                for n in range(N):
                    r = rows[n % NCH]
                    act.wait_ge(up_ps, n + 1)
                    if n >= 2:
                        act.wait_ge(hid_ok, n - 1)
                    nc.scalar.activation(act_sb[0:r, n % 2], ps[0:r, 3 * (n % 2), 0:GRP], ACT.Silu).then_inc(silu_ok, 1)
                    if n >= NCH and n % NCH == 1:
                        out(n // NCH - 1)
                out(NG - 1)

            @block.tensor
            def _(pe):
                pe.wait_ge(w_in, 160)
                for m in range(6):
                    for k in range(4):
                        c = 4 * (m % 3) + k
                        if c < NCH:
                            r = rows[c]
                            ins = nc.tensor.transpose(ps[:, m, 128 * k:128 * k + r], win[0:r, m // 3, c],
                                                      K.ident[0:r, 0:r])
                    ins.then_inc(w_ps, 1)
                for c in range(NCH):
                    r = rows[c]
                    ins = nc.tensor.transpose(ps[0:r, 6 + c // 8, 64 * (c % 8):64 * (c % 8) + 64],
                                              w2in[:, 128 * c:128 * c + r], K.ident[0:64, 0:64])
                nc.tensor.transpose(ps[0:64, 7, 192:200], rin[:], K.ident[0:8, 0:8]).then_inc(w_ps, 1)
                pe.wait_ge(w_sb, 7)
                pe.wait_ge(x_ok, 1)
                transposes(nc, K, lambda t: xf[:, t, :], P, 128, tr_ps)
                pe.wait_ge(xa_sb, 3 * NG)
                for t in range(T):
                    ins = nc.tensor.matmul(ps[0:P, 6, t * NE:(t + 1) * NE], XA[:, t * P:(t + 1) * P], rT[:],
                                           start=True, stop=True)
                ins.then_inc(lg_ps, 1)
                pe.wait_ge(lp_ok, 1)
                for g in range(NG):
                    for j in range(3):
                        ins = nc.tensor.transpose(ps[0:KW, g, :].bitcast(BF16)[:, j * P:(j + 1) * P], lp[:, 3 * g + j],
                                                  identb[:])
                    ins.then_inc(wt_ps, 1)
                pe.wait_ge(wt_sb, NG)
                pe.wait_ge(wp_ok, 1)

                def down(n):
                    g, c = n // NCH, n % NCH
                    r = rows[c]
                    pe.wait_ge(hid_ok, n + 1)
                    if c == 0 and g:
                        pe.wait_ge(dn_sb, g)
                    nc.tensor.matmul(ps[0:64, 6, 0:GRP], w2T[0:r, c], H[0:r, n % 4], start=(c == 0),
                                     stop=(c == NCH - 1)).then_inc(dn_ps, 1)

                def turn(g):
                    pe.wait_ge(dn_sb, g + 1)
                    if g:
                        pe.wait_ge(bk_ok, g)
                    for j in range(3):
                        ins = nc.tensor.transpose(ps[0:P, 7, 64 * j:64 * j + 64], OT[:, g % 2, j * P:(j + 1) * P],
                                                  K.ident[0:64, 0:64])
                    ins.then_inc(bk_ps, 1)

                for n in range(N + 2):
                    if n < N:
                        g, c = n // NCH, n % NCH
                        r = rows[c]
                        cols = slice(g * GRP, (g + 1) * GRP)
                        b0 = 3 * (n % 2)
                        if n >= 2:
                            pe.wait_ge(hid_ok, n - 1)
                        for i in range(2):
                            for k, x_ in enumerate((X1, X1, X3)):
                                nc.tensor.matmul(ps[0:r, b0 + i, 0:GRP], wp[:, k, i, 128 * c:128 * c + r],
                                                 x_[:, cols], start=(k == 0), stop=(k == 2))
                        nc.tensor.matmul(ps[0:r, b0 + 2, 0:GRP], ex[:, 128 * c:128 * c + r], WT[:, cols],
                                         start=True, stop=True).then_inc(up_ps, 1)
                    if n >= 2:
                        down(n - 2)
                        if n >= NCH and n % NCH == 4:
                            turn(n // NCH - 1)
                turn(NG - 1)



def stage_pairs(nc, K, A):
    with ExitStack() as ctx:
        Q12 = K.sb("pa_Q12", [P, T, 32, 32], BF16, ctx=ctx)
        K12 = K.sb("pa_K12", [P, T, 32, 32], BF16, ctx=ctx)
        V1 = K.sb("pa_V1", [P, T, 128], ctx=ctx)
        wpT = K.sb("pa_wpT", [64, 64], ctx=ctx)
        pairs_prepare(nc, K, A, Q12, K12, V1, wpT)
        Y = K.sb("pa_Y", [128, 8, COLS], ctx=ctx)
        pairs_attend(nc, K, A, Q12, K12, V1, Y)
        pairs_project(nc, K, A, Y, wpT)


def pairs_prepare(nc, K, A, Q12, K12, V1, wpT):
    with ExitStack() as ctx:
        sb = lambda n, s, dt=F32: K.sb("pp_" + n, s, dt, ctx=ctx)
        sem = lambda n: K.sem("pp_" + n)
        ps = K.ps
        xn, tmp, st = sb("xn", [P, T, 64]), sb("tmp", [P, T, 64]), sb("st", [P, 4, T])
        W3 = sb("W3", [64, 3, 64])
        wp = sb("wp", [64, 64])
        WT = sb("WT", [64, 192])
        XT = sb("XT", [64, COLS])
        qkv = sb("qkv", [P, T, 192])
        sq = sb("sq", [P, T, 128])
        hi, mid, lo = sb("hi", [P, T, 128], BF16), sb("mid", [P, T, 128], BF16), sb("lo", [P, T, 128], BF16)
        pm = sb("pm", [P, T, 64])
        qkw = sb("qkw", [P, 2, 2])
        c_in, chain, var_ready, std_ready = sem("c_in"), sem("chain"), sem("var"), sem("std")
        x_ok, wt_ps, wt_sb, tr_ps, tr_sb = sem("x_ok"), sem("wt_ps"), sem("wt_sb"), sem("tr_ps"), sem("tr_sb")
        qkv_ps, qkv_sb, z_ok, m_ok, r_ok = sem("qkv_ps"), sem("qkv_sb"), sem("zeros"), sem("m_ok"), sem("r_ok")
        with nc.Block() as block:
            @block.sync
            def _(sp):
                sp.dma_start(W3[:], A["L2_attn_w_qkv"].rearrange("(a o) d -> o a d", a=3)).then_inc(c_in, 16)
                sp.dma_start(wp[:], A["L2_attn_w_proj"]).then_inc(c_in, 16)
                sp.dma_start(qkw[:, 0], row(A["L2_attn_qn_w"], P)).then_inc(c_in, 16)
                sp.dma_start(qkw[:, 1], row(A["L2_attn_kn_w"], P)).then_inc(c_in, 16)

            @block.gpsimd
            def _(pool):
                nc.gpsimd.memset(Q12[:, :, :, 12:32], 0.0).then_inc(z_ok, 1)
                pool.wait_ge(z_ok, 1)
                nc.gpsimd.memset(K12[:, :, :, 12:32], 0.0).then_inc(z_ok, 1)
                pool.wait_ge(z_ok, 2)
                nc.gpsimd.memset(V1[:], 1.0).then_inc(z_ok, 1)

            @block.vector
            def _(dve):
                link = Chain(dve, chain)
                tt = nc.vector.tensor_tensor
                layernorm_dve(nc, dve, link, K.h[:], xn[:], tmp[:], st[:], var_ready, std_ready)
                nc.vector.tensor_copy(st[:, 0, :], st[:, 3, :]).then_inc(x_ok, 1)
                dve.wait_ge(c_in, 64)
                dve.wait_ge(qkv_sb, T)
                qk = qkv[:, :, 0:128]
                link(tt(sq[:], qk, qk, ALU.mult))
                link(nc.vector.tensor_reduce(pm[:], sq[:].rearrange("p t (h e) -> p t h e", e=2), AX.X, ALU.add))
                nc.vector.tensor_scalar(pm[:], pm[:], 0.5, 1e-6, ALU.mult, ALU.add).then_inc(m_ok, 1)
                dve.wait_ge(r_ok, 1)
                link(nc.vector.reciprocal(tmp[:], pm[:]))
                link(tt(qk.rearrange("p t (h e) -> p t h e", e=2), qk.rearrange("p t (h e) -> p t h e", e=2),
                        tmp[:].unsqueeze(3).to_broadcast([P, T, 64, 2]), ALU.mult))
                for a in range(2):
                    v = qkv[:, :, 64 * a:64 * a + 64].rearrange("p t (h e) -> p t h e", e=2)
                    for e in range(2):
                        link(nc.vector.tensor_scalar(v[:, :, :, e], v[:, :, :, e], qkw[:, a, e:e + 1], None, ALU.mult))
                link(nc.vector.tensor_copy(hi[:], qk))
                link(tt(sq[:], qk, hi[:], ALU.subtract))
                link(nc.vector.tensor_copy(mid[:], sq[:]))
                link(tt(sq[:], sq[:], mid[:], ALU.subtract))
                link(nc.vector.tensor_copy(lo[:], sq[:]))
                dve.wait_ge(z_ok, 3)
                for dst, off, parts in ((Q12, 0, (hi, hi, mid, mid, hi, lo)), (K12, 64, (hi, mid, hi, mid, lo, hi))):
                    for k, part in enumerate(parts):
                        nc.vector.tensor_copy(dst[:, :, :, 2 * k:2 * k + 2],
                                              part[:, :, off:off + 64].rearrange("p t (h e) -> p t h e", e=2))
                nc.vector.tensor_copy(V1[:, :, 0:96].rearrange("p t (h e) -> p t h e", e=3)[:, :, :, 0:2],
                                      qkv[:, :, 128:192].rearrange("p t (h e) -> p t h e", e=2))

            @block.scalar
            def _(act):
                root_act(nc, act, st[:], var_ready, std_ready)
                act.wait_ge(wt_ps, 1)
                nc.scalar.copy(WT[:], ps[0:64, 7, 0:192]).then_inc(wt_sb, 1)
                nc.scalar.copy(wpT[:], ps[0:64, 7, 192:256]).then_inc(wt_sb, 1)
                for g in range(NG):
                    act.wait_ge(tr_ps, g + 1)
                    nc.scalar.copy(XT[:, g * GRP:(g + 1) * GRP], ps[0:64, g, 0:GRP]).then_inc(tr_sb, 1)
                for t in range(T):
                    act.wait_ge(qkv_ps, t + 1)
                    nc.scalar.copy(qkv[:, t], ps[0:P, t % 8, 0:192]).then_inc(qkv_sb, 1)
                act.wait_ge(m_ok, 1)
                nc.scalar.activation(pm[:], pm[:], ACT.Sqrt).then_inc(r_ok, 1)

            @block.tensor
            def _(pe):
                pe.wait_ge(c_in, 64)
                for i in range(3):
                    nc.tensor.transpose(ps[0:64, 7, 64 * i:64 * i + 64], W3[:, i], K.ident[0:64, 0:64])
                nc.tensor.transpose(ps[0:64, 7, 192:256], wp[:], K.ident[0:64, 0:64]).then_inc(wt_ps, 1)
                pe.wait_ge(x_ok, 1)
                transposes(nc, K, lambda t: xn[:, t, :], P, 64, tr_ps)
                pe.wait_ge(tr_sb, NG)
                pe.wait_ge(wt_sb, 2)
                for t in range(T):
                    if t >= 8:
                        pe.wait_ge(qkv_sb, t - 7)
                    nc.tensor.matmul(ps[0:P, t % 8, 0:192], XT[:, t * P:(t + 1) * P], WT[:],
                                     start=True, stop=True).then_inc(qkv_ps, 1)


def pairs_attend(nc, K, A, Q12, K12, V1, Y):
    SCALE = float(np.float32(1.0 / np.sqrt(2)))
    HG = 8
    units, last_of = [], {}
    for bh in range(B * HG):
        for c in range(3):
            for j in range(3 * c + 3):
                for qp in range(2):
                    units.append((bh, c, j, qp))
            last_of[bh * 3 + c] = len(units) - 1
    per = len(units) // (B * HG)
    diag = [0]
    for bh, c, j, qp in units:
        diag.append(diag[-1] + (j >= 3 * c))
    N = len(units)
    SPLIT = 5
    with ExitStack() as ctx:
        sb = lambda n, s, dt=F32: K.sb("pt_" + n, s, dt, ctx=ctx)
        sem = lambda n: K.sem("pt_" + n)
        ps = K.ps
        identb = sb("identb", [P, P], BF16)
        causal = sb("causal", [P, P])
        QZ = sb("QZ", [128, 2, 4, PADSEQ], BF16)
        KT = sb("KT", [128, 2, PADSEQ], BF16)
        PT = sb("PT", [P, 4, 2, GRP])
        c_in, id_ok, z_ok, trq_ps, trk_ps, q_sb, k_sb = (sem("c_in"), sem("id_ok"), sem("zeros"), sem("trq_ps"),
                                                         sem("trk_ps"), sem("q_sb"), sem("k_sb"))
        s_ps, exp_ok, mask_ok, av_ps, y_sb = sem("s_ps"), sem("exp_ok"), sem("mask_ok"), sem("av_ps"), sem("y_sb")
        with nc.Block() as block:
            @block.sync
            def _(sp):
                sp.dma_start(causal[:], A["c_causal"]).then_inc(c_in, 16)

            @block.gpsimd
            def _(pool):
                nc.gpsimd.memset(QZ[:], 0.0).then_inc(z_ok, 1)

            @block.vector
            def _(dve):
                nc.vector.tensor_copy(identb[:], K.ident[0:P, 0:P]).then_inc(id_ok, 1)

                def bring_q(bh):
                    dve.wait_ge(trq_ps, bh + 1)
                    if bh >= 2:
                        dve.wait_ge(s_ps, per * (bh - 1))
                    for q in range(4):
                        for k, (t0, t1) in enumerate(((0, SPLIT), (SPLIT, NT))):
                            ins = nc.vector.tensor_copy(
                                QZ[32 * q:32 * q + 32, bh % 2, q, t0 * P:t1 * P],
                                ps[32 * q:32 * q + 32, 6 + k, :].bitcast(BF16)[:, 0:(t1 - t0) * P])
                    ins.then_inc(q_sb, 1)

                def bring_k(bh):
                    dve.wait_ge(trk_ps, bh + 1)
                    for k, (t0, t1) in enumerate(((0, SPLIT), (SPLIT, NT))):
                        ins = nc.vector.tensor_copy(KT[:, bh % 2, t0 * P:t1 * P],
                                                    ps[:, 6 + k, :].bitcast(BF16)[:, 0:(t1 - t0) * P])
                    ins.then_inc(k_sb, 1)

                dve.wait_ge(z_ok, 1)
                bring_q(0)
                bring_k(0)
                dve.wait_ge(c_in, 16)
                for n, (bh, c, j, qp) in enumerate(units):
                    if j >= 3 * c:
                        dve.wait_ge(exp_ok, n + 1)
                        d = PT[:, n % 4, :, 0:P]
                        nc.vector.tensor_tensor(d, d, bc(causal[:], 2), ALU.mult).then_inc(mask_ok, 1)
                    if n % per == 12 and bh + 1 < B * HG:
                        bring_q(bh + 1)
                    if n % per == 20 and bh + 1 < B * HG:
                        bring_k(bh + 1)
                    if n == last_of[bh * 3 + c]:
                        dve.wait_ge(av_ps, n + 1)
                        ac = bh * 3 + c
                        col = (bh // HG) * PADSEQ + c * GRP
                        nc.vector.tensor_copy(Y[:, bh % HG, col:col + GRP], ps[:, 4 + ac % 2, 0:GRP]).then_inc(y_sb, 1)

            @block.scalar
            def _(act):
                for n, (bh, c, j, qp) in enumerate(units):
                    w = GRP - max(0, j - 3 * c) * P
                    act.wait_ge(s_ps, n + 1)
                    if n >= 4:
                        act.wait_ge(av_ps, n - 3)
                    b0 = 2 * (n % 2)
                    nc.scalar.activation(PT[:, n % 4, :, 0:w], ps[0:P, b0:b0 + 2, 0:w], ACT.Exp,
                                         scale=SCALE).then_inc(exp_ok, 1)

            @block.tensor
            def _(pe):
                def turn(src, bh, done):
                    for t in range(NT):
                        k, col = (0, t) if t < SPLIT else (1, t - SPLIT)
                        ins = nc.tensor.transpose(
                            ps[:, 6 + k, :].bitcast(BF16)[:, col * P:(col + 1) * P],
                            src[:, (bh // HG) * NT + t, 4 * (bh % HG):4 * (bh % HG) + 4, :].rearrange("p h e -> p (h e)"),
                            identb[:])
                    ins.then_inc(done, 1)

                def weigh(n):
                    bh, c, j, qp = units[n]
                    ac = bh * 3 + c
                    w = GRP - max(0, j - 3 * c) * P
                    pe.wait_ge(exp_ok, n + 1)
                    if j >= 3 * c:
                        pe.wait_ge(mask_ok, diag[n + 1])
                    if j == 0 and ac >= 2:
                        pe.wait_ge(y_sb, ac - 1)
                    for qi in range(2):
                        q = 2 * qp + qi
                        v0 = 3 * (4 * (bh % HG) + q)
                        ins = nc.tensor.matmul(ps[32 * q:32 * q + 32, 4 + ac % 2, GRP - w:GRP],
                                               V1[:, (bh // HG) * NT + j, v0:v0 + 32], PT[:, n % 4, qi, 0:w],
                                               start=(j == 0), stop=(j == 3 * c + 2))
                    ins.then_inc(av_ps, 1)

                pe.wait_ge(id_ok, 1)
                turn(Q12, 0, trq_ps)
                pe.wait_ge(q_sb, 1)
                turn(K12, 0, trk_ps)
                for n in range(N + 4):
                    if n < N:
                        bh, c, j, qp = units[n]
                        if n % per == 0:
                            pe.wait_ge(k_sb, bh + 1)
                        if n >= 2:
                            pe.wait_ge(exp_ok, n - 1)
                        t0 = max(j, 3 * c) * P
                        for qi in range(2):
                            ins = nc.tensor.matmul(ps[0:P, 2 * (n % 2) + qi, 0:(3 * c + 3) * P - t0],
                                                   KT[:, bh % 2, j * P:(j + 1) * P],
                                                   QZ[:, bh % 2, 2 * qp + qi, t0:(3 * c + 3) * P], start=True, stop=True)
                        ins.then_inc(s_ps, 1)
                        if n % per == 12 and bh + 1 < B * HG:
                            pe.wait_ge(k_sb, bh + 1)
                            turn(Q12, bh + 1, trq_ps)
                        if n % per == 20 and bh + 1 < B * HG:
                            pe.wait_ge(q_sb, bh + 2)
                            turn(K12, bh + 1, trk_ps)
                    if n % 2 and n >= 3:
                        for m in (n - 3, n - 2):
                            if m < N:
                                weigh(m)


def pairs_project(nc, K, A, Y, wpT):
    with ExitStack() as ctx:
        sb = lambda n, s, dt=F32: K.sb("po_" + n, s, dt, ctx=ctx)
        sem = lambda n: K.sem("po_" + n)
        ps = K.ps
        Yt = sb("Yt", [P, T, 32, 2])
        rec = sb("rec", [P, 2, 4, 4])
        YT = sb("YT", [64, COLS])
        chain, tr_ps, y_ok, yt_ps, yt_sb, o_ps = (sem("chain"), sem("tr_ps"), sem("y_ok"), sem("yt_ps"),
                                                  sem("yt_sb"), sem("o_ps"))
        N = 2 * T
        with nc.Block() as block:
            @block.tensor
            def _(pe):
                for n in range(N):
                    t = n // 2
                    if n >= 8:
                        pe.wait_ge(y_ok, n - 7)
                    for k in range(4):
                        ins = nc.tensor.transpose(ps[0:P, n % 8, 128 * k:128 * k + 128],
                                                  Y[:, 4 * (n % 2) + k, t * P:(t + 1) * P], K.ident[:])
                    ins.then_inc(tr_ps, 1)
                pe.wait_ge(y_ok, N)
                transposes(nc, K, lambda t: Yt[:, t].rearrange("p h e -> p (h e)"), P, 64, yt_ps)
                for g in range(NG):
                    pe.wait_ge(yt_sb, g + 1)
                    for j in range(3):
                        t = 3 * g + j
                        ins = nc.tensor.matmul(ps[0:P, g, j * 64:(j + 1) * 64], YT[:, t * P:(t + 1) * P], wpT[:],
                                               start=True, stop=True)
                    ins.then_inc(o_ps, 1)

            @block.vector
            def _(dve):
                link = Chain(dve, chain)
                for n in range(N):
                    dve.wait_ge(tr_ps, n + 1)
                    y = ps[0:P, n % 8, :].rearrange("p (k q e) -> p (k q) e", q=4, e=32)
                    r = rec[:, n % 2].rearrange("p k q -> p (k q)")
                    link(nc.vector.reciprocal(r, y[:, :, 2]))
                    nc.vector.tensor_tensor(Yt[:, n // 2, 16 * (n % 2):16 * (n % 2) + 16], y[:, :, 0:2], bcl(r, 2),
                                            ALU.mult).then_inc(y_ok, 1)
                for g in range(NG):
                    dve.wait_ge(o_ps, g + 1)
                    hh = K.h[:, 3 * g:3 * g + 3, :].rearrange("p a b -> p (a b)")
                    nc.vector.tensor_tensor(hh, ps[0:P, g, 0:192], hh, ALU.add)

            @block.scalar
            def _(act):
                for g in range(NG):
                    act.wait_ge(yt_ps, g + 1)
                    nc.scalar.copy(YT[:, g * GRP:(g + 1) * GRP], ps[0:64, g, 0:GRP]).then_inc(yt_sb, 1)


def routed(nc, K, A, pre, E, FF, names, capacity):
    BIG = 1e30
    HID = E * FF
    NCH = HID // 128
    rw, rb, w1n, b1n, w2n, b2n = names
    XR = 96
    RING = 8
    with ExitStack() as ctx:
        sb = lambda n, s, dt=F32: K.sb(pre + n, s, dt, ctx=ctx)
        sem = lambda n: K.sem(pre + n)
        ps = K.ps
        xo, tmp, st = sb("xo", [P, T, XR]), sb("tmp", [P, T, 64]), sb("st", [P, 4, T])
        rwT = sb("rwT", [64, E])
        rin = sb("rin", [E, 64]) if not capacity else None
        rbias = sb("rbias", [P, E])
        first = sb("first", [P, E])
        W1 = sb("W1", [XR, HID])
        W2 = sb("W2", [128, NCH, 64])
        b2 = sb("b2", [XR, 64])
        eye = sb("eye", [XR, E])
        XT = sb("XT", [XR, COLS])
        lg, key = sb("lg", [P, T, E]), sb("key", [P, T, E])
        s1 = sb("s1", [P, 4, T])
        H = sb("H", [128, RING, GRP])
        OT = sb("OT", [64, 2, GRP])
        c_in, wz_ok, chain, var_ready, std_ready = sem("c_in"), sem("wz_ok"), sem("chain"), sem("var"), sem("std")
        x_ok, tr_ps, tr_sb, w1_ok, rw_ps, rw_sb = (sem("x_ok"), sem("tr_ps"), sem("tr_sb"), sem("w1_ok"),
                                                   sem("rw_ps"), sem("rw_sb"))
        lg_ps, one_ok, xo_ps, xo_sb, z_ok = sem("lg_ps"), sem("one_ok"), sem("xo_ps"), sem("xo_sb"), sem("zeros")
        up_ps, re_act, re_dve, dn_ps, dn_sb, bk_ps, bk_ok = (sem("up_ps"), sem("re_act"), sem("re_dve"), sem("dn_ps"),
                                                             sem("dn_sb"), sem("bk_ps"), sem("bk_ok"))
        if capacity:
            tri, onesP = sb("tri", [P, P]), sb("onesP", [P, P])
            rmask, pos = sb("rmask", [P, 1]), sb("pos", [P, T, E])
            run = sb("run", [P, T, E])
            yy, mk, cst = sb("yy", [P, 2, 192]), sb("mk", [P, 2, 192], mybir.dt.uint32), sb("cst", [P, 3, 192])
            e_ok, le_ok, oh_ok, cum_ps = sem("e_ok"), sem("le_ok"), sem("oh_ok"), sem("cum_ps")
        N = NG * NCH
        n_in = 9 if not capacity else 11
        with nc.Block() as block:
            @block.sync
            def _(sp):
                if capacity:
                    sp.dma_start(rwT[:], A[rw]).then_inc(c_in, 16)
                    sp.dma_start(tri[:], A["c_causal"]).then_inc(c_in, 16)
                    sp.dma_start(rmask[:], A["c_rowmask"]).then_inc(c_in, 16)
                else:
                    sp.dma_start(rin[:], A[rw]).then_inc(c_in, 16)
                sp.dma_start(rbias[:], row(A[rb], P)).then_inc(c_in, 16)
                sp.dma_start(first[:], A[f"c_first{E}"]).then_inc(c_in, 16)
                sp.dma_start(W1[0:64].rearrange("d (e f) -> d e f", e=E), A[w1n].rearrange("e d f -> d e f")
                             ).then_inc(c_in, 16)
                sp.dma_start(W2[:], A[w2n].rearrange("e f d -> (e f) d").rearrange("(c p) d -> p c d", p=128)
                             ).then_inc(c_in, 16)
                sp.wait_ge(z_ok, 3)
                sp.dma_start(W1[64:64 + E], row(A[b1n].rearrange("e f -> (e f)"), E)).then_inc(c_in, 16)
                sp.dma_start(b2[64:64 + E], A[b2n]).then_inc(c_in, 16)
                sp.dma_start(eye[64:64 + E], A[f"c_eye{E}"]).then_inc(c_in, 16)
                sp.dma_start(eye[0:E], A[f"c_eye{E}"]).then_inc(c_in, 16)

            @block.gpsimd
            def _(pool):
                nc.gpsimd.memset(xo[:, :, 64:XR], 0.0).then_inc(z_ok, 1)
                pool.wait_ge(z_ok, 1)
                nc.gpsimd.memset(W1[64:XR], 0.0).then_inc(z_ok, 1)
                pool.wait_ge(z_ok, 2)
                nc.gpsimd.memset(b2[64:XR], 0.0).then_inc(z_ok, 1)

            @block.vector
            def _(dve):
                link = Chain(dve, chain)
                tt = nc.vector.tensor_tensor
                layernorm_dve(nc, dve, link, K.h[:], xo[:, :, 0:64], tmp[:], st[:], var_ready, std_ready)
                nc.vector.tensor_copy(st[:, 0, :], st[:, 3, :]).then_inc(x_ok, 1)
                dve.wait_ge(c_in, 16 * n_in)
                w = W1[64:64 + E].rearrange("p (e f) -> p e f", e=E)
                link(tt(w, w, bcl(eye[64:64 + E], FF), ALU.mult))
                link(nc.vector.tensor_scalar(eye[64:64 + E], eye[64:64 + E], -1.0, BIG, ALU.add, ALU.mult))
                tt(w, w, bcl(eye[64:64 + E], FF), ALU.add).then_inc(w1_ok, 1)
                dve.wait_ge(lg_ps, 1)
                per = 512 // E
                for k in range((T + per - 1) // per):
                    t0, t1 = k * per, min(T, (k + 1) * per)
                    link(tt(lg[:, t0:t1], ps[0:P, 6 + k, 0:(t1 - t0) * E].rearrange("p (t e) -> p t e", e=E),
                            bc(rbias[:], t1 - t0), ALU.add))
                link(nc.vector.tensor_reduce(s1[:, 0], lg[:], AX.X, ALU.max))
                if capacity:
                    tt(lg[:], lg[:], bcl(s1[:, 0], E), ALU.subtract).then_inc(e_ok, 1)
                    dve.wait_ge(le_ok, 1)
                    link(nc.vector.tensor_reduce(s1[:, 1], lg[:], AX.X, ALU.add))
                    link(nc.vector.reciprocal(s1[:, 1], s1[:, 1]))
                    link(tt(lg[:], lg[:], bcl(s1[:, 1], E), ALU.mult))
                    link(nc.vector.tensor_reduce(s1[:, 0], lg[:], AX.X, ALU.max))
                link(tt(key[:], lg[:], bcl(s1[:, 0], E), ALU.is_equal))
                link(tt(key[:], key[:], bc(first[:], T), ALU.mult))
                link(nc.vector.tensor_reduce(s1[:, 1], key[:], AX.X, ALU.max))
                tt(xo[:, :, 64:64 + E], key[:], bcl(s1[:, 1], E), ALU.is_equal).then_inc(one_ok, 1)
                if capacity:
                    link(nc.vector.memset(onesP[:], 1.0))
                    dve.wait_ge(one_ok, 1)
                    link(nc.vector.tensor_copy(key[:], xo[:, :, 64:64 + E]))
                    for b in range(B):
                        t = b * NT + NT - 1
                        nc.vector.tensor_scalar(key[:, t], key[:, t], rmask[:, 0:1], None, ALU.mult).then_inc(oh_ok, 1)
                    dve.wait_ge(cum_ps, 1)
                    link(nc.vector.memset(run[:, 0], 0.0))
                    for t in range(1, T):
                        link(tt(run[:, t], ps[0:P, 7, E * (t - 1):E * t], run[:, t - 1], ALU.add))
                    link(tt(pos[:], ps[0:P, 6, 0:T * E].rearrange("p (t e) -> p t e", e=E), run[:], ALU.add))
                    link(tt(pos[:], pos[:], key[:], ALU.mult))
                    link(nc.vector.tensor_reduce(s1[:, 2], pos[:], AX.X, ALU.add))
                    link(nc.vector.tensor_scalar(s1[:, 2], s1[:, 2], float(capacity), None, ALU.is_le))
                    link(tt(s1[:, 3], s1[:, 2], s1[:, 0], ALU.mult))
                    for k, v in enumerate((1e4, -1e4, 0.0)):
                        link(nc.vector.memset(cst[:, k], v))

                def back(g):
                    dve.wait_ge(bk_ps, g + 1)
                    s = slice(3 * g, 3 * g + 3)
                    hh = K.h[:, s].rearrange("p a b -> p (a b)")
                    if not capacity:
                        tt(hh, ps[0:P, 6 + g % 2, 0:192], hh, ALU.add).then_inc(bk_ok, 1)
                        return
                    y = yy[:, g % 2]
                    link(tt(y.rearrange("p (a b) -> p a b", a=3),
                            ps[0:P, 6 + g % 2, 0:192].rearrange("p (a b) -> p a b", a=3), bcl(s1[:, 3, s], 64),
                            ALU.mult))
                    FMAX = 3.4028234663852886e38
                    for k, (op, v) in enumerate(((ALU.is_gt, FMAX), (ALU.is_lt, -FMAX), (ALU.not_equal, None))):
                        if v is None:
                            link(tt(mk[:, g % 2], y, y, op))
                        else:
                            link(nc.vector.tensor_scalar(mk[:, g % 2], y, v, None, op))
                        link(nc.vector.copy_predicated(y, mk[:, g % 2], cst[:, k]))
                    tt(hh, y, hh, ALU.add).then_inc(bk_ok, 1)

                for g in range(NG):
                    for c in range(NCH):
                        n = g * NCH + c
                        if n % 2:
                            dve.wait_ge(up_ps, n + 1)
                            if n >= RING:
                                dve.wait_ge(dn_ps, n - RING + 1)
                            nc.vector.tensor_scalar(H[:, n % RING], ps[:, n % 4, 0:GRP], 0.0, None,
                                                    ALU.max).then_inc(re_dve, 1)
                    if g:
                        back(g - 1)
                back(NG - 1)

            @block.scalar
            def _(act):
                root_act(nc, act, st[:], var_ready, std_ready)
                for g in range(NG):
                    act.wait_ge(tr_ps, g + 1)
                    nc.scalar.copy(XT[0:64, g * GRP:(g + 1) * GRP], ps[0:64, g, 0:GRP]).then_inc(tr_sb, 1)
                if not capacity:
                    act.wait_ge(rw_ps, 1)
                    nc.scalar.copy(rwT[:], ps[0:64, 6, 0:E]).then_inc(rw_sb, 1)
                else:
                    act.wait_ge(e_ok, 1)
                    nc.scalar.activation(lg[:], lg[:], ACT.Exp).then_inc(le_ok, 1)
                for g in range(NG):
                    act.wait_ge(xo_ps, g + 1)
                    nc.scalar.copy(XT[:, g * GRP:(g + 1) * GRP], ps[0:XR, g, 0:GRP]).then_inc(xo_sb, 1)

                def out(g):
                    act.wait_ge(dn_ps, (g + 1) * NCH)
                    act.wait_ge(bk_ok, g) if g else None
                    nc.scalar.activation(OT[:, g % 2], ps[0:64, 4 + g % 2, 0:GRP],
                                         ACT.Copy if capacity else ACT.Relu).then_inc(dn_sb, 1)

                for g in range(NG):
                    for c in range(0, NCH, 2):
                        n = g * NCH + c
                        act.wait_ge(up_ps, n + 1)
                        if n >= RING:
                            act.wait_ge(dn_ps, n - RING + 1)
                        nc.scalar.activation(H[:, n % RING], ps[:, n % 4, 0:GRP], ACT.Relu).then_inc(re_act, 1)
                    if g:
                        out(g - 1)
                out(NG - 1)

            @block.tensor
            def _(pe):
                pe.wait_ge(x_ok, 1)
                transposes(nc, K, lambda t: xo[:, t, 0:64], P, 64, tr_ps)
                pe.wait_ge(c_in, 16 * n_in)
                if not capacity:
                    nc.tensor.transpose(ps[0:64, 6, 0:E], rin[:], K.ident[0:E, 0:E]).then_inc(rw_ps, 1)
                    pe.wait_ge(rw_sb, 1)
                pe.wait_ge(tr_sb, NG)
                per = 512 // E
                for t in range(T):
                    ins = nc.tensor.matmul(ps[0:P, 6 + t // per, (t % per) * E:(t % per + 1) * E],
                                           XT[0:64, t * P:(t + 1) * P], rwT[:], start=True, stop=True)
                ins.then_inc(lg_ps, 1)
                pe.wait_ge(one_ok, 1)
                pe.wait_ge(z_ok, 3)
                transposes(nc, K, lambda t: xo[:, t, :], P, XR, xo_ps)
                if capacity:
                    pe.wait_ge(oh_ok, 2)
                    k2 = key[:].rearrange("p t e -> p (t e)")
                    nc.tensor.matmul(ps[0:P, 6, 0:T * E], tri[:], k2, start=True, stop=True)
                    nc.tensor.matmul(ps[0:P, 7, 0:T * E], onesP[:], k2, start=True, stop=True).then_inc(cum_ps, 1)
                pe.wait_ge(w1_ok, 1)
                pe.wait_ge(xo_sb, NG)

                def down(n):
                    g, c = n // NCH, n % NCH
                    pe.wait_ge(re_dve if n % 2 else re_act, n // 2 + 1)
                    if c == 0 and g >= 2:
                        pe.wait_ge(dn_sb, g - 1)
                    o = ps[0:64, 4 + g % 2, 0:GRP]
                    if c == 0:
                        nc.tensor.matmul(o, b2[64:XR], XT[64:XR, g * GRP:(g + 1) * GRP], start=True, stop=False)
                    nc.tensor.matmul(o, W2[:, c], H[:, n % RING], start=False, stop=(c == NCH - 1)).then_inc(dn_ps, 1)

                def turn(g):
                    pe.wait_ge(dn_sb, g + 1)
                    if g >= 2:
                        pe.wait_ge(bk_ok, g - 1)
                    for j in range(3):
                        ins = nc.tensor.transpose(ps[0:P, 6 + g % 2, 64 * j:64 * j + 64],
                                                  OT[:, g % 2, j * P:(j + 1) * P], K.ident[0:64, 0:64])
                    ins.then_inc(bk_ps, 1)

                for n in range(N + 3):
                    if n < N:
                        g, c = n // NCH, n % NCH
                        if n >= 4:
                            pe.wait_ge(re_dve if n % 2 else re_act, (n - 4) // 2 + 1)
                        nc.tensor.matmul(ps[:, n % 4, 0:GRP], W1[:, c * 128:(c + 1) * 128],
                                         XT[:, g * GRP:(g + 1) * GRP], start=True, stop=True).then_inc(up_ps, 1)
                    if n >= 3:
                        down(n - 3)
                        if (n - 3) % NCH == NCH - 1 and (n - 3) // NCH:
                            turn((n - 3) // NCH - 1)
                turn(NG - 1)


def stage_switch(nc, K, A):
    routed(nc, K, A, "sw_", 32, 16, ["L2_ffn_" + n for n in ("router_w", "router_b", "W1", "b1", "W2", "b2")], None)


def stage_capacity(nc, K, A):
    slots = -(-5 * B * SEQ // (4 * 8))
    routed(nc, K, A, "cp_", 8, 256, ["L3_ffn_" + n for n in ("gate_w", "gate_b", "w1", "b1", "w2", "b2")], slots)


NSEL = 255
SELP = 256


def stage_distance(nc, K, A):
    with ExitStack() as ctx:
        sb = lambda n, s, dt=F32: K.sb("ds_" + n, s, dt, ctx=ctx)
        xn = sb("xn", [P, T, 128])
        SelT = sb("SelT", [128, 2, PADSEQ])
        fT = sb("fT", [65, 64])
        acc = sb("acc", [128, B, 2, 64])
        with ExitStack() as inner:
            si = lambda n, s, dt=F32: K.sb("di_" + n, s, dt, ctx=inner)
            QH = si("QH", [128, 8, SELP])
            KH, NK = si("KH", [128, 8, SELP]), si("NK", [128, 8, SELP])
            VR = si("VR", [128, B, 4, 8, 65])
            KS = si("KS", [128, B, 4, 4])
            distance_prepare(nc, K, A, xn, SelT, fT, QH, KH, NK, VR, KS)
            distance_attend(nc, K, A, QH, KH, NK, VR, KS, acc)
        distance_output(nc, K, A, xn, SelT, fT, acc)


def distance_prepare(nc, K, A, xn, SelT, fT, QH, KH, NK, VR, KS):
    with ExitStack() as ctx:
        sb = lambda n, s, dt=F32: K.sb("dp_" + n, s, dt, ctx=ctx)
        sem = lambda n: K.sem("dp_" + n)
        ps = K.ps
        tmp, st = sb("tmp", [P, T, 64]), sb("st", [P, 4, T])
        ai, ci = sb("ai", [P, NSEL], I32), sb("ci", [128, 2], I32)
        af, cf = sb("af", [P, SELP]), sb("cf", [128, 2])
        tok, tokrow = sb("tok", [P, NT]), sb("tokrow", [128, PADSEQ])
        Sel = sb("Sel", [P, NT, SELP])
        wq, wv, fo = sb("wq", [128, 4, 65]), sb("wv", [128, 4, 65]), sb("fo", [64, 65])
        WqT, WvT = sb("WqT", [65, 512]), sb("WvT", [65, 512])
        wk = sb("wk", [128, 4])
        half = sb("half", [128, 2])
        wkT = sb("wkT", [64, 8])
        kh = sb("kh", [128, 2, 4])
        XG2 = sb("XG2", [128, B, SELP])
        XG1 = sb("XG1", [65, B, SELP])
        XD = sb("XD", [65, B, 4, 128])
        c_in, z_ok, chain, var_ready, std_ready = sem("c_in"), sem("zeros"), sem("chain"), sem("var"), sem("std")
        x_ok, sel_ok, w_ps, w_sb, g_ps, g_sb, xd_ok = (sem("x_ok"), sem("sel_ok"), sem("w_ps"), sem("w_sb"),
                                                       sem("g_ps"), sem("g_sb"), sem("xd_ok"))
        q_ps, q_sb, v_ps, v_sb, ks_ps = sem("q_ps"), sem("q_sb"), sem("v_ps"), sem("v_sb"), sem("ks_ps")
        with nc.Block() as block:
            @block.sync
            def _(sp):
                sp.dma_start(ai[:], row(A["L3_attn_a2a"], P)).then_inc(c_in, 16)
                sp.dma_start(ci[:, 0:1], A["L3_attn_a2a"][0:128].unsqueeze(1)).then_inc(c_in, 16)
                sp.dma_start(ci[0:127, 1:2], A["L3_attn_a2a"][128:NSEL].unsqueeze(1)).then_inc(c_in, 16)
                sp.dma_start(tok[:], A["c_token"]).then_inc(c_in, 16)
                sp.dma_start(tokrow[:], row(A["c_tokenrow"], 128)).then_inc(c_in, 16)
                sp.dma_start(wq[:], A["L3_attn_wq"].rearrange("(k p) d -> p k d", p=128)).then_inc(c_in, 16)
                sp.dma_start(wv[:], A["L3_attn_wv"].rearrange("(k p) d -> p k d", p=128)).then_inc(c_in, 16)
                sp.dma_start(fo[:], A["L3_attn_fanout_w"]).then_inc(c_in, 16)
                with nc.allow_non_contiguous_dma(reason="four columns"):
                    for h in range(2):
                        sp.dma_start(wk[64 * h:64 * h + 64],
                                     A["L3_attn_wk"].rearrange("(p h) c -> h c p", h=2)[h]).then_inc(c_in, 16)
                    sp.dma_start(wkT[:], A["L3_attn_wk"].rearrange("h c -> c h")).then_inc(c_in, 16)
                sp.dma_start(half[:], A["c_half"]).then_inc(c_in, 16)

            @block.gpsimd
            def _(pool):
                nc.gpsimd.memset(XG1[64:65], 1.0).then_inc(z_ok, 1)
                pool.wait_ge(z_ok, 1)
                nc.gpsimd.memset(XG1[64:65, :, NSEL:SELP], 0.0).then_inc(z_ok, 1)

            @block.vector
            def _(dve):
                link = Chain(dve, chain)
                tt = nc.vector.tensor_tensor
                link(nc.vector.memset(af[:], -1.0))
                link(nc.vector.memset(cf[:], -1.0))
                dve.wait_ge(c_in, 192)
                link(nc.vector.tensor_copy(af[:, 0:NSEL], ai[:]))
                link(nc.vector.tensor_copy(cf[:, 0:1], ci[:, 0:1]))
                link(nc.vector.tensor_copy(cf[0:127, 1:2], ci[0:127, 1:2]))
                for i in range(NT):
                    nc.vector.tensor_scalar(Sel[:, i], af[:], tok[:, i:i + 1], None, ALU.is_equal).then_inc(sel_ok, 1)
                for k in range(2):
                    nc.vector.tensor_scalar(SelT[:, k], tokrow[:], cf[:, k:k + 1], None, ALU.is_equal)
                layernorm_dve(nc, dve, link, K.h[:], xn[:, :, 0:64], tmp[:], st[:], var_ready, std_ready)
                nc.vector.tensor_copy(xn[:, :, 64:128], xn[:, :, 0:64]).then_inc(x_ok, 1)
                for b in range(B):
                    dve.wait_ge(g_ps, b + 1)
                    link(nc.vector.tensor_copy(XG2[:, b], ps[:, 2 + b, 0:SELP]))
                    nc.vector.tensor_copy(XG1[0:64, b], XG2[0:64, b]).then_inc(g_sb, 1)
                dve.wait_ge(z_ok, 2)
                dve.wait_ge(g_sb, 2)
                for b in range(B):
                    nc.vector.tensor_copy(
                        XD[:, b].rearrange("p k (q h m) -> p (k q) h m", q=4, h=2),
                        XG1[:, b].rearrange("p (a m) -> p a m", m=16).unsqueeze(2).to_broadcast([65, 16, 2, 16])
                    ).then_inc(xd_ok, 1)
                for u in range(8):
                    link(nc.vector.tensor_scalar(KH[:, u], XG2[:, u // 4], wk[:, u % 4:u % 4 + 1], None, ALU.mult))
                link(nc.vector.tensor_scalar(NK[:], KH[:], -1.0, None, ALU.mult))
                for b in range(B):
                    for k in range(4):
                        n = 4 * b + k
                        if n == 0:
                            dve.wait_ge(ks_ps, 1)
                        ks = ps[:, 0, 8 * n:8 * n + 8].rearrange("p (a h) -> p a h", h=2)
                        for h in range(2):
                            link(nc.vector.tensor_scalar(kh[:, h], ks[:, :, h], half[:, h:h + 1], -0.125, ALU.mult,
                                                         ALU.mult))
                        link(tt(KS[:, b, k], kh[:, 0], kh[:, 1], ALU.add))
                        nc.vector.tensor_copy(VR[:, b, k, :, 64].rearrange("p (a h) -> p a h", h=2), bc(half[:], 4))
                        dve.wait_ge(v_ps, n + 1)
                        for hp in range(4):
                            ins = tt(VR[:, b, k, 2 * hp:2 * hp + 2, 0:64],
                                     ps[:, 4 + n % 4, 128 * hp:128 * hp + 128].rearrange("p (h w) -> p h w", h=2),
                                     bcl(half[:], 64), ALU.mult)
                        ins.then_inc(v_sb, 1)

            @block.scalar
            def _(act):
                root_act(nc, act, st[:], var_ready, std_ready)
                act.wait_ge(w_ps, 1)
                nc.scalar.copy(WqT[:], ps[0:65, 0, :]).then_inc(w_sb, 1)
                nc.scalar.copy(WvT[:], ps[0:65, 1, :]).then_inc(w_sb, 1)
                nc.scalar.copy(fT[:], ps[0:65, 7, 0:64]).then_inc(w_sb, 1)
                for u in range(8):
                    act.wait_ge(q_ps, u + 1)
                    nc.scalar.copy(QH[:, u], ps[:, u % 4, 0:SELP]).then_inc(q_sb, 1)

            @block.tensor
            def _(pe):
                pe.wait_ge(c_in, 192)
                for i, w in enumerate((wq, wv)):
                    for k in range(4):
                        nc.tensor.transpose(ps[0:65, i, 128 * k:128 * k + 128], w[:, k], K.ident[:])
                nc.tensor.transpose(ps[0:65, 7, 0:64], fo[:], K.ident[0:64, 0:64]).then_inc(w_ps, 1)
                pe.wait_ge(sel_ok, NT)
                pe.wait_ge(x_ok, 1)
                for b in range(B):
                    for i in range(NT):
                        ins = nc.tensor.matmul(ps[:, 2 + b, 0:SELP], xn[:, b * NT + i, :], Sel[:, i],
                                               start=(i == 0), stop=(i == NT - 1))
                    ins.then_inc(g_ps, 1)
                pe.wait_ge(xd_ok, 2)
                pe.wait_ge(w_sb, 3)
                for u in range(8):
                    if u >= 4:
                        pe.wait_ge(q_sb, u - 3)
                    nc.tensor.matmul(ps[:, u % 4, 0:SELP], WqT[:, 128 * (u % 4):128 * (u % 4) + 128], XG1[:, u // 4],
                                     start=True, stop=True).then_inc(q_ps, 1)
                pe.wait_ge(q_sb, 8)
                for n in range(8):
                    ins = nc.tensor.matmul(ps[:, 0, 8 * n:8 * n + 8], XD[0:64, n // 4, n % 4], wkT[:],
                                           start=True, stop=True)
                ins.then_inc(ks_ps, 1)
                for n in range(8):
                    if n >= 4:
                        pe.wait_ge(v_sb, n - 3)
                    nc.tensor.matmul(ps[:, 4 + n % 4, :], XD[:, n // 4, n % 4], WvT[:],
                                     start=True, stop=True).then_inc(v_ps, 1)


def distance_attend(nc, K, A, QH, KH, NK, VR, KS, acc):
    RING = 16
    ACT_SHARE = (1, 4, 6, 9)
    items = []
    for u in range(8):
        for k in range(4):
            for i in range(64):
                q, m = i % 4, i // 4
                if 64 * k + 16 * q + m < NSEL:
                    items.append((u, k, q, m))
    mine = [n % 10 in ACT_SHARE for n in range(len(items))]
    before = [0]
    for a in mine:
        before.append(before[-1] + a)
    end = {}
    for n, (u, k, q, m) in enumerate(items):
        end[4 * u + k] = n + 1
    with ExitStack() as ctx:
        sb = lambda n, s, dt=F32: K.sb("da_" + n, s, dt, ctx=ctx)
        sem = lambda n: K.sem("da_" + n)
        ps = K.ps
        win = sb("win", [128, 47])
        own = sb("own", [128, 2, 128])
        AD = sb("AD", [128, RING, SELP])
        PP = sb("PP", [128, 8, SELP])
        rec = sb("rec", [128, 2, 2])
        c_in, ad_act, ad_dve, red_ps, exp_ok, av_ps, av_sb, chain = (
            sem("c_in"), sem("ad_act"), sem("ad_dve"), sem("red_ps"), sem("exp_ok"), sem("av_ps"), sem("av_sb"),
            sem("chain"))
        with nc.Block() as block:
            @block.sync
            def _(sp):
                sp.dma_start(win[:], A["c_window"]).then_inc(c_in, 16)
                sp.dma_start(own[:], A["c_own"]).then_inc(c_in, 16)

            @block.vector
            def _(dve):
                link = Chain(dve, chain)

                def gather(u):
                    b = u // 4
                    for d in range(2):
                        dve.wait_ge(av_ps, 2 * u + d + 1)
                        o = ps[:, 4 + (2 * u + d) % 4, 0:130].rearrange("p (h w) -> p h w", h=2)
                        link(nc.vector.reciprocal(rec[:, d], o[:, :, 64]))
                        for h in range(2):
                            if u % 4 == 0 and h == 0:
                                ins = nc.vector.tensor_scalar(acc[:, b, d], o[:, h, 0:64], rec[:, d, h:h + 1], None,
                                                              ALU.mult)
                            else:
                                ins = nc.vector.scalar_tensor_tensor(acc[:, b, d], o[:, h, 0:64], rec[:, d, h:h + 1],
                                                                     acc[:, b, d], ALU.mult, ALU.add)
                            if h == 0:
                                link(ins)
                        ins.then_inc(av_sb, 1)
                    dve.wait_ge(av_sb, 2 * u + 2)

                for n, (u, k, q, m) in enumerate(items):
                    if not mine[n]:
                        if n >= RING:
                            dve.wait_ge(red_ps, n - RING + 1)
                        s = 64 * k + 16 * q + m
                        nc.vector.tensor_scalar(AD[:, n % RING], QH[:, u], KH[:, u, s:s + 1], 0.0, ALU.subtract,
                                                ALU.max).then_inc(ad_dve, 1)
                    if k == 1 and u and n + 1 == end[4 * u + 1]:
                        gather(u - 1)
                gather(7)

            @block.scalar
            def _(act):
                def exps(e):
                    act.wait_ge(red_ps, end[e])
                    if e >= 8:
                        act.wait_ge(av_ps, 2 * (e // 4 - 1))
                    nc.scalar.activation(PP[:, e % 8], ps[:, e % 4, 0:SELP], ACT.Exp, scale=-0.125,
                                         bias=KS[:, e // 16, e % 4, e // 4 % 4:e // 4 % 4 + 1]).then_inc(exp_ok, 1)

                for n, (u, k, q, m) in enumerate(items):
                    if mine[n]:
                        if n >= RING:
                            act.wait_ge(red_ps, n - RING + 1)
                        s = 64 * k + 16 * q + m
                        nc.scalar.activation(AD[:, n % RING], QH[:, u], ACT.Relu,
                                             bias=NK[:, u, s:s + 1]).then_inc(ad_act, 1)
                    e = 4 * u + k
                    if e and n == end[e - 1] + 20:
                        exps(e - 1)
                exps(31)

            @block.tensor
            def _(pe):
                pe.wait_ge(c_in, 32)

                def weigh(u):
                    pe.wait_ge(exp_ok, 4 * u + 4)
                    for d in range(2):
                        if u >= 2:
                            pe.wait_ge(av_sb, 2 * u + d - 3)
                        for k in range(4):
                            ins = nc.tensor.matmul(ps[:, 4 + (2 * u + d) % 4, 0:130],
                                                   PP[:, (4 * u + k) % 8, 128 * d:128 * d + 128],
                                                   VR[:, u // 4, k, 2 * (u % 4):2 * (u % 4) + 2, :]
                                                   .rearrange("p h w -> p (h w)"), start=(k == 0), stop=(k == 3))
                        ins.then_inc(av_ps, 1)

                for n, (u, k, q, m) in enumerate(items):
                    if mine[n]:
                        pe.wait_ge(ad_act, before[n + 1])
                    else:
                        pe.wait_ge(ad_dve, n + 1 - before[n + 1])
                    e = 4 * u + k
                    if m == 0 and q == 0 and e >= 4:
                        pe.wait_ge(exp_ok, e - 3)
                    if m == 0 and q == 0:
                        nc.tensor.matmul(ps[:, e % 4, 0:SELP], own[:, k // 3], QH[:, u], start=True, stop=False,
                                         skip_group_check=True)
                    last = m == (14 if (k, q) == (3, 3) else 15)
                    nc.tensor.matmul(ps[32 * q:32 * q + 32, e % 4, 0:SELP], win[:, 15 - m:47 - m], AD[:, n % RING],
                                     start=False, stop=last, skip_group_check=True).then_inc(red_ps, 1)
                    if u and n + 1 == end[4 * u]:
                        weigh(u - 1)
                weigh(7)


def distance_output(nc, K, A, xn, SelT, fT, acc):
    with ExitStack() as ctx:
        sb = lambda n, s, dt=F32: K.sb("dq_" + n, s, dt, ctx=ctx)
        sem = lambda n: K.sem("dq_" + n)
        ps = K.ps
        sig, y = sb("sig", [P, T, 64]), sb("y", [P, T, 64])
        YT = sb("YT", [65, COLS])
        s_ps, sig_ok, y_ok, tr_ps, tr_sb, o_ps, one_ok = (sem("s_ps"), sem("sig_ok"), sem("y_ok"), sem("tr_ps"),
                                                          sem("tr_sb"), sem("o_ps"), sem("one_ok"))
        x_ok = sem("x_ok")
        flat = lambda a, g: a[:, 3 * g:3 * g + 3].rearrange("p a b -> p (a b)")
        with nc.Block() as block:
            @block.gpsimd
            def _(pool):
                nc.gpsimd.memset(YT[64:65], 1.0).then_inc(one_ok, 1)

            @block.tensor
            def _(pe):
                for g in range(NG):
                    for t in range(3 * g, 3 * g + 3):
                        i = (t % NT) * P
                        for k in range(2):
                            ins = nc.tensor.matmul(ps[0:P, g, (t % 3) * 64:(t % 3) * 64 + 64], SelT[:, k, i:i + P],
                                                   acc[:, t // NT, k], start=(k == 0), stop=(k == 1))
                    ins.then_inc(s_ps, 1)
                pe.wait_ge(y_ok, NG)
                transposes(nc, K, lambda t: y[:, t], P, 64, tr_ps)
                pe.wait_ge(one_ok, 1)
                for g in range(NG):
                    pe.wait_ge(tr_sb, g + 1)
                    for j in range(3):
                        t = 3 * g + j
                        ins = nc.tensor.matmul(ps[0:P, g, j * 64:(j + 1) * 64], YT[:, t * P:(t + 1) * P], fT[:],
                                               start=True, stop=True)
                    ins.then_inc(o_ps, 1)

            @block.scalar
            def _(act):
                for g in range(NG):
                    act.wait_ge(s_ps, g + 1)
                    nc.scalar.activation(flat(sig, g), ps[0:P, g, 0:192], ACT.Sigmoid, scale=1.702).then_inc(sig_ok, 1)
                for g in range(NG):
                    act.wait_ge(tr_ps, g + 1)
                    nc.scalar.copy(YT[0:64, g * GRP:(g + 1) * GRP], ps[0:64, g, 0:GRP]).then_inc(tr_sb, 1)

            @block.vector
            def _(dve):
                nc.vector.tensor_tensor(K.h[:], K.h[:], xn[:, :, 0:64], ALU.add).then_inc(x_ok, 1)
                for g in range(NG):
                    dve.wait_ge(sig_ok, g + 1)
                    nc.vector.tensor_tensor(flat(y, g), ps[0:P, g, 0:192], flat(sig, g), ALU.mult).then_inc(y_ok, 1)
                dve.wait_ge(x_ok, 1)
                for g in range(NG):
                    dve.wait_ge(o_ps, g + 1)
                    nc.vector.tensor_tensor(flat(K.h, g), ps[0:P, g, 0:192], flat(K.h, g), ALU.add)


STAGES = [stage_embed, stage_rwkv, stage_depths, stage_linear, stage_gqa, stage_pairs, stage_switch, stage_distance,
          stage_capacity]


def program(nc, A, out, stages):
    with ExitStack() as ctx:
        K = Core(nc, A, ctx)
        for stage in stages:
            stage(nc, K, A)
            if stage in (stage_linear, stage_pairs):
                K.recycle_semaphores()
        written = K.written
        with nc.Block() as block:
            @block.sync
            def _(sp):
                for b in range(B):
                    sp.dma_start(out[b, 0:8 * P, :].rearrange("(t p) d -> p t d", p=P),
                                 K.h[:, b * NT:b * NT + 8, :]).then_inc(written, 16)
                    sp.dma_start(out[b, 8 * P:SEQ, :], K.h[0:P - 1, b * NT + 8, :]).then_inc(written, 16)
                sp.wait_ge(written, 64)


def kernel(**inputs):
    import numpy as _np
    import concourse.bacc as _bacc
    from concourse import mybir as _mybir
    from concourse.bass_utils import run_bass_kernel_spmd as _run

    nc = _bacc.Bacc("TRN2", target_bir_lowering=False, num_devices=1)
    arrays, args = {}, {}
    for name, a in list(inputs.items()) + list(constants().items()):
        a = _np.ascontiguousarray(a)
        arrays[f"in_{name}_dram"] = a
        args[name] = nc.dram_tensor(f"in_{name}_dram", a.shape, _mybir.dt.from_np(a.dtype), kind="ExternalInput").ap()
    out = nc.dram_tensor("out_0_dram", (B, SEQ, D), F32, kind="ExternalOutput").ap()
    program(nc, args, out, STAGES)
    r = _run(nc, [arrays], core_ids=[0])
    return r.results[0]["out_0_dram"]
```
